# Optimizing a Trainium2 kernel written in Bass

```python
import numpy as np
import jax
import jax.numpy as jnp

def _softmax(x, axis=-1):
    return jax.nn.softmax(x, axis=axis)

def _gelu(x):
    return jax.nn.gelu(x, approximate=True)

def _silu(x):
    return jax.nn.silu(x)

def _sigmoid(x):
    return jax.nn.sigmoid(x)

def _layernorm(x, axis=-1, eps=1e-05):
    m = jnp.mean(x, axis=axis, keepdims=True)
    v = jnp.var(x, axis=axis, keepdims=True)
    return (x - m) / jnp.sqrt(v + eps)

def _scatter_add(tgt, idx, src, axis=0):
    return tgt.at[idx].add(src)

def _segment_sum(src, seg, n):
    return jax.ops.segment_sum(src, seg, n)
kernel_name = 'mk_seq_preln_d2_jaxref_r8_dc6c08'

def setup_inputs(seed: int=0):
    np.random.seed(seed)
    _w = jnp.asarray

    def _L0_attn_setup():
        import jax, jax.numpy as jnp
        import numpy as np
        from jax import lax
        B, T, HID, H, DK, DV, K = (2, 256, 128, 16, 64, 64, 4)
        SCALE = float(DK) ** (-0.5)
        EPS = 1e-05

        def _causal_dwconv_silu(z, w, b):
            zc = z.transpose(0, 2, 1)
            y = lax.conv_general_dilated(zc, w, (1,), [(K - 1, 0)], dimension_numbers=('NCH', 'OIH', 'NCH'), feature_group_count=zc.shape[1])
            return jax.nn.silu((y + b[None, :, None]).transpose(0, 2, 1))
        key = jax.random.key(seed)
        ks = jax.random.split(key, 12)
        n = lambda k, sh, s=0.02: jax.random.normal(k, sh, jnp.float32) * s
        return {'x': jax.random.normal(ks[0], (B, T, HID), jnp.float32), 'Wq': n(ks[1], (H * DK, HID)), 'Wk': n(ks[2], (H * DK, HID)), 'Wv': n(ks[3], (H * DV, HID)), 'Wa': n(ks[4], (H * DV, HID)), 'ba': jnp.zeros((H * DV,), jnp.float32), 'Wb': n(ks[5], (H, HID)), 'bb': jnp.zeros((H,), jnp.float32), 'Wg': n(ks[6], (H * DV, HID)), 'Wo': n(ks[7], (HID, H * DV)), 'qcw': n(ks[8], (H * DK, 1, K), 0.3), 'qcb': jnp.zeros((H * DK,), jnp.float32), 'kcw': n(ks[9], (H * DK, 1, K), 0.3), 'kcb': jnp.zeros((H * DK,), jnp.float32), 'vcw': n(ks[10], (H * DV, 1, K), 0.3), 'vcb': jnp.zeros((H * DV,), jnp.float32), 'ln_w': jnp.ones((DV,), jnp.float32), 'ln_b': jnp.zeros((DV,), jnp.float32)}
    _L0_attn_in = _L0_attn_setup()

    def _L0_ffn_setup():
        import math
        import jax, jax.numpy as jnp
        import numpy as np
        B, L, D, F_FF, E = (4, 256, 128, 512, 8)
        TOP_K = 1
        CAPACITY_FACTOR = 1.25
        key = jax.random.key(seed)
        ks = jax.random.split(key, 4)
        h = jax.random.normal(ks[0], (B, L, D), dtype=jnp.float32)
        gate_w = jax.random.normal(ks[1], (E, D), dtype=jnp.float32) * 0.02
        gate_b = jnp.zeros((E,), dtype=jnp.float32)
        w1 = jax.random.normal(ks[2], (E, D, F_FF), dtype=jnp.float32) * 0.02
        b1 = jnp.zeros((E, F_FF), dtype=jnp.float32)
        w2 = jax.random.normal(ks[3], (E, F_FF, D), dtype=jnp.float32) * 0.02
        b2 = jnp.zeros((E, D), dtype=jnp.float32)
        return {'h': h, 'gate_w': gate_w, 'gate_b': gate_b, 'w1': w1, 'b1': b1, 'w2': w2, 'b2': b2}
    _L0_ffn_in = _L0_ffn_setup()

    def _L1_attn_setup():
        import jax, jax.numpy as jnp
        import numpy as np
        D = 128
        H = 16
        HD = D // H
        R = HD
        N, T = (2, 256)
        W_LEFT, W_RIGHT = (127, 128)
        ROPE_BASE = 10000.0

        def _rope(x, cos, sin):
            x1 = x[..., :R // 2]
            x2 = x[..., R // 2:R]
            rot = jnp.concatenate([x1 * cos - x2 * sin, x2 * cos + x1 * sin], axis=-1)
            if R < x.shape[-1]:
                rot = jnp.concatenate([rot, x[..., R:]], axis=-1)
            return rot
        key = jax.random.key(seed)
        k1, k2, k3, k4 = jax.random.split(key, 4)
        x = jax.random.normal(k1, (N, T, D), dtype=jnp.float32)
        w_qkv = jax.random.normal(k2, (3 * D, D), dtype=jnp.float32) * 0.02
        w_out = jax.random.normal(k3, (D, D), dtype=jnp.float32) * 0.02
        b_out = jax.random.normal(k4, (D,), dtype=jnp.float32) * 0.02
        return {'x': x, 'w_qkv': w_qkv, 'w_out': w_out, 'b_out': b_out}
    _L1_attn_in = _L1_attn_setup()

    def _L1_ffn_setup():
        import jax, jax.numpy as jnp
        import numpy as np
        DIM = 128
        DEPTH = 2
        HEADS = 8
        DIM_HEAD = 64
        WINDOW = 64
        INNER = HEADS * DIM_HEAD
        HID = int(DIM * 4 * 2 / 3)
        B, N = (2, 1024)
        QK_SCALE = 8.0

        def shift_token(t):
            t1, t2 = jnp.split(t, 2, axis=-1)
            t2 = jnp.pad(t2, ((0, 0), (1, 0), (0, 0)))[:, :-1]
            return jnp.concatenate([t1, t2], axis=-1)

        def l2norm(t):
            return t / jnp.clip(jnp.linalg.norm(t, axis=-1, keepdims=True), 1e-12)

        def rotate_half(x):
            x1, x2 = jnp.split(x, 2, axis=-1)
            return jnp.concatenate([-x2, x1], axis=-1)

        def rotary_xpos(q, k):
            n = q.shape[-2]
            half_idx = jnp.arange(0, DIM_HEAD, 2, dtype=jnp.float32)
            inv_freq = 1.0 / 10000.0 ** (half_idx / DIM_HEAD)
            t = jnp.arange(n, dtype=jnp.float32)
            freqs = t[:, None] * inv_freq[None, :]
            freqs = jnp.concatenate([freqs, freqs], axis=-1)
            base = (half_idx + 0.4 * DIM_HEAD) / (1.4 * DIM_HEAD)
            power = (t - n // 2) / float(WINDOW // 2)
            scale = base[None, :] ** power[:, None]
            scale = jnp.concatenate([scale, scale], axis=-1)
            cos, sin = (jnp.cos(freqs), jnp.sin(freqs))
            q = q * cos * scale + rotate_half(q) * sin * scale
            k = k * cos / scale + rotate_half(k) * sin / scale
            return (q, k)

        def local_attention(q, k, v):
            b, h, n, d = q.shape
            w = n // WINDOW
            bq = q.reshape(b, h, w, WINDOW, d) * QK_SCALE
            bk = k.reshape(b, h, w, WINDOW, d)
            bv = v.reshape(b, h, w, WINDOW, d)

            def look_around(t):
                p = jnp.pad(t, ((0, 0), (0, 0), (1, 0), (0, 0), (0, 0)))
                return jnp.concatenate([p[:, :, :w], p[:, :, 1:]], axis=3)
            bk, bv = (look_around(bk), look_around(bv))
            bt = jnp.arange(n).reshape(w, WINDOW)
            btp = jnp.pad(bt, ((1, 0), (0, 0)), constant_values=-1)
            btk = jnp.concatenate([btp[:w], btp[1:]], axis=1)
            sim = jnp.einsum('bhwid,bhwjd->bhwij', bq, bk)
            i = bt[:, :, None]
            j = btk[:, None, :]
            mask = (i < j) | (i > j + WINDOW) | (j == -1)
            sim = jnp.where(mask, -jnp.finfo(sim.dtype).max, sim)
            attn = jax.nn.softmax(sim, axis=-1)
            out = jnp.einsum('bhwij,bhwjd->bhwid', attn, bv)
            return out.reshape(b, h, n, d)

        def _layer(x, wqkv, qs, ksc, wo, lg, lb, w1, b1, w2, b2):
            b, n, _ = x.shape
            h = shift_token(x)
            qkv = h @ wqkv
            q, k, v = jnp.split(qkv, 3, axis=-1)
            to_heads = lambda t: t.reshape(b, n, HEADS, DIM_HEAD).transpose(0, 2, 1, 3)
            q, k, v = (to_heads(q), to_heads(k), to_heads(v))
            q = l2norm(q) * qs
            k = l2norm(k) * ksc
            q, k = rotary_xpos(q, k)
            o = local_attention(q, k, v)
            o = o.transpose(0, 2, 1, 3).reshape(b, n, INNER)
            x = x + o @ wo
            h = shift_token(x)
            mu = h.mean(-1, keepdims=True)
            var = h.var(-1, keepdims=True)
            h = (h - mu) / jnp.sqrt(var + 1e-05) * lg + lb
            h = h @ w1 + b1
            a, g = jnp.split(h, 2, axis=-1)
            h = a * jax.nn.gelu(g, approximate=False)
            x = x + h @ w2 + b2
            return x
        key = jax.random.key(seed)
        ks = jax.random.split(key, 6)
        return {'x': jax.random.normal(ks[0], (B, N, DIM), jnp.float32), 'wqkv': jax.random.normal(ks[1], (DEPTH, DIM, 3 * INNER), jnp.float32) * 0.02, 'q_scale': jnp.ones((DEPTH, DIM_HEAD), jnp.float32), 'k_scale': jnp.ones((DEPTH, DIM_HEAD), jnp.float32), 'wo': jax.random.normal(ks[2], (DEPTH, INNER, DIM), jnp.float32) * 0.02, 'ln_g': jnp.ones((DEPTH, DIM), jnp.float32), 'ln_b': jnp.zeros((DEPTH, DIM), jnp.float32), 'w1': jax.random.normal(ks[3], (DEPTH, DIM, 2 * HID), jnp.float32) * 0.02, 'b1': jnp.zeros((DEPTH, 2 * HID), jnp.float32), 'w2': jax.random.normal(ks[4], (DEPTH, HID, DIM), jnp.float32) * 0.02, 'b2': jnp.zeros((DEPTH, DIM), jnp.float32)}
    _L1_ffn_in = _L1_ffn_setup()
    _d = {'L0_attn_x': _L0_attn_in['x'], 'L0_attn_Wq': _L0_attn_in['Wq'], 'L0_attn_Wk': _L0_attn_in['Wk'], 'L0_attn_Wv': _L0_attn_in['Wv'], 'L0_attn_Wa': _L0_attn_in['Wa'], 'L0_attn_ba': _L0_attn_in['ba'], 'L0_attn_Wb': _L0_attn_in['Wb'], 'L0_attn_bb': _L0_attn_in['bb'], 'L0_attn_Wg': _L0_attn_in['Wg'], 'L0_attn_Wo': _L0_attn_in['Wo'], 'L0_attn_qcw': _L0_attn_in['qcw'], 'L0_attn_qcb': _L0_attn_in['qcb'], 'L0_attn_kcw': _L0_attn_in['kcw'], 'L0_attn_kcb': _L0_attn_in['kcb'], 'L0_attn_vcw': _L0_attn_in['vcw'], 'L0_attn_vcb': _L0_attn_in['vcb'], 'L0_attn_ln_w': _L0_attn_in['ln_w'], 'L0_attn_ln_b': _L0_attn_in['ln_b'], 'L0_ffn_gate_w': _L0_ffn_in['gate_w'], 'L0_ffn_gate_b': _L0_ffn_in['gate_b'], 'L0_ffn_w1': _L0_ffn_in['w1'], 'L0_ffn_b1': _L0_ffn_in['b1'], 'L0_ffn_w2': _L0_ffn_in['w2'], 'L0_ffn_b2': _L0_ffn_in['b2'], 'L1_attn_w_qkv': _L1_attn_in['w_qkv'], 'L1_attn_w_out': _L1_attn_in['w_out'], 'L1_attn_b_out': _L1_attn_in['b_out'], 'L1_ffn_wqkv': _L1_ffn_in['wqkv'], 'L1_ffn_q_scale': _L1_ffn_in['q_scale'], 'L1_ffn_k_scale': _L1_ffn_in['k_scale'], 'L1_ffn_wo': _L1_ffn_in['wo'], 'L1_ffn_ln_g': _L1_ffn_in['ln_g'], 'L1_ffn_ln_b': _L1_ffn_in['ln_b'], 'L1_ffn_w1': _L1_ffn_in['w1'], 'L1_ffn_b1': _L1_ffn_in['b1'], 'L1_ffn_w2': _L1_ffn_in['w2'], 'L1_ffn_b2': _L1_ffn_in['b2']}
    _x0 = _d['L0_attn_x']
    _d['L0_attn_x'] = jax.random.normal(jax.random.fold_in(jax.random.key(seed), 1), (4, 1024, 128), dtype=_x0.dtype)
    del _x0
    return _d

def reference(L0_attn_x, L0_attn_Wq, L0_attn_Wk, L0_attn_Wv, L0_attn_Wa, L0_attn_ba, L0_attn_Wb, L0_attn_bb, L0_attn_Wg, L0_attn_Wo, L0_attn_qcw, L0_attn_qcb, L0_attn_kcw, L0_attn_kcb, L0_attn_vcw, L0_attn_vcb, L0_attn_ln_w, L0_attn_ln_b, L0_ffn_gate_w, L0_ffn_gate_b, L0_ffn_w1, L0_ffn_b1, L0_ffn_w2, L0_ffn_b2, L1_attn_w_qkv, L1_attn_w_out, L1_attn_b_out, L1_ffn_wqkv, L1_ffn_q_scale, L1_ffn_k_scale, L1_ffn_wo, L1_ffn_ln_g, L1_ffn_ln_b, L1_ffn_w1, L1_ffn_b1, L1_ffn_w2, L1_ffn_b2):

    def _L0_attn_ref(x, Wq, Wk, Wv, Wa, ba, Wb, bb, Wg, Wo, qcw, qcb, kcw, kcb, vcw, vcb, ln_w, ln_b):
        import jax, jax.numpy as jnp
        import numpy as np
        from jax import lax
        B, T, HID, H, DK, DV, K = (2, 256, 128, 16, 64, 64, 4)
        SCALE = float(DK) ** (-0.5)
        EPS = 1e-05

        def _causal_dwconv_silu(z, w, b):
            zc = z.transpose(0, 2, 1)
            y = lax.conv_general_dilated(zc, w, (1,), [(K - 1, 0)], dimension_numbers=('NCH', 'OIH', 'NCH'), feature_group_count=zc.shape[1])
            return jax.nn.silu((y + b[None, :, None]).transpose(0, 2, 1))
        Bb, Tt, _ = x.shape
        q = _causal_dwconv_silu(x @ Wq.T, qcw, qcb).reshape(Bb, Tt, H, DK)
        k = _causal_dwconv_silu(x @ Wk.T, kcw, kcb).reshape(Bb, Tt, H, DK) * SCALE
        v = _causal_dwconv_silu(x @ Wv.T, vcw, vcb).reshape(Bb, Tt, H, DV)
        a = jax.nn.sigmoid(x @ Wa.T + ba).reshape(Bb, Tt, H, DV)
        beta = jax.nn.sigmoid(x @ Wb.T + bb)

        def step(S, inp):
            qt, kt, vt, at, bt = inp
            err = jnp.einsum('bhij,bhj->bhi', S, kt) - vt
            S = at[..., None] * S - bt[..., None, None] * (err[..., None] * kt[:, :, None, :])
            o = jnp.einsum('bhij,bhj->bhi', S, qt)
            return (S, o)
        xs = tuple((jnp.moveaxis(t, 1, 0) for t in (q, k, v, a, beta)))
        S0 = jnp.zeros((Bb, H, DV, DK), x.dtype)
        _, o = lax.scan(step, S0, xs)
        o = jnp.moveaxis(o, 0, 1)
        mu = o.mean(-1, keepdims=True)
        var = ((o - mu) ** 2).mean(-1, keepdims=True)
        o = (o - mu) / jnp.sqrt(var + EPS) * ln_w + ln_b
        g = jax.nn.sigmoid(x @ Wg.T).reshape(Bb, Tt, H, DV)
        o = (o * g).reshape(Bb, Tt, H * DV)
        return o @ Wo.T

    def _L0_ffn_ref(h, gate_w, gate_b, w1, b1, w2, b2):
        import math
        import jax, jax.numpy as jnp
        import numpy as np
        B, L, D, F_FF, E = (4, 256, 128, 512, 8)
        TOP_K = 1
        CAPACITY_FACTOR = 1.25
        Bh, Lh, Dh = h.shape
        T = Bh * Lh
        capacity = max(1, math.ceil(CAPACITY_FACTOR * (T * TOP_K / E)))
        x = h.reshape(T, Dh)
        logits = x @ gate_w.T + gate_b
        probs = jax.nn.softmax(logits, axis=-1)
        idx = jnp.argmax(probs, axis=-1)
        top_prob = jnp.max(probs, axis=-1)
        one_hot = jax.nn.one_hot(idx, E, dtype=jnp.int32)
        pos = jnp.take_along_axis(jnp.cumsum(one_hot, axis=0), idx[:, None], axis=1)[:, 0] - 1
        keep = pos < capacity
        safe_pos = jnp.where(keep, pos, 0)
        buf = jnp.zeros((E, capacity, Dh), dtype=x.dtype)
        buf = buf.at[idx, safe_pos].add(x * keep[:, None].astype(x.dtype))
        hdn = jax.nn.relu(jnp.einsum('ecd,edf->ecf', buf, w1) + b1[:, None, :])
        eout = jnp.einsum('ecf,efd->ecd', hdn, w2) + b2[:, None, :]
        gathered = eout[idx, safe_pos]
        out = gathered * (top_prob * keep.astype(x.dtype))[:, None]
        return out.reshape(Bh, Lh, Dh)

    def _L1_attn_ref(x, w_qkv, w_out, b_out):
        import jax, jax.numpy as jnp
        import numpy as np
        D = 128
        H = 16
        HD = D // H
        R = HD
        N, T = (2, 256)
        W_LEFT, W_RIGHT = (127, 128)
        ROPE_BASE = 10000.0

        def _rope(x, cos, sin):
            x1 = x[..., :R // 2]
            x2 = x[..., R // 2:R]
            rot = jnp.concatenate([x1 * cos - x2 * sin, x2 * cos + x1 * sin], axis=-1)
            if R < x.shape[-1]:
                rot = jnp.concatenate([rot, x[..., R:]], axis=-1)
            return rot
        n, t, _ = x.shape
        qkv = (x @ w_qkv.T).reshape(n, t, 3, H, HD)
        q, k, v = (qkv[:, :, 0], qkv[:, :, 1], qkv[:, :, 2])
        pos = jnp.arange(t, dtype=jnp.float32)
        inv_freq = 1.0 / ROPE_BASE ** (jnp.arange(0, R, 2, dtype=jnp.float32) / R)
        freqs = pos[:, None] * inv_freq[None, :]
        cos = jnp.cos(freqs)[None, :, None, :]
        sin = jnp.sin(freqs)[None, :, None, :]
        q = _rope(q, cos, sin)
        k = _rope(k, cos, sin)
        i = jnp.arange(t)[:, None]
        j = jnp.arange(t)[None, :]
        band = (j >= i - W_LEFT) & (j <= i + W_RIGHT)
        bias = jnp.where(band, 0.0, -jnp.inf).astype(x.dtype)
        scale = np.float32(1.0 / np.sqrt(HD))
        scores = jnp.einsum('nthd,nshd->nhts', q, k) * scale + bias
        probs = jax.nn.softmax(scores, axis=-1)
        attn = jnp.einsum('nhts,nshd->nthd', probs, v).reshape(n, t, D)
        return attn @ w_out.T + b_out

    def _L1_ffn_ref(x, wqkv, q_scale, k_scale, wo, ln_g, ln_b, w1, b1, w2, b2):
        import jax, jax.numpy as jnp
        import numpy as np
        DIM = 128
        DEPTH = 2
        HEADS = 8
        DIM_HEAD = 64
        WINDOW = 64
        INNER = HEADS * DIM_HEAD
        HID = int(DIM * 4 * 2 / 3)
        B, N = (2, 1024)
        QK_SCALE = 8.0

        def shift_token(t):
            t1, t2 = jnp.split(t, 2, axis=-1)
            t2 = jnp.pad(t2, ((0, 0), (1, 0), (0, 0)))[:, :-1]
            return jnp.concatenate([t1, t2], axis=-1)

        def l2norm(t):
            return t / jnp.clip(jnp.linalg.norm(t, axis=-1, keepdims=True), 1e-12)

        def rotate_half(x):
            x1, x2 = jnp.split(x, 2, axis=-1)
            return jnp.concatenate([-x2, x1], axis=-1)

        def rotary_xpos(q, k):
            n = q.shape[-2]
            half_idx = jnp.arange(0, DIM_HEAD, 2, dtype=jnp.float32)
            inv_freq = 1.0 / 10000.0 ** (half_idx / DIM_HEAD)
            t = jnp.arange(n, dtype=jnp.float32)
            freqs = t[:, None] * inv_freq[None, :]
            freqs = jnp.concatenate([freqs, freqs], axis=-1)
            base = (half_idx + 0.4 * DIM_HEAD) / (1.4 * DIM_HEAD)
            power = (t - n // 2) / float(WINDOW // 2)
            scale = base[None, :] ** power[:, None]
            scale = jnp.concatenate([scale, scale], axis=-1)
            cos, sin = (jnp.cos(freqs), jnp.sin(freqs))
            q = q * cos * scale + rotate_half(q) * sin * scale
            k = k * cos / scale + rotate_half(k) * sin / scale
            return (q, k)

        def local_attention(q, k, v):
            b, h, n, d = q.shape
            w = n // WINDOW
            bq = q.reshape(b, h, w, WINDOW, d) * QK_SCALE
            bk = k.reshape(b, h, w, WINDOW, d)
            bv = v.reshape(b, h, w, WINDOW, d)

            def look_around(t):
                p = jnp.pad(t, ((0, 0), (0, 0), (1, 0), (0, 0), (0, 0)))
                return jnp.concatenate([p[:, :, :w], p[:, :, 1:]], axis=3)
            bk, bv = (look_around(bk), look_around(bv))
            bt = jnp.arange(n).reshape(w, WINDOW)
            btp = jnp.pad(bt, ((1, 0), (0, 0)), constant_values=-1)
            btk = jnp.concatenate([btp[:w], btp[1:]], axis=1)
            sim = jnp.einsum('bhwid,bhwjd->bhwij', bq, bk)
            i = bt[:, :, None]
            j = btk[:, None, :]
            mask = (i < j) | (i > j + WINDOW) | (j == -1)
            sim = jnp.where(mask, -jnp.finfo(sim.dtype).max, sim)
            attn = jax.nn.softmax(sim, axis=-1)
            out = jnp.einsum('bhwij,bhwjd->bhwid', attn, bv)
            return out.reshape(b, h, n, d)

        def _layer(x, wqkv, qs, ksc, wo, lg, lb, w1, b1, w2, b2):
            b, n, _ = x.shape
            h = shift_token(x)
            qkv = h @ wqkv
            q, k, v = jnp.split(qkv, 3, axis=-1)
            to_heads = lambda t: t.reshape(b, n, HEADS, DIM_HEAD).transpose(0, 2, 1, 3)
            q, k, v = (to_heads(q), to_heads(k), to_heads(v))
            q = l2norm(q) * qs
            k = l2norm(k) * ksc
            q, k = rotary_xpos(q, k)
            o = local_attention(q, k, v)
            o = o.transpose(0, 2, 1, 3).reshape(b, n, INNER)
            x = x + o @ wo
            h = shift_token(x)
            mu = h.mean(-1, keepdims=True)
            var = h.var(-1, keepdims=True)
            h = (h - mu) / jnp.sqrt(var + 1e-05) * lg + lb
            h = h @ w1 + b1
            a, g = jnp.split(h, 2, axis=-1)
            h = a * jax.nn.gelu(g, approximate=False)
            x = x + h @ w2 + b2
            return x
        for l in range(DEPTH):
            x = _layer(x, wqkv[l], q_scale[l], k_scale[l], wo[l], ln_g[l], ln_b[l], w1[l], b1[l], w2[l], b2[l])
        return x
    x = L0_attn_x
    x = x + _L0_attn_ref(_layernorm(x, axis=-1), L0_attn_Wq, L0_attn_Wk, L0_attn_Wv, L0_attn_Wa, L0_attn_ba, L0_attn_Wb, L0_attn_bb, L0_attn_Wg, L0_attn_Wo, L0_attn_qcw, L0_attn_qcb, L0_attn_kcw, L0_attn_kcb, L0_attn_vcw, L0_attn_vcb, L0_attn_ln_w, L0_attn_ln_b)
    x = x + _L0_ffn_ref(_layernorm(x, axis=-1), L0_ffn_gate_w, L0_ffn_gate_b, L0_ffn_w1, L0_ffn_b1, L0_ffn_w2, L0_ffn_b2)
    x = x + _L1_attn_ref(_layernorm(x, axis=-1), L1_attn_w_qkv, L1_attn_w_out, L1_attn_b_out)
    x = x + _L1_ffn_ref(_layernorm(x, axis=-1), L1_ffn_wqkv, L1_ffn_q_scale, L1_ffn_k_scale, L1_ffn_wo, L1_ffn_ln_g, L1_ffn_ln_b, L1_ffn_w1, L1_ffn_b1, L1_ffn_w2, L1_ffn_b2)
    return x

_drawn_inputs = setup_inputs


def setup_inputs(seed=0):
    import zlib

    import numpy as np

    out = dict(_drawn_inputs(seed))
    spreads = {'L0_attn_ba': (0.0, 0.8),
     'L0_attn_bb': (0.0, 0.8),
     'L0_attn_qcb': (0.0, 0.296),
     'L0_attn_kcb': (0.0, 0.1),
     'L0_attn_vcb': (0.0, 0.1),
     'L0_attn_ln_w': (1.0, 0.6),
     'L0_attn_ln_b': (0.0, 0.1),
     'L0_ffn_gate_b': (0.0, 0.478),
     'L0_ffn_b1': (0.0, 0.8),
     'L0_ffn_b2': (0.0, 0.517),
     'L1_ffn_q_scale': (1.0, 0.6),
     'L1_ffn_k_scale': (1.0, 0.6),
     'L1_ffn_ln_g': (1.0, 0.6),
     'L1_ffn_ln_b': (0.0, 0.8),
     'L1_ffn_b1': (0.0, 0.8),
     'L1_ffn_b2': (0.0, 0.572)}
    factors = {'L0_attn_Wa': 8.0,
     'L0_attn_Wb': 8.0,
     'L0_attn_Wg': 8.0,
     'L0_ffn_gate_w': 3.043,
     'L0_ffn_w1': 5.784,
     'L0_ffn_w2': 4.529,
     'L1_attn_w_qkv': 8.0,
     'L1_attn_w_out': 8.0,
     'L1_attn_b_out': 2.748,
     'L1_ffn_wqkv': 3.777,
     'L1_ffn_wo': 3.799,
     'L1_ffn_w1': 6.547,
     'L1_ffn_w2': 6.406}
    for name, (base, spread) in spreads.items():
        noise = np.random.default_rng([zlib.crc32(name.encode()), seed]).standard_normal(out[name].shape)
        drawn = base * np.exp(spread * noise) if base else spread * noise
        out[name] = jnp.asarray(drawn.astype(out[name].dtype))
    for name, factor in factors.items():
        out[name] = (out[name] * factor).astype(out[name].dtype)
    return out
```

```python
from contextlib import ExitStack

import numpy as np
import concourse.bass as bass
from concourse import mybir

F32 = mybir.dt.float32
ALU = mybir.AluOpType
ACT = mybir.ActivationFunctionType
AX = mybir.AxisListType

P = 128
NB, T, D = 4, 1024, 128
NT = NB * T
TPB = T // P
NTILE = NT // P
BANK = 512
EPS = 1e-5


class Token:

    def __init__(self, sem, value):
        self.sem, self.value = sem, value


class Stream:

    def __init__(self, sem, in_line=False):
        self.sem, self.count, self.queue, self.seen, self.in_line = sem, 0, [], {}, in_line

    def wait(self, *tokens):
        for t in tokens:
            if t is None:
                continue
            if self.seen.get(t.sem, 0) >= t.value:
                continue
            self.seen[t.sem] = t.value
            self.queue.append((t, None))

    def do(self, fn, *after):
        self.wait(*after)
        if self.in_line:
            self.wait(self.last())
        self.count += 1
        self.queue.append((self.sem, fn))
        return Token(self.sem, self.count)

    def run(self, fn, *after):
        self.wait(*after)
        self.queue.append((None, fn))

    def last(self):
        return Token(self.sem, self.count) if self.count else None

    def emit(self, engine):
        for what, fn in self.queue:
            if fn is None:
                engine.wait_ge(what.sem, what.value)
            elif what is None:
                fn(engine)
            else:
                fn(engine).then_inc(what, 1)


class DmaCount:

    def __init__(self, sem):
        self.sem, self.count = sem, 0

    def start(self, stream, out, in_, *after):
        stream.wait(*after)
        self.count += 16
        sem = self.sem
        stream.queue.append((None, lambda e: e.dma_start(out, in_).then_inc(sem, 16)))
        return Token(self.sem, self.count)


class Slot:

    def __init__(self, ap):
        self.ap, self.free = ap, []


class Ring:
    def __init__(self, slots):
        self.slots, self.at = slots, 0

    def next(self):
        s = self.slots[self.at % len(self.slots)]
        self.at += 1
        return s


class Core:

    def __init__(self, nc, ctx):
        self.nc, self.ctx = nc, ctx
        self.names = 0
        self.pe, self.dve, self.act, self.pool, self.sp = (
            Stream(ctx.enter_context(nc.semaphore(n)), in_line=n in ("s_dve", "s_act", "s_pool")) for n in ("s_pe", "s_dve", "s_act", "s_pool", "s_sp"))
        self.banks = ctx.enter_context(nc.psum_tensor("banks", [P, 8 * BANK], F32))
        self.stores = DmaCount(ctx.enter_context(nc.semaphore("s_stores")))
        self.dram_writes = []

    def sem(self, name):
        return self.ctx.enter_context(self.nc.semaphore(name))

    def bank(self, n, k=1):
        return self.banks[:, n * BANK:(n + k) * BANK]

    def sb(self, ctx, name, shape):
        return ctx.enter_context(self.nc.sbuf_tensor(name, shape, F32))

    def barrier(self, *more):
        streams = (self.pe, self.dve, self.act, self.pool)
        tokens = [s.last() for s in streams]
        for s in streams + (self.sp,):
            s.wait(*[t for t in tokens], *more)


def layer_norm_rows(c, src, stats, mv, rstd, eps, ready):
    for g in range(NTILE):
        t = c.dve.do(lambda e, g=g: e.bn_stats(stats[:, g, :], src[:, g, :]), *ready(g))
    for g in range(NTILE):
        t = c.dve.do(lambda e, g=g: e.bn_aggr(mv[:, g, :], stats[:, g, :]), t)
    t = c.act.do(lambda e: e.activation(rstd[:, :], mv[:, :, 1], ACT.Sqrt, bias=eps[:, 0:1]), t)
    return c.dve.do(lambda e: e.reciprocal(rstd[:, :], rstd[:, :]), t)
H0, DK = 16, 64
CH = H0 * DK
NCT = CH // P
R = NCT * NB
SEG, CK = 32, 16
NSEG, NCK = T // SEG, SEG // CK
TAPS = 4
PAD = TAPS - 1
SW = NB * SEG
assert R == 32 and SEG == 32


def delta_rule_attention(c, k, x_in, x1, xn_dram, cst, nseg=NSEG):
    pe, dve, act, pool, sp = c.pe, c.dve, c.act, c.pool, c.sp
    ident, ones_row, eps = cst["ident"], cst["ones_row"], cst["eps"]
    w_pads = DmaCount(c.sem("s_xn_pads"))
    w_xn = [DmaCount(c.sem(f"s_xn_store{i}")) for i in range(2)]

    with ExitStack() as ctx:
        X = c.sb(ctx, "a_x", [P, NTILE, D])
        stats = c.sb(ctx, "a_stats", [P, NTILE, 6])
        mv = c.sb(ctx, "a_mv", [P, NTILE, 2])
        rstd = c.sb(ctx, "a_rstd", [P, NTILE])
        xn = Ring([Slot(c.sb(ctx, f"a_xn{i}", [P, 4, D])) for i in range(2)])
        xnT = Ring([Slot(c.sb(ctx, f"a_xnT{i}", [P, BANK])) for i in range(2)])
        zero = c.sb(ctx, "a_zero", [P, NB, PAD])
        l_x = DmaCount(c.sem("s_a_x"))
        loaded = l_x.start(sp, X[:], x_in.rearrange("b (n p) d -> p (b n) d", p=P))
        t_z = dve.do(lambda e: e.memset(zero[:], 0.0))
        w_pads.start(sp, xn_dram[:, :, 0:PAD], zero[:], t_z)
        t_n = layer_norm_rows(c, X, stats, mv, rstd, eps, lambda g: (loaded,))
        bank = Ring([Slot(c.bank(i)) for i in range(2)])
        for n in range(NTILE // 4):
            s, o, b = xn.next(), xnT.next(), bank.next()
            for j in range(4):
                g = 4 * n + j
                t = dve.do(lambda e, g=g, j=j, s=s: e.tensor_scalar(s.ap[:, j, :], X[:, g, :], mv[:, g, 0:1],
                           rstd[:, g:g + 1], ALU.subtract, ALU.mult), t_n, *s.free)
            for j in range(4):
                tp = pe.do(lambda e, j=j, s=s, b=b: e.transpose(b.ap[:, j * P:(j + 1) * P], s.ap[:, j, :],
                           ident[:]), t, *b.free)
            s.free = [tp]
            ta = act.do(lambda e, o=o, b=b: e.activation(o.ap[:], b.ap, ACT.Copy), tp, *o.free)
            b.free = [ta]
            bi, t0 = divmod(n * BANK, T)
            o.free = [w_xn[n % 2].start(sp, xn_dram[:, bi, PAD + t0:PAD + t0 + BANK], o.ap[:], ta)]
        c.barrier(*[Token(w.sem, w.count) for w in w_xn + [w_pads]])

    with ExitStack() as ctx:
        sb = lambda name, shape: c.sb(ctx, "a_" + name, shape)
        wT = {n: sb("w_" + n, [P, TAPS if n in "qkv" else 1, CH]) for n in "qkvag"}
        woT = sb("w_o", [P, NCT, D])
        bias = {n: sb("bias_" + n, [P, NCT]) for n in "qkva"}
        wbT = sb("w_b", [P, H0])
        bb = sb("bb", [1, H0])
        lnw, lnb = sb("lnw", [P, 1]), sb("lnb", [P, 1])
        beta = sb("beta", [P, T])
        l_w = DmaCount(c.sem("s_a_w"))
        wtok = None
        with ExitStack() as wctx:
            raw = {n: c.sb(wctx, "a_raw_" + n, [P, NCT, D]) for n in "qkvag"}
            tap = {n: c.sb(wctx, "a_tap_" + n, [P, NCT, TAPS]) for n in "qkv"}
            raw_o = c.sb(wctx, "a_raw_o", [P, CH])
            raw_b = c.sb(wctx, "a_raw_b", [H0, D])
            scaled = Ring([Slot(c.sb(wctx, f"a_scaled{i}", [P, 4, D])) for i in range(2)])
            for n in "qkvag":
                wtok = l_w.start(sp, raw[n][:], k["L0_attn_W" + n].rearrange("(t p) d -> p t d", p=P))
            for n in "qkv":
                wtok = l_w.start(sp, tap[n][:], k[f"L0_attn_{n}cw"])
                wtok = l_w.start(sp, bias[n][:], k[f"L0_attn_{n}cb"])
            wtok = l_w.start(sp, bias["a"][:], k["L0_attn_ba"])
            wtok = l_w.start(sp, raw_o[:], k["L0_attn_Wo"])
            wtok = l_w.start(sp, raw_b[:], k["L0_attn_Wb"])
            wtok = l_w.start(sp, bb[:], k["L0_attn_bb"])
            wtok = l_w.start(sp, lnw[:], k["L0_attn_ln_w"])
            wtok = l_w.start(sp, lnb[:], k["L0_attn_ln_b"])
            bank = Ring([Slot(c.bank(i)) for i in range(4)])
            for n in "qkvag":
                for half in range(2):
                    for j in range(TAPS if n in "qkv" else 1):
                        b = bank.next()
                        src = raw[n][:, 4 * half:4 * half + 4, :]
                        ready, s = [wtok], None
                        if n in "qkv":
                            s = scaled.next()
                            tj = tap[n][:, 4 * half:4 * half + 4, j:j + 1].broadcast_to([P, 4, D])
                            ready = [dve.do(lambda e, s=s, src=src, tj=tj: e.tensor_tensor(s.ap[:], src, tj, ALU.mult),
                                            wtok, *s.free)]
                            src = s.ap[:]
                        for m in range(4):
                            tp = pe.do(lambda e, b=b, m=m, src=src: e.transpose(b.ap[:, m * P:(m + 1) * P],
                                       src[:, m, :], ident[:]), *ready, *b.free)
                        if s is not None:
                            s.free = [tp]
                        b.free = [act.do(lambda e, n=n, j=j, half=half, b=b: e.activation(
                            wT[n][:, j, half * BANK:(half + 1) * BANK], b.ap, ACT.Copy), tp)]
            for half in range(2):
                b = bank.next()
                for m in range(4):
                    ct = 4 * half + m
                    tp = pe.do(lambda e, b=b, m=m, ct=ct: e.transpose(b.ap[:, m * P:(m + 1) * P],
                               raw_o[:, ct * P:(ct + 1) * P], ident[:]), wtok, *b.free)
                b.free = [act.do(lambda e, b=b, half=half: e.activation(
                    woT[:, 4 * half:4 * half + 4, :], b.ap.rearrange("p (m d) -> p m d", m=4), ACT.Copy), tp)]
            b = bank.next()
            tp = pe.do(lambda e, b=b: e.transpose(b.ap[:, 0:H0], raw_b[:], ident[0:H0, 0:H0]), wtok, *b.free)
            b.free = [act.do(lambda e, b=b: e.activation(wbT[:], b.ap[:, 0:H0], ACT.Copy), tp)]
            w_ready = act.last()
            c.barrier()

        with ExitStack() as bctx:
            xb = c.sb(bctx, "a_xb", [P, NB, T])
            bt = c.sb(bctx, "a_bt", [P, NTILE, H0])
            btx = c.sb(bctx, "a_btx", [P, TPB, 2, 2, NCT, NB])
            t = l_w.start(sp, xb[:], xn_dram[:, :, PAD:])
            logits = c.bank(0)
            for g in range(NTILE):
                bi, tt = divmod(g, TPB)
                pe.run(lambda e, g=g, bi=bi, tt=tt: e.matmul(logits[:, g * H0:(g + 1) * H0],
                       xb[:, bi, tt * P:(tt + 1) * P], wbT[:], start=(g == 0), stop=False, skip_group_check=True),
                       t, w_ready)
                tp = pe.do(lambda e, g=g: e.matmul(logits[:, g * H0:(g + 1) * H0], ones_row[0:1, 0:P], bb[:],
                           start=False, stop=True, skip_group_check=True))
            t = act.do(lambda e: e.activation(bt[:].rearrange("p g h -> p (g h)"), logits, ACT.Sigmoid), tp)
            for tt in range(TPB):
                for ih in range(2):
                    for par in range(2):
                        src = bt[:, tt::TPB, par::2].rearrange("p b c -> p c b")
                        td = dve.do(lambda e, tt=tt, ih=ih, par=par, src=src: e.tensor_copy(btx[:, tt, par, ih, :, :], src), t)
            for tt in range(TPB):
                b = c.bank(1 + tt // 4)[:, (tt % 4) * P:(tt % 4 + 1) * P]
                tp = pe.do(lambda e, tt=tt, b=b: e.transpose(b, btx[:, tt].rearrange("p a i c b -> p (a i c b)"),
                           ident[:]), td)
            for half in range(2):
                act.do(lambda e, half=half: e.activation(beta[:, half * BANK:(half + 1) * BANK], c.bank(1 + half),
                       ACT.Copy), tp)
            c.barrier()

        xseg = Ring([Slot(sb(f"xseg{i}", [P, NB, PAD + SEG])) for i in range(3)])
        KQ = Ring([Slot(sb(f"kq{i}", [P, R, 3, SEG])) for i in range(2)])
        kraw = Slot(sb("kraw", [P, R, SEG]))
        v1, a1 = Slot(sb("v1", [P, SEG, R])), Slot(sb("a1", [P, SEG, R]))
        a2 = Ring([Slot(sb(f"a2_{i}", [P, SEG, 32])) for i in range(2)])
        bv = Ring([Slot(sb(f"bv{i}", [P, SEG, 32])) for i in range(2)])
        Dc = Ring([Slot(sb(f"dc{i}", [P, SEG, 32])) for i in range(2)])
        Dk = Slot(sb("dk", [P, CK, 32]))
        G1 = Slot(sb("g1", [P, R, 2, CK]))
        G2 = Ring([Slot(sb(f"g2_{i}", [P, 2, CK, SEG])) for i in range(2)])
        Kt = Slot(sb("kt", [P, R, DK]))
        W = [sb(f"w{i}", [P, SEG, 32]) for i in range(NCK)]
        Wm = sb("wm", [P, 2, 32, R])
        ST = sb("st", [P, R, DK])
        AB = sb("ab", [P, R, DK])
        Dx = Ring([Slot(sb(f"dx{i}", [P, 8, 2, 32])) for i in range(2)])
        P2 = sb("p2", [P, 2, CK, 32])
        tmp_e, tmp_o = sb("tmp_e", [P, CK, 32]), sb("tmp_o", [P, CK, 32])
        red = sb("red", [P, 2, 32])
        O2 = sb("o2", [P, SEG, 32])
        o1, sq = sb("o1", [P, R, SEG]), sb("sq", [P, R, SEG])
        xrow = Slot(sb("xrow", [P, D]))
        back = Ring([Slot(c.bank(i)) for i in range(4)])
        Pb = Slot(c.bank(4, 2))
        Ub = Ring([Slot(c.bank(6 + i)) for i in range(2)])
        l_seg = [DmaCount(c.sem(f"s_a_seg{i}")) for i in range(3)]
        l_row, w_row = (DmaCount(c.sem(n)) for n in ("s_a_row", "s_a_out"))
        half_of, pair_ones, pair_mean, ih_mask, own = (cst[n] for n in ("half_of", "pair_ones", "pair_mean", "ih_mask", "own"))

        for w in W + [ST]:
            zeroed = dve.do(lambda e, w=w: e.memset(w[:], 0.0))

        def project(n, b, xs, ct, m):
            taps = TAPS if n in "qkv" else 1
            for j in range(taps):
                off = j if taps > 1 else PAD
                fn = lambda e, j=j, off=off: e.matmul(
                    b.ap[:, m * SW:(m + 1) * SW].rearrange("p (b t) -> p b t", b=NB), wT[n][:, j, ct * P:(ct + 1) * P],
                    xs.ap[:, :, off:off + SEG], start=(j == 0), stop=(j == taps - 1))
                if j < taps - 1:
                    pe.run(fn, *b.free, *xs.ready)
                else:
                    return pe.do(fn, *b.free, *xs.ready)

        def segment_inputs(s):
            seg = dict(xs=xseg.next(), kq=KQ.next(), a2=a2.next(), bv=bv.next(), dc=Dc.next(), g2=G2.next())
            xs, kq = seg["xs"], seg["kq"]
            t0 = s * SEG
            xs.ready = [l_seg[s % 3].start(sp, xs.ap[:], xn_dram[:, :, t0:t0 + SEG + PAD], *xs.free)]
            done = {}

            def proj(n, half):
                b = back.next()
                for m in range(4):
                    tp = project(n, b, xs, 4 * half + m, m)
                for m in range(4):
                    ct = 4 * half + m
                    src = b.ap[:, m * SW:(m + 1) * SW].rearrange("p (b t) -> p b t", b=NB)
                    rr = slice(ct * NB, (ct + 1) * NB)
                    if n == "k":
                        dst, fn, free = kraw.ap[:, rr, :], ACT.Silu, kraw.free
                    elif n == "q":
                        dst, fn, free = kq.ap[:, rr, 2, :], ACT.Silu, kq.free
                    elif n == "v":
                        dst, fn, free = v1.ap[:, :, rr].rearrange("p t b -> p b t"), ACT.Silu, v1.free
                    else:
                        dst, fn, free = a1.ap[:, :, rr].rearrange("p t b -> p b t"), ACT.Sigmoid, a1.free
                    t = act.do(lambda e, dst=dst, src=src, fn=fn, ct=ct, n=n: e.activation(
                        dst, src, fn, bias=bias[n][:, ct:ct + 1]), tp, *free)
                b.free = [t]
                done[n] = t
                if n == "k" and half == 1:
                    src = kraw.ap[:].rearrange("p r (o t) -> p r o t", o=1).broadcast_to([P, R, 2, SEG])
                    done["kk"] = pool.do(lambda e, src=src: e.tensor_scalar(kq.ap[:, :, 0:2, :], src, DK ** -0.5, None,
                                         ALU.mult), t, *kq.free)
                    kraw.free = [done["kk"]]

            def gates():
                t = dve.do(lambda e: e.transpose(seg["a2"].ap[:].rearrange("p t i -> p (t i)"),
                                                 a1.ap[:].rearrange("p t r -> p (t r)")), done["a"], *seg["a2"].free)
                a1.free = [t]
                A, Dd = seg["a2"].ap, seg["dc"].ap
                view = lambda x, j: x[:].rearrange("p (c t) i -> p c t i", t=CK)[:, :, j, :]
                tt = pool.do(lambda e: e.tensor_copy(view(Dd, 0), view(A, 0)), t, *seg["dc"].free)
                for j in range(1, CK):
                    tt = pool.do(lambda e, j=j: e.tensor_tensor(view(Dd, j), view(Dd, j - 1), view(A, j), ALU.mult), tt)
                seg["a_ready"], seg["d_ready"] = t, tt

            def values():
                t = dve.do(lambda e: e.transpose(seg["bv"].ap[:].rearrange("p t i -> p (t i)"),
                                                 v1.ap[:].rearrange("p t r -> p (t r)")), done["v"], *seg["bv"].free)
                v1.free = [t]
                bcol = beta[:, t0:t0 + SEG].rearrange("p (t o) -> p t o", o=1).broadcast_to([P, SEG, 32])
                seg["v_ready"] = pool.do(lambda e: e.tensor_tensor(seg["bv"].ap[:], seg["bv"].ap[:], bcol, ALU.mult), t)

            def gram(n):
                b = back.next()
                for m in range(8):
                    r = 8 * n + m
                    for par in range(2):
                        ps = slice(par * DK, (par + 1) * DK)
                        tp = pe.do(lambda e, r=r, m=m, ps=ps: e.matmul(
                            b.ap[ps, m * 2 * SEG:(m + 1) * 2 * SEG].rearrange("p (z t) -> p z t", z=2),
                            kq.ap[ps, r, 0:2, :].rearrange("p z t -> p (z t)"), kq.ap[ps, r, 0:3:2, :],
                            start=True, stop=True), done["kk"], done["q"], *b.free)
                v = b.ap.rearrange("p (rz c t) -> p rz c t", c=NCK, t=CK)
                dst = G1.ap[:, 8 * n:8 * n + 8, :, :].rearrange("p r z t -> p (r z) t")
                t = act.do(lambda e, v=v, dst=dst: e.activation(dst, v[:, :, 0, :], ACT.Copy, scale=half_of[:, 0:1]), tp, *G1.free)
                seg["g1"] = dve.do(lambda e, v=v, dst=dst: e.scalar_tensor_tensor(dst, v[:, :, 1, :], half_of[:, 1:2], dst,
                                   ALU.mult, ALU.add), t)
                b.free = [seg["g1"]]

            def gram_rows():
                g2 = seg["g2"]
                tr = dve.do(lambda e: e.transpose(g2.ap[:].rearrange("p z t j -> p (z t) j"),
                                                  G1.ap[:].rearrange("p r z t -> p (z t) r")), seg["g1"], *g2.free)
                G1.free = [tr]
                for ch in range(NCK):
                    v = g2.ap[:, 0, :, ch * CK:(ch + 1) * CK]
                    bc = beta[:, t0 + ch * CK:t0 + (ch + 1) * CK].rearrange("p (t o) -> p t o", o=1).broadcast_to([P, CK, CK])
                    seg["g_ready"] = pool.do(lambda e, v=v, bc=bc: e.tensor_tensor(v, v, bc, ALU.mult), tr)

            def late():
                for n in range(4):
                    b = back.next()
                    for m in range(8):
                        r = 8 * n + m
                        for par in range(2):
                            ps = slice(par * DK, (par + 1) * DK)
                            tp = pe.do(lambda e, r=r, m=m, ps=ps, b=b: e.matmul(
                                b.ap[ps, m * DK:(m + 1) * DK], kq.ap[ps, r, 0:2, :].rearrange("p z t -> p (z t)"),
                                ident[ps, ps], start=True, stop=True), done["kk"], *b.free)
                    t = act.do(lambda e, n=n, b=b: e.activation(Kt.ap[:, 8 * n:8 * n + 8, :].rearrange("p r d -> p (r d)"),
                               b.ap, ACT.Copy), tp, *Kt.free)
                    b.free = [t]
                seg["kt_ready"] = t

            jobs = [lambda n=n, half=half: proj(n, half) for n in "kqva" for half in range(2)]
            jobs = jobs[:8] + [gates, values] + [lambda n=n: gram(n) for n in range(4)] + [gram_rows]
            seg["jobs"], seg["late"] = jobs, late
            return seg

        def chunk(s, ch, seg, jobs):
            t0 = s * SEG + ch * CK
            kq, a2_, bv_, dc, g2 = (seg[n] for n in ("kq", "a2", "bv", "dc", "g2"))
            js = slice(ch * CK, (ch + 1) * CK)
            Wc = W[ch]
            njobs = -(-len(jobs) // CK) if jobs else 0

            for r in range(R):
                for par in range(2):
                    ps = slice(par * DK, (par + 1) * DK)
                    tp = pe.do(lambda e, r=r, ps=ps: e.matmul(
                        Pb.ap[ps, r * 2 * CK:(r + 1) * 2 * CK].rearrange("p (z t) -> p z t", z=2), ST[ps, r, :],
                        kq.ap[ps, r, 0:3:2, js], start=True, stop=True), chain["state"], *Pb.free)
            if ch == 0:
                seg["late"]()
            t = pool.do(lambda e: e.tensor_copy(Dk.ap[:, 1:, :], dc.ap[:, ch * CK:(ch + 1) * CK - 1, :]), seg["d_ready"], *Dk.free)
            t1 = pool.do(lambda e: e.memset(Dk.ap[:, 0, :], 1.0), *Dk.free)
            bc = beta[:, t0:t0 + CK].rearrange("p (t o) -> p t o", o=1).broadcast_to([P, CK, 32])
            t_dk = pool.do(lambda e: e.tensor_tensor(Dk.ap[:], Dk.ap[:], bc, ALU.mult), t, t1)
            tt = dve.do(lambda e: e.transpose(P2[:].rearrange("p z t i -> p (z t) i"),
                        Pb.ap.rearrange("p (r n) -> p n r", r=R)), tp)
            Pb.free = [tt]
            tk = dve.do(lambda e: e.tensor_tensor(P2[:, 0], P2[:, 0], Dk.ap[:], ALU.mult), tt, t_dk)
            Dk.free = [tk]
            tq = dve.do(lambda e: e.tensor_tensor(P2[:, 1], P2[:, 1], dc.ap[:, js, :], ALU.mult), tt, seg["d_ready"])
            te = dve.do(lambda e: e.tensor_tensor(P2[:, 0], bv_.ap[:, js, :], P2[:, 0], ALU.subtract), tk, seg["v_ready"])
            ab = None
            for n in range(4):
                b, dx = back.next(), Dx.next()
                d15 = dc.ap[:, (ch + 1) * CK - 1:(ch + 1) * CK, :].rearrange("p (o q) i -> p o q i", o=1).broadcast_to([P, 8, 2, 32])
                ow = own[:, 16 * n:16 * n + 16].rearrange("p (r h o) -> p r h o", h=2, o=1).broadcast_to([P, 8, 2, 32])
                t = pool.do(lambda e, dx=dx, d15=d15, ow=ow: e.tensor_tensor(dx.ap[:], d15, ow, ALU.mult), seg["d_ready"], *dx.free)
                tb = pe.do(lambda e, b=b, dx=dx: e.matmul(b.ap, pair_ones[:], dx.ap[:].rearrange("p r h i -> p (r h i)"),
                           start=True, stop=True), t, *b.free)
                dx.free = [tb]
                ab = act.do(lambda e, b=b, n=n: e.activation(AB[:, 8 * n:8 * n + 8, :].rearrange("p r i -> p (r i)"), b.ap,
                            ACT.Copy), tb, chain["ab_free"])
                b.free = [ab]
            t_sd = pool.do(lambda e: e.tensor_tensor(ST[:], ST[:], AB[:], ALU.mult), ab, tp, chain["state"])
            chain["ab_free"] = t_sd

            w_ok = chain["w_free"][ch]
            tw = dve.do(lambda e: e.tensor_scalar(Wc[:, ch * CK, :], P2[:, 0, 0, :], -1.0, None, ALU.mult), te, w_ok)
            prev_o = None
            for t in range(CK):
                row = ch * CK + t
                if t:
                    wj = Wc[:, ch * CK:row, :]
                    gk = g2.ap[:, 0, t, ch * CK:row].rearrange("p (j o) -> p j o", o=1).broadcast_to([P, t, 32])
                    tm = dve.do(lambda e, t=t, wj=wj, gk=gk: e.tensor_tensor(tmp_e[:, 0:t, :], wj, gk, ALU.mult), tw, seg["g_ready"])
                    if prev_o is not None:
                        dve.do(*prev_o)
                    tr = dve.do(lambda e, t=t: e.tensor_reduce(red[:, 0, :], tmp_e[:, 0:t, :].rearrange("p j i -> p i j"),
                                AX.X, ALU.add), tm)
                    at = a2_.ap[:, row:row + 1, :].broadcast_to([P, t, 32])
                    td = dve.do(lambda e, wj=wj, at=at: e.tensor_tensor(wj, wj, at, ALU.mult), tm, seg["a_ready"])
                    tw = dve.do(lambda e, t=t, row=row: e.scalar_tensor_tensor(Wc[:, row, :], red[:, 0, :], -1.0, P2[:, 0, t, :],
                                ALU.mult, ALU.subtract), tr, td)
                wj = Wc[:, ch * CK:row + 1, :]
                gq = g2.ap[:, 1, t, ch * CK:row + 1].rearrange("p (j o) -> p j o", o=1).broadcast_to([P, t + 1, 32])
                to = dve.do(lambda e, t=t, wj=wj, gq=gq: e.tensor_tensor(tmp_o[:, 0:t + 1, :], wj, gq, ALU.mult), tw)
                prev_o = (lambda e, t=t, row=row: e.tensor_reduce(O2[:, row, :], tmp_o[:, 0:t + 1, :].rearrange("p j i -> p i j"),
                          AX.X, ALU.add), to)
                for _ in range(njobs):
                    if jobs:
                        jobs.pop(0)()
            tt = dve.do(lambda e: e.transpose(Wm[:, 1].rearrange("p i r -> p i r"), Wc[:].rearrange("p j i -> p i j")),
                        tw, chain["wm_free"])
            chain["w_free"][ch] = tt
            t_o = dve.do(*prev_o)
            tm0 = dve.do(lambda e: e.tensor_scalar(Wm[:, 0], Wm[:, 1], ih_mask[:, 0:1], None, ALU.mult), tt)
            tm1 = dve.do(lambda e: e.tensor_scalar(Wm[:, 1], Wm[:, 1], ih_mask[:, 1:2], None, ALU.mult), tm0)
            for n in range(4):
                b = Ub.next()
                for m in range(8):
                    r = 8 * n + m
                    for par in range(2):
                        ps = slice(par * DK, (par + 1) * DK)
                        tu = pe.do(lambda e, r=r, m=m, ps=ps, b=b: e.matmul(
                            b.ap[ps, m * DK:(m + 1) * DK], Kt.ap[ps, r, :], Wm[ps, :, :, r].rearrange("p h i -> p (h i)"),
                            start=True, stop=True), tm1, seg["kt_ready"], *b.free)
                ts = dve.do(lambda e, n=n, b=b: e.tensor_tensor(
                    ST[:, 8 * n:8 * n + 8, :].rearrange("p r i -> p (r i)"), ST[:, 8 * n:8 * n + 8, :].rearrange("p r i -> p (r i)"),
                    b.ap, ALU.subtract), tu, t_sd)
                b.free = [ts]
            chain["state"], chain["wm_free"] = ts, tu
            Kt.free = [tu]
            seg["o"] = dve.do(lambda e: e.tensor_tensor(O2[:, js, :], P2[:, 1], O2[:, js, :], ALU.subtract), t_o, tq)
            for n in ("kq", "a2", "bv", "dc", "g2"):
                seg[n].free = [seg["o"], tu, tw, t_sd]

        def finish(s, seg):
            xs = seg["xs"]
            t0 = s * SEG
            st = {"scaled": {}, "affine": {}}

            def turn():
                st["o"] = dve.do(lambda e: e.transpose(o1[:].rearrange("p r t -> p t r"), O2[:]), seg["o"],
                                  chain["o1_free"])

            def gate(half):
                b = back.next()
                for m in range(4):
                    tp = project("g", b, xs, 4 * half + m, m)
                xs.free = [tp]
                v = o1[:, 16 * half:16 * half + 16, :].rearrange("p r t -> p (r t)")
                w = sq[:, 16 * half:16 * half + 16, :].rearrange("p r t -> p (r t)")
                t = act.do(lambda e: e.activation(w, b.ap, ACT.Sigmoid), tp, st["scaled"][half])
                b.free = [t]
                st["y"] = dve.do(lambda e: e.tensor_tensor(v, v, w, ALU.mult), t, st["affine"][half])

            def centre(half):
                b = back.next()
                v = o1[:, 16 * half:16 * half + 16, :].rearrange("p r t -> p (r t)")
                w = sq[:, 16 * half:16 * half + 16, :].rearrange("p r t -> p (r t)")
                tp = pe.do(lambda e, b=b: e.matmul(b.ap, pair_mean[:], v, start=True, stop=True), st["o"], *b.free)
                t = dve.do(lambda e, b=b: e.tensor_tensor(v, v, b.ap, ALU.subtract), tp)
                b.free = [t]
                st["sq"] = act.do(lambda e: e.activation(w, v, ACT.Square), t, chain["y"])

            def scale(half):
                b = back.next()
                v = o1[:, 16 * half:16 * half + 16, :].rearrange("p r t -> p (r t)")
                w = sq[:, 16 * half:16 * half + 16, :].rearrange("p r t -> p (r t)")
                tp = pe.do(lambda e, b=b: e.matmul(b.ap, pair_mean[:], w, start=True, stop=True), st["sq"], *b.free)
                t = act.do(lambda e, b=b: e.activation(w, b.ap, ACT.Sqrt, bias=eps[:, 0:1]), tp)
                b.free = [t]
                t = dve.do(lambda e: e.reciprocal(w, w), t)
                t = dve.do(lambda e: e.tensor_tensor(v, v, w, ALU.mult), t)
                st["scaled"][half] = t
                st["affine"][half] = act.do(lambda e: e.activation(v, v, ACT.Identity, scale=lnw[:, 0:1],
                                            bias=lnb[:, 0:1]), t)

            def out():
                for b_ in range(NB):
                    tl = l_row.start(sp, xrow.ap[b_ * SEG:(b_ + 1) * SEG, :], x_in[b_, t0:t0 + SEG, :], *xrow.free)
                b = back.next()
                for ct in range(NCT):
                    tp = pe.do(lambda e, ct=ct, b=b: e.matmul(b.ap[:, 0:D], o1[:, ct * NB:(ct + 1) * NB, :].rearrange("p b t -> p (b t)"),
                               woT[:, ct, :], start=(ct == 0), stop=(ct == NCT - 1)), st["y"], *b.free)
                t = dve.do(lambda e, b=b: e.tensor_tensor(xrow.ap[:], xrow.ap[:], b.ap[:, 0:D], ALU.add), tp, tl)
                b.free = [t]
                chain["o1_free"], chain["y"] = tp, st["y"]
                for b_ in range(NB):
                    xrow.free = [w_row.start(sp, x1[b_, t0:t0 + SEG, :], xrow.ap[b_ * SEG:(b_ + 1) * SEG, :], t)]
            return [turn, lambda: centre(0), lambda: centre(1), lambda: scale(0), lambda: scale(1), lambda: gate(0), lambda: gate(1), out]

        chain = dict(state=zeroed, ab_free=None, w_free=[zeroed] * NCK, wm_free=None, y=None, o1_free=None)
        seg = segment_inputs(0)
        for job in seg["jobs"]:
            job()
        tail = []
        for s in range(nseg):
            nxt = segment_inputs(s + 1) if s + 1 < nseg else None
            jobs = tail + (nxt["jobs"] if nxt else [])
            for ch in range(NCK):
                cut = [0, len(jobs) // 2, len(jobs)]
                mine = jobs[cut[ch]:cut[ch + 1]]
                chunk(s, ch, seg, mine)
                for job in mine:
                    job()
            tail = finish(s, seg)
            if s + 1 < nseg:
                seg = nxt
        for job in tail:
            job()
        c.barrier(xrow.free[0])
def transposed(c, ctx, name, src, dst, scale_of=None, rows=None, affine=None):
    pe, dve, act = c.pe, c.dve, c.act
    bank = Ring([Slot(c.bank(i)) for i in range(2)])
    if scale_of:
        mv, rstd = scale_of
        xn = Ring([Slot(c.sb(ctx, f"{name}_xn{i}", [P, 4, D])) for i in range(2)])
    done = []
    for n in range(NTILE // 4):
        b, t = bank.next(), None
        s = xn.next() if scale_of else None
        for j in range(4):
            g = 4 * n + j
            if scale_of:
                t = dve.do(lambda e, g=g, j=j, s=s: e.tensor_scalar(s.ap[:, j, :], src[:, g, :], mv[:, g, 0:1],
                           rstd[:, g:g + 1], ALU.subtract, ALU.mult), *rows(g), *s.free)
        for j in range(4):
            g = 4 * n + j
            row = s.ap[:, j, :] if scale_of else src[:, g, :]
            tp = pe.do(lambda e, j=j, b=b, row=row: e.transpose(b.ap[:, j * P:(j + 1) * P], row, c.ident[:]),
                       t, *(() if scale_of else rows(g)), *b.free)
        if s:
            s.free = [tp]
        out = dst[:, n * BANK:(n + 1) * BANK]
        if affine:
            fn = lambda e, b=b, out=out: e.activation(out, b.ap, ACT.Identity, scale=affine[0], bias=affine[1])
        else:
            fn = lambda e, b=b, out=out: e.activation(out, b.ap, ACT.Copy)
        b.free = [act.do(fn, tp)]
        done += b.free * 4
    return done


class Norm:

    def __init__(self, c, ctx, name):
        self.stats = c.sb(ctx, name + "_stats", [P, NTILE, 6])
        self.mv = c.sb(ctx, name + "_mv", [P, NTILE, 2])
        self.rstd = c.sb(ctx, name + "_rstd", [P, NTILE])

    def of(self, c, src, ready):
        return layer_norm_rows(c, src, self.stats, self.mv, self.rstd, c.eps, ready)


NE, FF = 8, 512
NF = FF // P
CAPACITY = -(-5 * NT // (4 * NE))


def expert_ffn(c, k, X, x_ready, cst):
    pe, dve, act, sp = c.pe, c.dve, c.act, c.sp
    with ExitStack() as ctx:
        sb = lambda name, shape: c.sb(ctx, "b_" + name, shape)
        w1, w2 = sb("w1", [P, NE, FF]), sb("w2", [P, NE, NF, D])
        b1, b2 = sb("b1", [P, NE, NF]), sb("b2", [NE, D])
        gw, gb = sb("gw", [P, NE]), sb("gb", [1, NE])
        xnT = sb("xnT", [P, NT])
        norm = Norm(c, ctx, "b")
        tri, ones = cst["tri"], cst["ones"]
        l_w = DmaCount(c.sem("s_b_w"))
        for dst, n in ((gw, "gate_w"), (gb, "gate_b"), (b1, "b1"), (b2, "b2")):
            l_w.start(sp, dst[:], k["L0_ffn_" + n])
        l_w.start(sp, w1[:], k["L0_ffn_w1"].rearrange("e d f -> d e f"))
        w_ok = l_w.start(sp, w2[:], k["L0_ffn_w2"].rearrange("e (n f) d -> f e n d", f=P))
        t = norm.of(c, X, lambda g: (x_ready,))
        xn_ok = transposed(c, ctx, "b", X, xnT, (norm.mv, norm.rstd), lambda g: (t,))

        G = [P, NTILE, NE]
        lg, ex, eq, oh, gate, pre = (sb(n, G) for n in ("lg", "ex", "eq", "oh", "gate", "pre"))
        top, prob = sb("top", [P, NTILE]), sb("prob", [P, NTILE])
        gateT = sb("gateT", [NE, NT])
        bank = c.bank(2)
        for g in range(NTILE):
            pe.run(lambda e, g=g: e.matmul(bank[:, g * NE:(g + 1) * NE], xnT[:, g * P:(g + 1) * P], gw[:],
                   start=True, stop=False), xn_ok[g], w_ok)
            tp = pe.do(lambda e, g=g: e.matmul(bank[:, g * NE:(g + 1) * NE], c.ones_row[0:1, 0:P], gb[:],
                       start=False, stop=True))
        flat = lambda a: a[:].rearrange("p g e -> p (g e)")
        over_e = lambda a: a[:].rearrange("p (g o) -> p g o", o=1).broadcast_to(G)
        dve.do(lambda e: e.tensor_copy(flat(lg), bank[:, 0:NTILE * NE]), tp)
        dve.do(lambda e: e.tensor_reduce(top[:], lg[:], AX.X, ALU.max))
        dve.do(lambda e: e.tensor_tensor(eq[:], lg[:], over_e(top), ALU.is_equal))
        t = dve.do(lambda e: e.tensor_tensor(lg[:], lg[:], over_e(top), ALU.subtract))
        t = act.do(lambda e: e.activation(flat(ex), flat(lg), ACT.Exp), t)
        dve.do(lambda e: e.tensor_reduce(prob[:], ex[:], AX.X, ALU.add), t)
        dve.do(lambda e: e.reciprocal(prob[:], prob[:]))
        dve.do(lambda e: e.memset(pre[:], 0.0))
        for j in range(1, NE):
            dve.do(lambda e, j=j: e.tensor_tensor(pre[:, :, j], pre[:, :, j - 1], eq[:, :, j - 1], ALU.add))
        dve.do(lambda e: e.tensor_scalar(pre[:], pre[:], 0.0, None, ALU.is_equal))
        t = dve.do(lambda e: e.tensor_tensor(oh[:], eq[:], pre[:], ALU.mult))
        within, totals = c.bank(3)[:, 0:NTILE * NE], c.bank(4)[:, 0:NTILE * NE]
        pe.run(lambda e: e.matmul(within, tri[:], flat(oh), start=True, stop=True), t)
        tp = pe.do(lambda e: e.matmul(totals, ones[:], flat(oh), start=True, stop=True))
        dve.do(lambda e: e.tensor_copy(flat(ex), totals), tp)
        dve.do(lambda e: e.memset(pre[:, 0, :], 0.0))
        for g in range(1, NTILE):
            dve.do(lambda e, g=g: e.tensor_tensor(pre[:, g, :], pre[:, g - 1, :], ex[:, g - 1, :], ALU.add))
        dve.do(lambda e: e.tensor_tensor(flat(pre), flat(pre), within, ALU.add))
        dve.do(lambda e: e.tensor_scalar(pre[:], pre[:], float(CAPACITY), None, ALU.is_le))
        dve.do(lambda e: e.tensor_tensor(gate[:], oh[:], pre[:], ALU.mult))
        g_ok = dve.do(lambda e: e.tensor_tensor(gate[:], gate[:], over_e(prob), ALU.mult))

        banks = Ring([Slot(c.bank(i)) for i in range(2)])
        for n in range(NTILE // 4):
            b = banks.next()
            b.free = b.free or [act.last()]
            for j in range(4):
                g = 4 * n + j
                tp = pe.do(lambda e, b=b, j=j, g=g: e.transpose(b.ap[0:NE, j * P:(j + 1) * P], gate[:, g, :], c.ident[:]),
                           g_ok, *b.free)
            b.free = [act.do(lambda e, b=b, n=n: e.activation(gateT[:, n * BANK:(n + 1) * BANK], b.ap[0:NE, :], ACT.Copy), tp)]
        gt_ok = act.last()
        for n in range(NTILE // 4):
            b = banks.next()
            for j in range(4):
                g = 4 * n + j
                tp = pe.do(lambda e, b=b, j=j, g=g: e.matmul(b.ap[:, j * P:(j + 1) * P], gateT[:, g * P:(g + 1) * P], b2[:],
                           start=True, stop=True), gt_ok, *b.free)
            b.free = [dve.do(lambda e, b=b, n=n: e.tensor_tensor(X[:, 4 * n:4 * n + 4, :].rearrange("p g d -> p (g d)"),
                             X[:, 4 * n:4 * n + 4, :].rearrange("p g d -> p (g d)"), b.ap, ALU.add), tp)]
        up = Ring([Slot(c.bank(i)) for i in range(4)])
        down = Ring([Slot(c.bank(4 + i)) for i in range(4)])
        for s in up.slots + down.slots:
            s.free = [act.last(), dve.last()]
        hid = Ring([Slot(sb(f"hid{i}", [P, NF, BANK])) for i in range(2)])

        def rise(n, ex_):
            h = hid.next()
            for f in range(NF):
                b = up.next()
                tp = pe.do(lambda e, b=b, f=f: e.matmul(b.ap, w1[:, ex_, f * P:(f + 1) * P], xnT[:, n * BANK:(n + 1) * BANK],
                           start=True, stop=True), *b.free)
                t = act.do(lambda e, b=b, f=f, h=h: e.activation(h.ap[:, f, :], b.ap, ACT.Relu, bias=b1[:, ex_, f:f + 1]),
                           tp, *h.free)
                b.free = [t]
            return h, t

        def fall(n, ex_, h, ready):
            b = down.next()
            for j in range(4):
                for f in range(NF):
                    tp = pe.do(lambda e, b=b, j=j, f=f: e.matmul(b.ap[:, j * P:(j + 1) * P], h.ap[:, f, j * P:(j + 1) * P],
                               w2[:, ex_, f, :], start=(f == 0), stop=(f == NF - 1)), ready, *b.free)
            h.free = [tp]
            for j in range(4):
                g = 4 * n + j
                t = dve.do(lambda e, b=b, j=j, g=g: e.scalar_tensor_tensor(X[:, g, :], b.ap[:, j * P:(j + 1) * P],
                           gate[:, g, ex_:ex_ + 1], X[:, g, :], ALU.mult, ALU.add), tp)
            b.free = [t]

        waiting = None
        for n in range(NT // BANK):
            for ex_ in range(NE):
                h, t = rise(n, ex_)
                if waiting:
                    fall(*waiting)
                waiting = (n, ex_, h, t)
        fall(*waiting)
        c.barrier()


NEG = -1e30


class Attention:
    LAG = 2

    def __init__(self, c, ctx, name, nkeys, width):
        self.c, self.nkeys, self.width = c, nkeys, width
        self.score = Ring([Slot(c.bank(i)) for i in range(3)])
        self.turn = Ring([Slot(c.bank(3 + i)) for i in range(2)])
        self.out = Ring([Slot(c.bank(5)), Slot(c.bank(6))])
        self.S = Ring([Slot(c.sb(ctx, f"{name}_s{i}", [P, nkeys])) for i in range(3)])
        self.PT = Ring([Slot(c.sb(ctx, f"{name}_pt{i}", [P, nkeys])) for i in range(2)])
        self.low = Ring([Slot(c.sb(ctx, f"{name}_low{i}", [P, 1])) for i in range(3)])
        self.pending, self.n = [], 0

    def unit(self, score, mask, scale, rowsum, values, o, after, then=None):
        c, w = self.c, mask.shape[-1]
        b, s, lo = self.score.next(), self.S.next(), self.low.next()
        for fn in score[:-1]:
            c.pe.run(lambda e, fn=fn: fn(e, b.ap), *after, *b.free)
        tp = c.pe.do(lambda e: score[-1](e, b.ap), *after, *b.free)
        t = c.dve.do(lambda e: e.tensor_tensor_reduce(out=s.ap[:, 0:w], in0=b.ap[:, 0:w], in1=mask, scale=scale,
                     scalar=3e38, op0=ALU.add, op1=ALU.min, accum_out=lo.ap[:, 0:1]), tp, *s.free, *lo.free)
        b.free = [t]
        ta = c.act.do(lambda e: e.activation(s.ap[:, 0:w], s.ap[:, 0:w], ACT.Exp, scale=-1.0, bias=lo.ap[:, 0:1],
                      accum_out=rowsum), t)
        lo.free = [ta]
        self.pending.append((s, ta, w, values, o, then))
        if len(self.pending) > self.LAG:
            self.finish()
        return tp

    def finish(self):
        c = self.c
        s, ta, w, values, o, then = self.pending.pop(0)
        b, pt = self.turn.next(), self.PT.next()
        for j in range(w // P):
            tp = c.pe.do(lambda e, j=j: e.transpose(b.ap[:, j * P:(j + 1) * P], s.ap[:, j * P:(j + 1) * P], c.ident[:]),
                         ta, *b.free)
        s.free = [tp]
        self.n += 1
        if self.n % 2:
            t = c.act.do(lambda e: e.activation(pt.ap[:, 0:w], b.ap[:, 0:w], ACT.Copy), tp, *pt.free)
        else:
            t = c.dve.do(lambda e: e.tensor_copy(pt.ap[:, 0:w], b.ap[:, 0:w]), tp, *pt.free)
        b.free = [t]
        for j, v in enumerate(values):
            tp = c.pe.do(lambda e, j=j, v=v: e.matmul(o.ap_of(b), pt.ap[:, j * P:(j + 1) * P], v, start=(j == 0),
                         stop=(j == len(values) - 1)), t, *o.free)
        pt.free = [tp]
        if then:
            then(tp, ta)

    def drain(self):
        while self.pending:
            self.finish()


class Part:

    def __init__(self, slot, ap):
        self.slot, self.ap = slot, ap

    @property
    def free(self):
        return self.slot.free

    def ap_of(self, _):
        return self.ap


H1, HD = 16, 8
LEFT, RIGHT = 127, 128


def banded_attention(c, k, X, cst_dram):
    pe, dve, act, pool, sp = c.pe, c.dve, c.act, c.pool, c.sp
    with ExitStack() as ctx:
        sb = lambda name, shape: c.sb(ctx, "c_" + name, shape)
        wqk, wv = sb("wqk", [P, 4, P]), sb("wv", [P, P])
        wo, bo = sb("wo", [P, D]), sb("bo", [1, D])
        cos, sin, heads, band = sb("cos", [P, T]), sb("sin", [P, T]), sb("heads", [P, H1]), sb("band", [P, 3 * P])
        qT, kT = sb("qT", [P, NT]), sb("kT", [P, NT])
        V = sb("V", [P, NTILE, D])
        l_w = DmaCount(c.sem("s_c_w"))
        l_w.start(sp, wqk[:], k["L1_wqk"])
        l_w.start(sp, wv[:], k["L1_wv"])
        l_w.start(sp, wo[:], k["L1_attn_w_out"])
        l_w.start(sp, bo[:], k["L1_attn_b_out"])
        for dst, n in ((cos, "rope_cos"), (sin, "rope_sin"), (heads, "head_rows")):
            l_w.start(sp, dst[:], cst_dram[n])
        w_ok = l_w.start(sp, band[:], cst_dram["band"])
        with ExitStack() as pctx:
            xnT = c.sb(pctx, "c_xnT", [P, NT])
            tmp = Ring([Slot(c.sb(pctx, f"c_tmp{i}", [P, BANK])) for i in range(2)])
            norm = Norm(c, pctx, "c")
            t = norm.of(c, X, lambda g: ())
            xn_ok = transposed(c, pctx, "c", X, xnT, (norm.mv, norm.rstd), lambda g: (t,))
            pair = Ring([Slot(c.bank(2, 2)), Slot(c.bank(4, 2))])
            for n in range(NT // BANK):
                cols, pos = slice(n * BANK, (n + 1) * BANK), slice(n * BANK % T, n * BANK % T + BANK)
                for z, dst in enumerate((qT, kT)):
                    b, s = pair.next(), tmp.next()
                    for m in range(2):
                        tp = pe.do(lambda e, b=b, m=m, z=z, cols=cols: e.matmul(b.ap[:, m * BANK:(m + 1) * BANK],
                                   wqk[:, 2 * z + m, :], xnT[:, cols], start=True, stop=True), xn_ok[4 * n + 3], w_ok, *b.free)
                    dve.do(lambda e, b=b, dst=dst, cols=cols, pos=pos: e.tensor_tensor(dst[:, cols], b.ap[:, 0:BANK], cos[:, pos],
                           ALU.mult), tp)
                    t = dve.do(lambda e, b=b, s=s, pos=pos: e.tensor_tensor(s.ap[:], b.ap[:, BANK:], sin[:, pos], ALU.mult), *s.free)
                    b.free = [t]
                    s.free = [pool.do(lambda e, dst=dst, s=s, cols=cols: e.tensor_tensor(dst[:, cols], dst[:, cols], s.ap[:], ALU.add), t)]
            vb = Ring([Slot(c.bank(6)), Slot(c.bank(7))])
            for n in range(NTILE // 4):
                b = vb.next()
                for j in range(4):
                    g = 4 * n + j
                    tp = pe.do(lambda e, b=b, j=j, g=g: e.matmul(b.ap[:, j * P:(j + 1) * P], xnT[:, g * P:(g + 1) * P], wv[:],
                               start=True, stop=True), xn_ok[g], *b.free)
                b.free = [act.do(lambda e, b=b, n=n: e.activation(V[:, 4 * n:4 * n + 4, :].rearrange("p g d -> p (g d)"), b.ap,
                                 ACT.Copy), tp)]
            c.barrier()
        att = Attention(c, ctx, "c", 3 * P, HD)
        qm = Ring([Slot(sb(f"qm{i}", [P, H1, P])) for i in range(2)])
        rows = Ring([Slot(sb(f"rows{i}", [P, H1])) for i in range(2)])
        on = Ring([Slot(sb(f"on{i}", [P, D])) for i in range(2)])
        oT = Ring([Slot(sb(f"oT{i}", [P, P])) for i in range(2)])
        last = Slot(c.bank(7))
        for g in range(NTILE):
            bi, tt = divmod(g, TPB)
            q = qm.next()
            src = qT[:, g * P:(g + 1) * P].rearrange("p (o t) -> p o t", o=1).broadcast_to([P, H1, P])
            hm = heads[:].rearrange("p (h o) -> p h o", o=1).broadcast_to([P, H1, P])
            tq = pool.do(lambda e, q=q, src=src, hm=hm: e.tensor_tensor(q.ap[:], src, hm, ALU.mult), *q.free)
            lo, hi = max(tt - 1, 0), min(tt + 1, TPB - 1)
            nk = hi - lo + 1
            m0 = (lo - tt + 1) * P
            mask = band[:, m0:m0 + nk * P]
            keys = kT[:, (bi * TPB + lo) * P:(bi * TPB + hi + 1) * P]
            rs, ob = rows.next(), att.out.next()
            for h in range(H1):
                part = Part(ob, ob.ap[:, h * HD:(h + 1) * HD])
                vals = [V[:, bi * TPB + j, h * HD:(h + 1) * HD] for j in range(lo, hi + 1)]
                then = None
                if h == H1 - 1:
                    def then(tp, ta, rs=rs, ob=ob, g=g):
                        o, ot = on.next(), oT.next()
                        dve.do(lambda e: e.reciprocal(rs.ap[:], rs.ap[:]), ta)
                        t = dve.do(lambda e: e.tensor_tensor(o.ap[:].rearrange("p (h d) -> p h d", d=HD),
                                   ob.ap[:, 0:D].rearrange("p (h d) -> p h d", d=HD),
                                   rs.ap[:].rearrange("p (h o) -> p h o", o=1).broadcast_to([P, H1, HD]), ALU.mult), tp, *o.free)
                        rs.free, ob.free = [t], [t]
                        tp = pe.do(lambda e: e.transpose(last.ap[:, 0:P], o.ap[:], c.ident[:]), t, *last.free)
                        o.free = [tp]
                        t = act.do(lambda e: e.activation(ot.ap[:], last.ap[:, 0:P], ACT.Copy), tp, *ot.free)
                        pe.run(lambda e: e.matmul(last.ap[:, P:2 * P], ot.ap[:], wo[:], start=True, stop=False), t)
                        tp = pe.do(lambda e: e.matmul(last.ap[:, P:2 * P], c.ones_row[0:1, 0:P], bo[:], start=False, stop=True))
                        ot.free = [tp]
                        last.free = [dve.do(lambda e: e.tensor_tensor(X[:, g, :], X[:, g, :], last.ap[:, P:2 * P], ALU.add), tp)]
                score = [lambda e, ap, q=q, h=h, keys=keys, nk=nk: e.matmul(ap[:, 0:nk * P], q.ap[:, h, :], keys, start=True, stop=True)]
                tp = att.unit(score, mask, -HD ** -0.5, rs.ap[:, h:h + 1], vals, part, [tq, *rs.free], then)
            q.free = [tp]
        att.drain()
        c.barrier()
DEPTH, H2, DH, WINDOW = 2, 8, 64, 64
INNER = H2 * DH
HID = int(D * 4 * 2 / 3)
NH = -(-HID // P)
QK_SCALE = 8.0


def shift_tokens(c, X, Hs, dma, zeroed):
    sp, half = c.sp, D // 2
    xr, tail = X[:], slice(half, D)
    ready = [c.dve.last(), zeroed]
    dma.start(sp, Hs[:, :, 0:half], X[:, :, 0:half], *ready)
    dma.start(sp, Hs[1:P, :, tail], X[0:P - 1, :, tail], *ready)
    for b in range(NB):
        g = b * TPB
        t = dma.start(sp, Hs[0:1, g + 1:g + TPB, tail], X[P - 1:P, g:g + TPB - 1, tail], *ready)
    return t


def local_layer(c, k, X, l, cst_dram):
    pe, dve, act, pool, sp = c.pe, c.dve, c.act, c.pool, c.sp
    with ExitStack() as ctx:
        sb = lambda name, shape: c.sb(ctx, f"d{l}_" + name, shape)
        wqkv = sb("wqkv", [P, 3 * INNER])
        wo = sb("wo", [P, INNER // P, D])
        w1 = sb("w1", [P, 2 * HID])
        w2 = sb("w2", [P, NH, D])
        b1a, b1g, b2 = sb("b1a", [P, NH]), sb("b1g", [P, NH]), sb("b2", [1, D])
        lnw, lnb = sb("lnw", [P, 1]), sb("lnb", [P, 1])
        Hs = sb("hs", [P, NTILE, D])
        hT = sb("hT", [P, NT])
        norm = Norm(c, ctx, f"d{l}")
        l_w, l_h = DmaCount(c.sem(f"s_d{l}_w")), DmaCount(c.sem(f"s_d{l}_shift"))
        z = dve.do(lambda e: e.memset(Hs[0:1, 0:NTILE:TPB, D // 2:D], 0.0))
        h_ok = shift_tokens(c, X, Hs, l_h, z)
        l_w.start(sp, wqkv[:], k["L1_ffn_wqkv"][l])
        l_w.start(sp, wo[:], k["L1_ffn_wo"][l].rearrange("(n p) d -> p n d", p=P))
        l_w.start(sp, w1[:], k["L1_ffn_w1"][l])
        full = HID // P
        l_w.start(sp, w2[:, 0:full, :], k["L1_ffn_w2"][l, 0:full * P].rearrange("(n p) d -> p n d", p=P))
        l_w.start(sp, w2[0:HID - full * P, full, :], k["L1_ffn_w2"][l, full * P:HID])
        for half, dst in enumerate((b1a, b1g)):
            l_w.start(sp, dst[:, 0:full], k["L1_b1_full"][l, half])
            l_w.start(sp, dst[0:HID - full * P, full:full + 1], k["L1_b1_rest"][l, half])
        l_w.start(sp, b2[:], k["L1_ffn_b2"][l:l + 1, :])
        l_w.start(sp, lnw[:], k["L1_ffn_ln_g"][l])
        w_ok = l_w.start(sp, lnb[:], k["L1_ffn_ln_b"][l])

        with ExitStack() as actx:
            asb = lambda name, shape: c.sb(actx, f"d{l}_" + name, shape)
            tab = asb("tab", [P, 2, 2, TPB, DH])
            sc = asb("sc", [P, 2, DH])
            mask = asb("mask", [P, 2 * P])
            l_t = DmaCount(c.sem(f"s_d{l}_tab"))
            l_t.start(sp, tab[:], cst_dram["xpos"])
            l_t.start(sp, mask[:], cst_dram["local"])
            l_t.start(sp, sc[:, 0, :], k["L1_ffn_q_scale"][l:l + 1, :].broadcast_to([P, DH]))
            t_ok = l_t.start(sp, sc[:, 1, :], k["L1_ffn_k_scale"][l:l + 1, :].broadcast_to([P, DH]))
            hf = DH // 2
            for z in range(2):
                one = sc[:, z, :].rearrange("p (o d) -> p o d", o=1).broadcast_to([P, TPB, DH])
                dve.do(lambda e, z=z, one=one: e.tensor_tensor(tab[:, z, 0], tab[:, z, 0], one, ALU.mult), t_ok)
                for a in range(2):
                    v = tab[:, z, 1, :, a * hf:(a + 1) * hf]
                    o = sc[:, z, (1 - a) * hf:(2 - a) * hf].rearrange("p (o d) -> p o d", o=1).broadcast_to([P, TPB, hf])
                    tab_ok = dve.do(lambda e, v=v, o=o: e.tensor_tensor(v, v, o, ALU.mult))
            hT_ok = transposed(c, actx, f"d{l}a", Hs, hT, rows=lambda g: (h_ok,))
            c.barrier()

            att = Attention(c, actx, f"d{l}", 2 * P, DH)
            acc = Ring([Slot(c.bank(7))])
            raw = Ring([Slot(asb(f"raw{i}", [P, 2, INNER])) for i in range(2)])
            rot = Ring([Slot(asb(f"rot{i}", [P, 2, INNER])) for i in range(2)])
            sw = Ring([Slot(asb(f"sw{i}", [P, 2, INNER])) for i in range(2)])
            nrm = Ring([Slot(asb(f"nrm{i}", [P, 2, H2])) for i in range(2)])
            qT = Ring([Slot(asb(f"qT{i}", [P, 4, P])) for i in range(2)])
            kT = Ring([Slot(asb(f"kT{i}", [P, 4, P])) for i in range(3)])
            V = Ring([Slot(asb(f"V{i}", [P, INNER])) for i in range(3)])
            rows = Ring([Slot(asb(f"rows{i}", [P, H2])) for i in range(2)])
            on = Ring([Slot(asb(f"on{i}", [P, INNER])) for i in range(2)])
            oT = Ring([Slot(asb(f"oT{i}", [P, 4, P])) for i in range(2)])
            last = acc.slots[0]
            heads = lambda a: a.rearrange("p (h d) -> p h d", d=DH)

            def prepare(g):
                tt = g % TPB
                r, ro, s, nr, q, kk, v = (x.next() for x in (raw, rot, sw, nrm, qT, kT, V))
                for z in range(3):
                    tp = pe.do(lambda e, z=z: e.matmul(last.ap, hT[:, g * P:(g + 1) * P], wqkv[:, z * INNER:(z + 1) * INNER],
                               start=True, stop=True), w_ok, hT_ok[g], *last.free)
                    dst = r.ap[:, z, :] if z < 2 else v.ap[:]
                    last.free = [act.do(lambda e, dst=dst: e.activation(dst, last.ap, ACT.Copy), tp, *(r.free if z < 2 else v.free))]
                v_ok = last.free[0]
                t2 = act.do(lambda e: e.activation(s.ap[:], r.ap[:], ACT.Square), *s.free)
                t = dve.do(lambda e: e.tensor_reduce(nr.ap[:].rearrange("p z h -> p (z h)"),
                           s.ap[:].rearrange("p z (h d) -> p (z h) d", d=DH), AX.X, ALU.add), t2, *nr.free)
                t = act.do(lambda e: e.activation(nr.ap[:], nr.ap[:], ACT.Sqrt), t)
                dve.do(lambda e: e.tensor_scalar(nr.ap[:], nr.ap[:], 1e-12, None, ALU.max), t)
                t_n = dve.do(lambda e: e.reciprocal(nr.ap[:], nr.ap[:]))
                t_n = dve.do(lambda e: e.tensor_scalar(nr.ap[:, 0, :], nr.ap[:, 0, :], -QK_SCALE, None, ALU.mult))
                for z in range(2):
                    cs = tab[:, z, 0, tt, :].rearrange("p (o d) -> p o d", o=1).broadcast_to([P, H2, DH])
                    dve.do(lambda e, z=z, cs=cs: e.tensor_tensor(heads(ro.ap[:, z, :]), heads(r.ap[:, z, :]), cs, ALU.mult), *ro.free)
                    for a in range(2):
                        sn = tab[:, z, 1, tt, a * hf:(a + 1) * hf].rearrange("p (o d) -> p o d", o=1).broadcast_to([P, H2, hf])
                        t = pool.do(lambda e, z=z, a=a, sn=sn: e.tensor_tensor(heads(s.ap[:, z, :])[:, :, a * hf:(a + 1) * hf],
                                    heads(r.ap[:, z, :])[:, :, (1 - a) * hf:(2 - a) * hf], sn, ALU.mult), v_ok, t_n)
                t = dve.do(lambda e: e.tensor_tensor(ro.ap[:], ro.ap[:], s.ap[:], ALU.add), t)
                r.free, s.free = [t], [t]
                kn = nr.ap[:, 1, :].rearrange("p (h o) -> p h o", o=1).broadcast_to([P, H2, DH])
                t = dve.do(lambda e: e.tensor_tensor(heads(ro.ap[:, 1, :]), heads(ro.ap[:, 1, :]), kn, ALU.mult))
                for z, dst in enumerate((q, kk)):
                    for j in range(4):
                        tp = pe.do(lambda e, z=z, j=j: e.transpose(last.ap[:, j * P:(j + 1) * P], ro.ap[:, z, j * P:(j + 1) * P],
                                   c.ident[:]), t, *last.free)
                    last.free = [act.do(lambda e, dst=dst: e.activation(dst.ap[:].rearrange("p n t -> p (n t)"), last.ap, ACT.Copy),
                                        tp, *dst.free)]
                ro.free = [tp]
                return dict(q=q, k=kk, v=v, nr=nr, ok=last.free[0])

            prev = None
            for g in range(NTILE):
                cur = prepare(g)
                blocks = ([prev] if g % TPB else []) + [cur]
                m = mask[:, (2 - len(blocks)) * P:]
                rs, ob = rows.next(), att.out.next()
                for h in range(H2):
                    ps, pr = slice(h % 2 * DH, h % 2 * DH + DH), h // 2
                    part = Part(ob, ob.ap[:, h * DH:(h + 1) * DH])
                    then = None
                    if h == H2 - 1:
                        def then(tp, ta, rs=rs, ob=ob, g=g, cur=cur, prev=prev):
                            o, ot = on.next(), oT.next()
                            for x in (prev, cur) if g % TPB != TPB - 1 else (prev, cur):
                                if x:
                                    x["v"].free = x["k"].free = [tp]
                            dve.do(lambda e: e.reciprocal(rs.ap[:], rs.ap[:]), ta)
                            t = dve.do(lambda e: e.tensor_tensor(heads(o.ap[:]), heads(ob.ap),
                                       rs.ap[:].rearrange("p (h o) -> p h o", o=1).broadcast_to([P, H2, DH]), ALU.mult), tp, *o.free)
                            rs.free, ob.free = [t], [t]
                            for j in range(4):
                                tp = pe.do(lambda e, j=j: e.transpose(last.ap[:, j * P:(j + 1) * P], o.ap[:, j * P:(j + 1) * P],
                                           c.ident[:]), t, *last.free)
                            o.free = [tp]
                            t = act.do(lambda e: e.activation(ot.ap[:].rearrange("p n t -> p (n t)"), last.ap, ACT.Copy), tp, *ot.free)
                            for j in range(4):
                                tp = pe.do(lambda e, j=j: e.matmul(last.ap[:, 0:D], ot.ap[:, j, :], wo[:, j, :], start=(j == 0),
                                           stop=(j == 3)), t)
                            ot.free = [tp]
                            last.free = [dve.do(lambda e: e.tensor_tensor(X[:, g, :], X[:, g, :], last.ap[:, 0:D], ALU.add), tp)]
                    score = [lambda e, ap, j=j, x=x, ps=ps, pr=pr, cur=cur: e.matmul(ap[:, j * P:(j + 1) * P], cur["q"].ap[ps, pr, :],
                             x["k"].ap[ps, pr, :], start=True, stop=True) for j, x in enumerate(blocks)]
                    tp = att.unit(score, m, cur["nr"].ap[:, 0, h:h + 1], rs.ap[:, h:h + 1],
                                  [x["v"].ap[:, h * DH:(h + 1) * DH] for x in blocks], part, [cur["ok"], *rs.free], then)
                cur["q"].free, cur["nr"].free = [tp], [dve.last()]
                prev = cur
            att.drain()
            c.barrier()

        z = dve.do(lambda e: e.memset(Hs[0:1, 0:NTILE:TPB, D // 2:D], 0.0))
        h_ok = shift_tokens(c, X, Hs, l_h, z)
        t = norm.of(c, Hs, lambda g: (h_ok,))
        hT_ok = transposed(c, ctx, f"d{l}f", Hs, hT, (norm.mv, norm.rstd), lambda g: (t,), affine=(lnw[:, 0:1], lnb[:, 0:1]))
        c.barrier()
        up = Ring([Slot(c.bank(i, 2)) for i in (0, 2)])
        down = Ring([Slot(c.bank(i)) for i in (4, 5)])
        gl = Ring([Slot(sb(f"gl{i}", [P, BANK])) for i in range(2)])
        hid = Ring([Slot(sb(f"hid{i}", [P, NH, BANK])) for i in range(2)])

        def rise(n):
            h = hid.next()
            for f in range(NH):
                w = min(P, HID - f * P)
                b, s = up.next(), gl.next()
                for z in range(2):
                    c0 = z * HID + f * P
                    tp = pe.do(lambda e, b=b, z=z, c0=c0, w=w: e.matmul(b.ap[0:w, z * BANK:(z + 1) * BANK], w1[:, c0:c0 + w],
                               hT[:, n * BANK:(n + 1) * BANK], start=True, stop=True), *b.free)
                t = act.do(lambda e, b=b, s=s, f=f, w=w: e.activation(s.ap[0:w, :], b.ap[0:w, BANK:], ACT.Gelu, bias=b1g[0:w, f:f + 1]),
                           tp, *s.free)
                t = dve.do(lambda e, b=b, s=s, f=f, w=w, h=h: e.scalar_tensor_tensor(h.ap[0:w, f, :], b.ap[0:w, 0:BANK],
                           b1a[0:w, f:f + 1], s.ap[0:w, :], ALU.add, ALU.mult), t, *h.free)
                b.free, s.free = [t], [t]
            return n, h, t

        def fall(n, h, ready):
            b = down.next()
            for j in range(4):
                for f in range(NH):
                    w = min(P, HID - f * P)
                    pe.run(lambda e, b=b, j=j, f=f, w=w: e.matmul(b.ap[:, j * P:(j + 1) * P], h.ap[0:w, f, j * P:(j + 1) * P],
                           w2[0:w, f, :], start=(f == 0), stop=False), ready, *b.free)
                tp = pe.do(lambda e, b=b, j=j: e.matmul(b.ap[:, j * P:(j + 1) * P], c.ones_row[0:1, 0:P], b2[:], start=False, stop=True))
            h.free = [tp]
            xv = X[:, 4 * n:4 * n + 4, :].rearrange("p g d -> p (g d)")
            b.free = [dve.do(lambda e, b=b: e.tensor_tensor(xv, xv, b.ap, ALU.add), tp)]

        waiting = None
        for n in range(NT // BANK):
            nxt = rise(n)
            if waiting:
                fall(*waiting)
            waiting = nxt
        fall(*waiting)
        c.barrier()
def constants():
    p = np.arange(P)
    keep, phase = {}, {}
    keep["ident"] = np.eye(P)
    keep["ones_row"] = np.ones((1, P))
    keep["eps"] = np.full((P, 1), EPS)
    keep["half_of"] = np.stack([p % 32 < CK, p % 32 >= CK], 1)
    keep["ih_mask"] = np.stack([p // 32 % 2 == 0, p // 32 % 2 == 1], 1)
    same = p[:, None] // DK == p[None, :] // DK
    keep["pair_ones"] = same
    keep["pair_mean"] = same / DK
    keep["own"] = ((p[:, None, None] % 32 == np.arange(R)[None, :, None]) &
                   (p[:, None, None] // 32 % 2 == np.arange(2)[None, None, :])).reshape(P, 2 * R)
    phase["tri"] = p[:, None] <= p[None, :]
    phase["ones"] = np.ones((P, P))
    f32 = np.float32
    inv = f32(1.0) / f32(10000.0) ** (np.arange(0, HD, 2, dtype=f32) / f32(HD))
    ang = (np.arange(T, dtype=f32)[None, :] * inv[p % HD % (HD // 2)][:, None]).astype(f32)
    phase["rope_cos"] = np.cos(ang)
    phase["rope_sin"] = np.sin(ang) * np.where(p % HD < HD // 2, -1.0, 1.0)[:, None]
    phase["head_rows"] = p[:, None] // HD == np.arange(H1)[None, :]
    i, j = p[:, None], np.arange(3 * P)[None, :] - P
    phase["band"] = np.where((j >= i - LEFT) & (j <= i + RIGHT), 0.0, NEG)
    i, j = p[:, None], np.arange(2 * P)[None, :] - P
    phase["local"] = np.where((j <= i) & (j >= i - WINDOW), 0.0, NEG)
    half = np.arange(0, DH, 2, dtype=f32)
    inv = f32(1.0) / f32(10000.0) ** (half / f32(DH))
    t = np.arange(T, dtype=f32)
    ang = np.concatenate([t[:, None] * inv[None, :]] * 2, 1)
    base = (half + f32(0.4 * DH)) / f32(1.4 * DH)
    power = (t - T // 2) / f32(WINDOW // 2)
    scale = np.concatenate([base[None, :] ** power[:, None]] * 2, 1).astype(f32)
    sign = np.where(np.arange(DH) < DH // 2, -1.0, 1.0)[None, :].astype(f32)
    cos, sin = np.cos(ang), np.sin(ang) * sign
    tab = np.stack([[cos * scale, sin * scale], [cos / scale, sin / scale]])
    phase["xpos"] = tab.reshape(2, 2, TPB, P, DH).transpose(3, 0, 1, 2, 4)
    conv = lambda d: {n: np.ascontiguousarray(a, dtype=np.float32) for n, a in d.items()}
    return conv(keep), conv(phase)


def layouts(inputs):
    k = {n: np.ascontiguousarray(a) for n, a in inputs.items()}
    for n in ("L0_attn_qcb", "L0_attn_kcb", "L0_attn_vcb", "L0_attn_ba"):
        k[n] = k[n].reshape(NCT, P).T
    for n in ("L0_attn_qcw", "L0_attn_kcw", "L0_attn_vcw"):
        k[n] = k[n].reshape(NCT, P, TAPS).transpose(1, 0, 2)
    for n in ("L0_attn_ln_w", "L0_attn_ln_b"):
        k[n] = np.concatenate([k[n], k[n]])[:, None]
    k["L0_attn_bb"] = k["L0_attn_bb"][None, :]
    k["L0_ffn_gate_w"] = k["L0_ffn_gate_w"].T
    k["L0_ffn_gate_b"] = k["L0_ffn_gate_b"][None, :]
    k["L0_ffn_b1"] = k["L0_ffn_b1"].reshape(NE, NF, P).transpose(2, 0, 1)
    w = k.pop("L1_attn_w_qkv").reshape(3, H1, 2, HD // 2, D)
    rows = [w[0], w[0][:, ::-1], w[1], w[1][:, ::-1]]
    k["L1_wqk"] = np.stack([r.reshape(P, D).T for r in rows], 1)
    k["L1_wv"] = w[2].reshape(P, D).T
    k["L1_attn_w_out"] = k["L1_attn_w_out"].T
    k["L1_attn_b_out"] = k["L1_attn_b_out"][None, :]
    b1 = k.pop("L1_ffn_b1").reshape(DEPTH, 2, HID)
    full = HID // P * P
    k["L1_b1_full"] = b1[:, :, :full].reshape(DEPTH, 2, HID // P, P).transpose(0, 1, 3, 2)
    k["L1_b1_rest"] = b1[:, :, full:, None]
    for n in ("L1_ffn_ln_g", "L1_ffn_ln_b"):
        k[n] = k[n][:, :, None]
    return {n: np.ascontiguousarray(a) for n, a in k.items()}


def build(nc, shapes, phases="ABCD", nseg=NSEG, x_from="L0_attn_x"):
    keep, phase = constants()
    dram = lambda n, shape, kind: nc.dram_tensor(n, list(shape), F32, kind=kind).ap()
    k = {n: dram("in_" + n, s, "ExternalInput") for n, s in shapes.items()}
    cd = {n: dram("const_" + n, a.shape, "ExternalInput") for n, a in {**keep, **phase}.items()}
    out = dram("out_0", [NB, T, D], "ExternalOutput")
    x1, xn = dram("x1", [NB, T, D], "Internal"), dram("xn", [P, NB, T + PAD], "Internal")
    with ExitStack() as ctx:
        c = Core(nc, ctx)
        cst, l_c = {}, DmaCount(c.sem("s_const"))
        for n, a in keep.items():
            cst[n] = c.sb(ctx, "k_" + n, list(a.shape))
            ready = l_c.start(c.sp, cst[n][:], cd[n])
        for s in (c.pe, c.dve, c.act, c.pool):
            s.wait(ready)
        c.ident, c.eps, c.ones_row = cst["ident"], cst["eps"], cst["ones_row"]
        if "A" in phases:
            delta_rule_attention(c, k, k["L0_attn_x"], x1, xn, cst, nseg)
        rows = lambda a: a.rearrange("b (n p) d -> p (b n) d", p=P)
        X = c.sb(ctx, "x", [P, NTILE, D])
        l_x = DmaCount(c.sem("s_x"))
        for n in ("tri", "ones"):
            cst[n] = c.sb(ctx, "k_" + n, [P, P])
            l_x.start(c.sp, cst[n][:], cd[n])
        x_ready = l_x.start(c.sp, X[:], rows(x1 if "A" in phases else k[x_from]))
        for s in (c.pe, c.dve, c.act, c.pool):
            s.wait(x_ready)
        if "B" in phases:
            expert_ffn(c, k, X, x_ready, cst)
        if "C" in phases:
            banded_attention(c, k, X, cd)
        if "D" in phases:
            Y = c.sb(ctx, "y", [P, NTILE, D])
            with ExitStack() as nctx:
                norm = Norm(c, nctx, "y")
                t = norm.of(c, X, lambda g: ())
                for g in range(NTILE):
                    c.dve.do(lambda e, g=g: e.tensor_scalar(Y[:, g, :], X[:, g, :], norm.mv[:, g, 0:1], norm.rstd[:, g:g + 1],
                             ALU.subtract, ALU.mult), t)
                c.barrier()
            for l in range(DEPTH):
                local_layer(c, k, Y, l, cd)
            c.dve.do(lambda e: e.tensor_tensor(X[:], X[:], Y[:], ALU.add))
        c.sp.wait(c.stores.start(c.sp, rows(out), X[:], c.dve.last()))
        block = ctx.enter_context(nc.Block())
        for on, s in ((block.tensor, c.pe), (block.vector, c.dve), (block.scalar, c.act), (block.gpsimd, c.pool),
                      (block.sync, c.sp)):
            queue = lambda e, s=s: s.emit(e)
            on(queue)
    return {"const_" + n: a for n, a in {**keep, **phase}.items()}


_IN = "in_"


def kernel(**inputs):
    import concourse.bacc as bacc
    from concourse.bass_utils import run_bass_kernel_spmd

    nc = bacc.Bacc("TRN2", target_bir_lowering=False, num_devices=1)
    laid_out = layouts({n: np.asarray(a) for n, a in inputs.items()})
    tables = build(nc, {n: a.shape for n, a in laid_out.items()})
    arrays = {**{_IN + n: a for n, a in laid_out.items()}, **tables}
    return run_bass_kernel_spmd(nc, [arrays], core_ids=[0]).results[0]["out_0"]
```

```python
from contextlib import ExitStack

import numpy as np
import concourse.bass as bass
from concourse import mybir

F32 = mybir.dt.float32
ALU = mybir.AluOpType
ACT = mybir.ActivationFunctionType
AX = mybir.AxisListType

P = 128
NB, T, D = 4, 1024, 128
NT = NB * T
TPB = T // P
NTILE = NT // P
BANK = 512
EPS = 1e-5


class Token:

    def __init__(self, sem, value):
        self.sem, self.value = sem, value


class Stream:

    def __init__(self, sem, in_line=False):
        self.sem, self.count, self.queue, self.seen, self.in_line = sem, 0, [], {}, in_line

    def wait(self, *tokens):
        for t in tokens:
            if t is None:
                continue
            if self.seen.get(t.sem, 0) >= t.value:
                continue
            self.seen[t.sem] = t.value
            self.queue.append((t, None))

    def do(self, fn, *after):
        self.wait(*after)
        if self.in_line:
            self.wait(self.last())
        self.count += 1
        self.queue.append((self.sem, fn))
        return Token(self.sem, self.count)

    def go(self, fn, *after):
        self.wait(*after)
        self.count += 1
        self.queue.append((self.sem, fn))
        return Token(self.sem, self.count)

    def run(self, fn, *after):
        self.wait(*after)
        self.queue.append((None, fn))

    def last(self):
        return Token(self.sem, self.count) if self.count else None

    def emit(self, engine):
        for what, fn in self.queue:
            if fn is None:
                engine.wait_ge(what.sem, what.value)
            elif what is None:
                fn(engine)
            else:
                fn(engine).then_inc(what, 1)


class DmaCount:

    def __init__(self, sem):
        self.sem, self.count = sem, 0

    def start(self, stream, out, in_, *after):
        stream.wait(*after)
        self.count += 16
        sem = self.sem
        stream.queue.append((None, lambda e: e.dma_start(out, in_).then_inc(sem, 16)))
        return Token(self.sem, self.count)


class Slot:

    def __init__(self, ap):
        self.ap, self.free = ap, []


class Ring:
    def __init__(self, slots):
        self.slots, self.at = slots, 0

    def next(self):
        s = self.slots[self.at % len(self.slots)]
        self.at += 1
        return s


class Core:

    def __init__(self, nc, ctx):
        self.nc, self.ctx = nc, ctx
        self.names = 0
        self.pe, self.dve, self.act, self.pool, self.sp = (
            Stream(ctx.enter_context(nc.semaphore(n)), in_line=n in ("s_dve", "s_act", "s_pool")) for n in ("s_pe", "s_dve", "s_act", "s_pool", "s_sp"))
        self.banks = ctx.enter_context(nc.psum_tensor("banks", [P, 8 * BANK], F32))
        self.stores = DmaCount(ctx.enter_context(nc.semaphore("s_stores")))
        self.dram_writes = []

    def sem(self, name):
        return self.ctx.enter_context(self.nc.semaphore(name))

    def bank(self, n, k=1):
        return self.banks[:, n * BANK:(n + k) * BANK]

    def sb(self, ctx, name, shape):
        return ctx.enter_context(self.nc.sbuf_tensor(name, shape, F32))

    def barrier(self, *more):
        streams = (self.pe, self.dve, self.act, self.pool)
        tokens = [s.last() for s in streams]
        for s in streams + (self.sp,):
            s.wait(*[t for t in tokens], *more)


def layer_norm_rows(c, src, stats, mv, rstd, eps, ready):
    for g in range(NTILE):
        t = c.dve.do(lambda e, g=g: e.bn_stats(stats[:, g, :], src[:, g, :]), *ready(g))
    for g in range(NTILE):
        t = c.dve.do(lambda e, g=g: e.bn_aggr(mv[:, g, :], stats[:, g, :]), t)
    t = c.act.do(lambda e: e.activation(rstd[:, :], mv[:, :, 1], ACT.Sqrt, bias=eps[:, 0:1]), t)
    return c.dve.do(lambda e: e.reciprocal(rstd[:, :], rstd[:, :]), t)
H0, DK = 16, 64
CH = H0 * DK
NCT = CH // P
R = NCT * NB
SEG, CK = 32, 16
NSEG, NCK = T // SEG, SEG // CK
TAPS = 4
PAD = TAPS - 1
SW = NB * SEG
assert R == 32 and SEG == 32


def delta_rule_attention(c, k, x_in, x1, xn_dram, cst, nseg=NSEG):
    pe, dve, act, pool, sp = c.pe, c.dve, c.act, c.pool, c.sp
    ident, ones_row, eps = cst["ident"], cst["ones_row"], cst["eps"]
    w_pads = DmaCount(c.sem("s_xn_pads"))
    w_xn = [DmaCount(c.sem(f"s_xn_store{i}")) for i in range(2)]

    with ExitStack() as ctx:
        X = c.sb(ctx, "a_x", [P, NTILE, D])
        stats = c.sb(ctx, "a_stats", [P, NTILE, 6])
        mv = c.sb(ctx, "a_mv", [P, NTILE, 2])
        rstd = c.sb(ctx, "a_rstd", [P, NTILE])
        xn = Ring([Slot(c.sb(ctx, f"a_xn{i}", [P, 4, D])) for i in range(2)])
        xnT = Ring([Slot(c.sb(ctx, f"a_xnT{i}", [P, BANK])) for i in range(2)])
        zero = c.sb(ctx, "a_zero", [P, NB, PAD])
        l_x = DmaCount(c.sem("s_a_x"))
        loaded = l_x.start(sp, X[:], x_in.rearrange("b (n p) d -> p (b n) d", p=P))
        t_z = dve.do(lambda e: e.memset(zero[:], 0.0))
        w_pads.start(sp, xn_dram[:, :, 0:PAD], zero[:], t_z)
        t_n = layer_norm_rows(c, X, stats, mv, rstd, eps, lambda g: (loaded,))
        bank = Ring([Slot(c.bank(i)) for i in range(2)])
        for n in range(NTILE // 4):
            s, o, b = xn.next(), xnT.next(), bank.next()
            for j in range(4):
                g = 4 * n + j
                t = dve.do(lambda e, g=g, j=j, s=s: e.tensor_scalar(s.ap[:, j, :], X[:, g, :], mv[:, g, 0:1],
                           rstd[:, g:g + 1], ALU.subtract, ALU.mult), t_n, *s.free)
            for j in range(4):
                tp = pe.do(lambda e, j=j, s=s, b=b: e.transpose(b.ap[:, j * P:(j + 1) * P], s.ap[:, j, :],
                           ident[:]), t, *b.free)
            s.free = [tp]
            ta = act.do(lambda e, o=o, b=b: e.activation(o.ap[:], b.ap, ACT.Copy), tp, *o.free)
            b.free = [ta]
            bi, t0 = divmod(n * BANK, T)
            o.free = [w_xn[n % 2].start(sp, xn_dram[:, bi, PAD + t0:PAD + t0 + BANK], o.ap[:], ta)]
        c.barrier(*[Token(w.sem, w.count) for w in w_xn + [w_pads]])

    with ExitStack() as ctx:
        sb = lambda name, shape: c.sb(ctx, "a_" + name, shape)
        wT = {n: sb("w_" + n, [P, TAPS if n in "qkv" else 1, CH]) for n in "qkvag"}
        woT = sb("w_o", [P, NCT, D])
        bias = {n: sb("bias_" + n, [P, NCT]) for n in "qkva"}
        wbT = sb("w_b", [P, H0])
        bb = sb("bb", [1, H0])
        lnw, lnb = sb("lnw", [P, 1]), sb("lnb", [P, 1])
        beta = sb("beta", [P, T])
        l_w = DmaCount(c.sem("s_a_w"))
        wtok = None
        with ExitStack() as wctx:
            raw = {n: c.sb(wctx, "a_raw_" + n, [P, NCT, D]) for n in "qkvag"}
            tap = {n: c.sb(wctx, "a_tap_" + n, [P, NCT, TAPS]) for n in "qkv"}
            raw_o = c.sb(wctx, "a_raw_o", [P, CH])
            raw_b = c.sb(wctx, "a_raw_b", [H0, D])
            scaled = Ring([Slot(c.sb(wctx, f"a_scaled{i}", [P, 4, D])) for i in range(2)])
            for n in "qkvag":
                wtok = l_w.start(sp, raw[n][:], k["L0_attn_W" + n].rearrange("(t p) d -> p t d", p=P))
            for n in "qkv":
                wtok = l_w.start(sp, tap[n][:], k[f"L0_attn_{n}cw"])
                wtok = l_w.start(sp, bias[n][:], k[f"L0_attn_{n}cb"])
            wtok = l_w.start(sp, bias["a"][:], k["L0_attn_ba"])
            wtok = l_w.start(sp, raw_o[:], k["L0_attn_Wo"])
            wtok = l_w.start(sp, raw_b[:], k["L0_attn_Wb"])
            wtok = l_w.start(sp, bb[:], k["L0_attn_bb"])
            wtok = l_w.start(sp, lnw[:], k["L0_attn_ln_w"])
            wtok = l_w.start(sp, lnb[:], k["L0_attn_ln_b"])
            bank = Ring([Slot(c.bank(i)) for i in range(4)])
            for n in "qkvag":
                for half in range(2):
                    for j in range(TAPS if n in "qkv" else 1):
                        b = bank.next()
                        src = raw[n][:, 4 * half:4 * half + 4, :]
                        ready, s = [wtok], None
                        if n in "qkv":
                            s = scaled.next()
                            tj = tap[n][:, 4 * half:4 * half + 4, j:j + 1].broadcast_to([P, 4, D])
                            ready = [dve.do(lambda e, s=s, src=src, tj=tj: e.tensor_tensor(s.ap[:], src, tj, ALU.mult),
                                            wtok, *s.free)]
                            src = s.ap[:]
                        for m in range(4):
                            tp = pe.do(lambda e, b=b, m=m, src=src: e.transpose(b.ap[:, m * P:(m + 1) * P],
                                       src[:, m, :], ident[:]), *ready, *b.free)
                        if s is not None:
                            s.free = [tp]
                        b.free = [act.do(lambda e, n=n, j=j, half=half, b=b: e.activation(
                            wT[n][:, j, half * BANK:(half + 1) * BANK], b.ap, ACT.Copy), tp)]
            for half in range(2):
                b = bank.next()
                for m in range(4):
                    ct = 4 * half + m
                    tp = pe.do(lambda e, b=b, m=m, ct=ct: e.transpose(b.ap[:, m * P:(m + 1) * P],
                               raw_o[:, ct * P:(ct + 1) * P], ident[:]), wtok, *b.free)
                b.free = [act.do(lambda e, b=b, half=half: e.activation(
                    woT[:, 4 * half:4 * half + 4, :], b.ap.rearrange("p (m d) -> p m d", m=4), ACT.Copy), tp)]
            b = bank.next()
            tp = pe.do(lambda e, b=b: e.transpose(b.ap[:, 0:H0], raw_b[:], ident[0:H0, 0:H0]), wtok, *b.free)
            b.free = [act.do(lambda e, b=b: e.activation(wbT[:], b.ap[:, 0:H0], ACT.Copy), tp)]
            w_ready = act.last()
            c.barrier()

        with ExitStack() as bctx:
            xb = c.sb(bctx, "a_xb", [P, NB, T])
            bt = c.sb(bctx, "a_bt", [P, NTILE, H0])
            btx = c.sb(bctx, "a_btx", [P, TPB, 2, 2, NCT, NB])
            t = l_w.start(sp, xb[:], xn_dram[:, :, PAD:])
            logits = c.bank(0)
            for g in range(NTILE):
                bi, tt = divmod(g, TPB)
                pe.run(lambda e, g=g, bi=bi, tt=tt: e.matmul(logits[:, g * H0:(g + 1) * H0],
                       xb[:, bi, tt * P:(tt + 1) * P], wbT[:], start=(g == 0), stop=False, skip_group_check=True),
                       t, w_ready)
                tp = pe.do(lambda e, g=g: e.matmul(logits[:, g * H0:(g + 1) * H0], ones_row[0:1, 0:P], bb[:],
                           start=False, stop=True, skip_group_check=True))
            t = act.do(lambda e: e.activation(bt[:].rearrange("p g h -> p (g h)"), logits, ACT.Sigmoid), tp)
            for tt in range(TPB):
                for ih in range(2):
                    for par in range(2):
                        src = bt[:, tt::TPB, par::2].rearrange("p b c -> p c b")
                        td = dve.do(lambda e, tt=tt, ih=ih, par=par, src=src: e.tensor_copy(btx[:, tt, par, ih, :, :], src), t)
            for tt in range(TPB):
                b = c.bank(1 + tt // 4)[:, (tt % 4) * P:(tt % 4 + 1) * P]
                tp = pe.do(lambda e, tt=tt, b=b: e.transpose(b, btx[:, tt].rearrange("p a i c b -> p (a i c b)"),
                           ident[:]), td)
            for half in range(2):
                act.do(lambda e, half=half: e.activation(beta[:, half * BANK:(half + 1) * BANK], c.bank(1 + half),
                       ACT.Copy), tp)
            c.barrier()

        xseg = Ring([Slot(sb(f"xseg{i}", [P, NB, PAD + SEG])) for i in range(3)])
        KQ = Ring([Slot(sb(f"kq{i}", [P, R, 3, SEG])) for i in range(2)])
        kraw = Slot(sb("kraw", [P, R, SEG]))
        v1, a1 = Slot(sb("v1", [P, SEG, R])), Slot(sb("a1", [P, SEG, R]))
        a2 = Ring([Slot(sb(f"a2_{i}", [P, SEG, 32])) for i in range(2)])
        bv = Ring([Slot(sb(f"bv{i}", [P, SEG, 32])) for i in range(2)])
        Dc = Ring([Slot(sb(f"dc{i}", [P, SEG, 32])) for i in range(2)])
        Dk = Slot(sb("dk", [P, CK, 32]))
        G1, G1b = Slot(sb("g1", [P, R, 2, CK])), Slot(sb("g1b", [P, 8, 2, CK]))
        G2 = Ring([Slot(sb(f"g2_{i}", [P, 2, CK, SEG])) for i in range(2)])
        Kt = Slot(sb("kt", [P, R, DK]))
        W = [sb(f"w{i}", [P, SEG, 32]) for i in range(NCK)]
        Wm = sb("wm", [P, 2, 32, R])
        ST = sb("st", [P, R, DK])
        AB = sb("ab", [P, R, DK])
        Dx = Ring([Slot(sb(f"dx{i}", [P, 8, 2, 32])) for i in range(2)])
        P2 = sb("p2", [P, 2, CK, 32])
        tmp_e, tmp_o = sb("tmp_e", [P, CK, 32]), sb("tmp_o", [P, CK, 32])
        red = sb("red", [P, 2, 32])
        O2 = sb("o2", [P, SEG, 32])
        o1, sq = sb("o1", [P, R, SEG]), sb("sq", [P, R, SEG])
        xrow = Slot(sb("xrow", [P, D]))
        back = Ring([Slot(c.bank(i)) for i in range(4)])
        Pb = Slot(c.bank(4, 2))
        Ub = Ring([Slot(c.bank(6 + i)) for i in range(2)])
        l_seg = [DmaCount(c.sem(f"s_a_seg{i}")) for i in range(3)]
        l_row, w_row = (DmaCount(c.sem(n)) for n in ("s_a_row", "s_a_out"))
        half_of, pair_ones, ih_mask, own = (cst[n] for n in ("half_of", "pair_ones", "ih_mask", "own"))

        for w in W + [ST]:
            zeroed = dve.do(lambda e, w=w: e.memset(w[:], 0.0))

        def project(n, b, xs, ct, m):
            taps = TAPS if n in "qkv" else 1
            for j in range(taps):
                off = j if taps > 1 else PAD
                fn = lambda e, j=j, off=off: e.matmul(
                    b.ap[:, m * SW:(m + 1) * SW].rearrange("p (b t) -> p b t", b=NB), wT[n][:, j, ct * P:(ct + 1) * P],
                    xs.ap[:, :, off:off + SEG], start=(j == 0), stop=(j == taps - 1))
                if j < taps - 1:
                    pe.run(fn, *b.free, *xs.ready)
                else:
                    return pe.do(fn, *b.free, *xs.ready)

        def segment_inputs(s):
            seg = dict(xs=xseg.next(), kq=KQ.next(), a2=a2.next(), bv=bv.next(), dc=Dc.next(), g2=G2.next())
            xs, kq = seg["xs"], seg["kq"]
            t0 = s * SEG
            xs.ready = [l_seg[s % 3].start(sp, xs.ap[:], xn_dram[:, :, t0:t0 + SEG + PAD], *xs.free)]
            done = {}

            def proj(n, half):
                b = back.next()
                for m in range(4):
                    tp = project(n, b, xs, 4 * half + m, m)
                for m in range(4):
                    ct = 4 * half + m
                    src = b.ap[:, m * SW:(m + 1) * SW].rearrange("p (b t) -> p b t", b=NB)
                    rr = slice(ct * NB, (ct + 1) * NB)
                    if n == "k":
                        dst, fn, free = kraw.ap[:, rr, :], ACT.Silu, kraw.free
                    elif n == "q":
                        dst, fn, free = kq.ap[:, rr, 2, :], ACT.Silu, kq.free
                    elif n == "v":
                        dst, fn, free = v1.ap[:, :, rr].rearrange("p t b -> p b t"), ACT.Silu, v1.free
                    else:
                        dst, fn, free = a1.ap[:, :, rr].rearrange("p t b -> p b t"), ACT.Sigmoid, a1.free
                    t = act.go(lambda e, dst=dst, src=src, fn=fn, ct=ct, n=n: e.activation(
                        dst, src, fn, bias=bias[n][:, ct:ct + 1]), tp, *free)
                b.free = [t]
                done[n] = t
                if n == "k" and half == 1:
                    src = kraw.ap[:].rearrange("p r (o t) -> p r o t", o=1).broadcast_to([P, R, 2, SEG])
                    done["kk"] = pool.go(lambda e, src=src: e.tensor_scalar(kq.ap[:, :, 0:2, :], src, DK ** -0.5, None,
                                         ALU.mult), t, *kq.free)
                    kraw.free = [done["kk"]]

            def gates():
                t = dve.go(lambda e: e.transpose(seg["a2"].ap[:].rearrange("p t i -> p (t i)"),
                                                 a1.ap[:].rearrange("p t r -> p (t r)")), done["a"], *seg["a2"].free)
                a1.free = [t]
                A, Dd = seg["a2"].ap, seg["dc"].ap
                view = lambda x, j: x[:].rearrange("p (c t) i -> p c t i", t=CK)[:, :, j, :]
                tt = pool.do(lambda e: e.tensor_copy(view(Dd, 0), view(A, 0)), t, *seg["dc"].free)
                for j in range(1, CK):
                    tt = pool.do(lambda e, j=j: e.tensor_tensor(view(Dd, j), view(Dd, j - 1), view(A, j), ALU.mult), tt)
                seg["a_ready"], seg["d_ready"] = t, tt

            def values():
                t = dve.go(lambda e: e.transpose(seg["bv"].ap[:].rearrange("p t i -> p (t i)"),
                                                 v1.ap[:].rearrange("p t r -> p (t r)")), done["v"], *seg["bv"].free)
                v1.free = [t]
                bcol = beta[:, t0:t0 + SEG].rearrange("p (t o) -> p t o", o=1).broadcast_to([P, SEG, 32])
                seg["v_ready"] = pool.go(lambda e: e.tensor_tensor(seg["bv"].ap[:], seg["bv"].ap[:], bcol, ALU.mult), t)

            def gram(n):
                b = back.next()
                for m in range(8):
                    r = 8 * n + m
                    for par in range(2):
                        ps = slice(par * DK, (par + 1) * DK)
                        fn = lambda e, r=r, m=m, ps=ps: e.matmul(
                            b.ap[ps, m * 2 * SEG:(m + 1) * 2 * SEG].rearrange("p (z t) -> p z t", z=2),
                            kq.ap[ps, r, 0:2, :].rearrange("p z t -> p (z t)"), kq.ap[ps, r, 0:3:2, :],
                            start=True, stop=True)
                        if m < 7 or par < 1:
                            pe.run(fn, done["kk"], done["q"], *b.free)
                tp = pe.do(fn)
                v = b.ap.rearrange("p (rz c t) -> p rz c t", c=NCK, t=CK)
                dst = G1.ap[:, 8 * n:8 * n + 8, :, :].rearrange("p r z t -> p (r z) t")
                oth = G1b.ap[:, :, :, :].rearrange("p r z t -> p (r z) t")
                act.go(lambda e: e.activation(oth, v[:, :, 0, :], ACT.Copy, scale=half_of[:, 0:1]), tp, *G1b.free)
                t = act.go(lambda e: e.activation(dst, v[:, :, 1, :], ACT.Copy, scale=half_of[:, 1:2]), *G1.free)
                b.free = [t]
                seg["g1"] = pool.go(lambda e: e.tensor_tensor(dst, dst, oth, ALU.add), t)
                G1b.free = [seg["g1"]]

            def gram_rows():
                g2 = seg["g2"]
                tr = dve.go(lambda e: e.transpose(g2.ap[:].rearrange("p z t j -> p (z t) j"),
                                                  G1.ap[:].rearrange("p r z t -> p (z t) r")), seg["g1"], *g2.free)
                G1.free = [tr]
                for ch in range(NCK):
                    v = g2.ap[:, 0, :, ch * CK:(ch + 1) * CK]
                    bc = beta[:, t0 + ch * CK:t0 + (ch + 1) * CK].rearrange("p (t o) -> p t o", o=1).broadcast_to([P, CK, CK])
                    seg["g_ready"] = pool.go(lambda e, v=v, bc=bc: e.tensor_tensor(v, v, bc, ALU.mult), tr)

            def time_rows(n):
                b = back.next()
                for m in range(8):
                    r = 8 * n + m
                    for par in range(2):
                        ps = slice(par * DK, (par + 1) * DK)
                        fn = lambda e, r=r, m=m, ps=ps: e.matmul(
                            b.ap[ps, m * DK:(m + 1) * DK], kq.ap[ps, r, 0:2, :].rearrange("p z t -> p (z t)"),
                            ident[ps, ps], start=True, stop=True)
                        if m < 7 or par < 1:
                            pe.run(fn, done["kk"], *b.free)
                tp = pe.do(fn)
                t = act.go(lambda e: e.activation(Kt.ap[:, 8 * n:8 * n + 8, :].rearrange("p r d -> p (r d)"), b.ap, ACT.Copy),
                           tp, *Kt.free)
                b.free = [t]
                seg["kt_ready"] = t

            each = lambda fn, args: [lambda a=a: fn(*a) for a in args]
            halves = lambda n: each(proj, [(n, 0), (n, 1)])
            seg["early"] = halves("k") + halves("q")
            seg["mid"] = halves("a") + halves("v")
            seg["gates"], seg["values"], seg["gram_rows"] = gates, values, gram_rows
            seg["gram"] = each(gram, [(n,) for n in range(4)])
            seg["time_rows"] = each(time_rows, [(n,) for n in range(4)])
            return seg

        def chunk(s, ch, seg, jobs, in_p, in_u):
            t0 = s * SEG + ch * CK
            kq, a2_, bv_, dc, g2 = (seg[n] for n in ("kq", "a2", "bv", "dc", "g2"))
            js = slice(ch * CK, (ch + 1) * CK)
            Wc = W[ch]

            for r in range(R):
                for par in range(2):
                    ps = slice(par * DK, (par + 1) * DK)
                    fn = lambda e, r=r, ps=ps: e.matmul(
                        Pb.ap[ps, r * 2 * CK:(r + 1) * 2 * CK].rearrange("p (z t) -> p z t", z=2), ST[ps, r, :],
                        kq.ap[ps, r, 0:3:2, js], start=True, stop=True)
                    if r < R - 1 or par < 1:
                        pe.run(fn, chain["state"][r // 8], *Pb.free)
            tp = pe.do(fn)
            t = pool.go(lambda e: e.tensor_copy(Dk.ap[:, 1:, :], dc.ap[:, ch * CK:(ch + 1) * CK - 1, :]), seg["d_ready"], *Dk.free)
            t1 = pool.go(lambda e: e.memset(Dk.ap[:, 0, :], 1.0), *Dk.free)
            bc = beta[:, t0:t0 + CK].rearrange("p (t o) -> p t o", o=1).broadcast_to([P, CK, 32])
            t_dk = pool.go(lambda e: e.tensor_tensor(Dk.ap[:], Dk.ap[:], bc, ALU.mult), t, t1)
            for job in in_p:
                job()
            tt = dve.go(lambda e: e.transpose(P2[:].rearrange("p z t i -> p (z t) i"),
                        Pb.ap.rearrange("p (r n) -> p n r", r=R)), tp, chain["p2_free"])
            Pb.free = [tt]
            tk = dve.go(lambda e: e.tensor_tensor(P2[:, 0], P2[:, 0], Dk.ap[:], ALU.mult), tt, t_dk)
            Dk.free = [tk]
            tq = dve.go(lambda e: e.tensor_tensor(P2[:, 1], P2[:, 1], dc.ap[:, js, :], ALU.mult), tt, seg["d_ready"])
            te = dve.go(lambda e: e.tensor_tensor(P2[:, 0], bv_.ap[:, js, :], P2[:, 0], ALU.subtract), tk, seg["v_ready"])
            st = {}

            def decay(n):
                b, dx = back.next(), Dx.next()
                d15 = dc.ap[:, (ch + 1) * CK - 1:(ch + 1) * CK, :].rearrange("p (o q) i -> p o q i", o=1).broadcast_to([P, 8, 2, 32])
                ow = own[:, 16 * n:16 * n + 16].rearrange("p (r h o) -> p r h o", h=2, o=1).broadcast_to([P, 8, 2, 32])
                t = pool.go(lambda e: e.tensor_tensor(dx.ap[:], d15, ow, ALU.mult), seg["d_ready"], *dx.free)
                tb = pe.do(lambda e: e.matmul(b.ap, pair_ones[:], dx.ap[:].rearrange("p r h i -> p (r h i)"),
                           start=True, stop=True), t, *b.free)
                dx.free = [tb]
                ab = act.go(lambda e: e.activation(AB[:, 8 * n:8 * n + 8, :].rearrange("p r i -> p (r i)"), b.ap,
                            ACT.Copy), tb, chain["ab_free"])
                b.free = [ab]
                if n == 3:
                    st["sd"] = pool.go(lambda e: e.tensor_tensor(ST[:], ST[:], AB[:], ALU.mult), ab, tp, chain["state"][3])
                    chain["ab_free"] = st["sd"]

            jobs = [lambda n=n: decay(n) for n in range(4)] + jobs
            per = -(-len(jobs) // (CK - 1))

            products = None
            tr = to = None
            tw = dve.go(lambda e: e.tensor_scalar(Wc[:, ch * CK, :], P2[:, 0, 0, :], -1.0, None, ALU.mult), te, chain["w_free"][ch])
            td = None
            for t in range(1, CK + 1):
                row = ch * CK + t
                wj = Wc[:, ch * CK:row, :]
                if t < CK:
                    gk = g2.ap[:, 0, t, ch * CK:row].rearrange("p (j o) -> p j o", o=1).broadcast_to([P, t, 32])
                    tm = dve.go(lambda e, t=t, wj=wj, gk=gk: e.tensor_tensor(tmp_e[:, 0:t, :], wj, gk, ALU.mult), tw, td, tr,
                                seg["g_ready"])
                gq = g2.ap[:, 1, t - 1, ch * CK:row].rearrange("p (j o) -> p j o", o=1).broadcast_to([P, t, 32])
                tm_o = dve.go(lambda e, t=t, wj=wj, gq=gq: e.tensor_tensor(tmp_o[:, 0:t, :], wj, gq, ALU.mult), tw, td, to,
                              seg["g_ready"])
                if t < CK:
                    tr = dve.go(lambda e, t=t: e.tensor_reduce(red[:, t % 2, :], tmp_e[:, 0:t, :].rearrange("p j i -> p i j"),
                                AX.X, ALU.add), tm)
                    at = a2_.ap[:, row:row + 1, :].broadcast_to([P, t, 32])
                    td = dve.go(lambda e, wj=wj, at=at: e.tensor_tensor(wj, wj, at, ALU.mult), tm_o, seg["a_ready"])
                    tw = dve.go(lambda e, t=t, row=row: e.scalar_tensor_tensor(Wc[:, row, :], red[:, t % 2, :], -1.0,
                                P2[:, 0, t, :], ALU.mult, ALU.subtract), tr)
                    to = dve.go(lambda e, t=t, row=row: e.tensor_reduce(O2[:, row - 1, :], tmp_o[:, 0:t, :].rearrange(
                                "p j i -> p i j"), AX.X, ALU.add), tm_o, chain["o2_free"])
                    for _ in range(per):
                        if jobs:
                            jobs.pop(0)()
            tt = dve.go(lambda e: e.transpose(Wm[:, 1].rearrange("p i r -> p i r"), Wc[:].rearrange("p j i -> p i j")),
                        tw, td, chain["wm_free"])
            chain["w_free"][ch] = tt
            t_o = dve.go(lambda e, row=row: e.tensor_reduce(O2[:, row - 1, :], tmp_o[:, 0:CK, :].rearrange("p j i -> p i j"),
                         AX.X, ALU.add), tm_o, to)
            tm0 = dve.go(lambda e: e.tensor_scalar(Wm[:, 0], Wm[:, 1], ih_mask[:, 0:1], None, ALU.mult), tt)
            seg["o"] = dve.go(lambda e: e.tensor_tensor(O2[:, js, :], P2[:, 1], O2[:, js, :], ALU.subtract), t_o, tq)
            chain["p2_free"] = seg["o"]
            tm1 = dve.go(lambda e: e.tensor_scalar(Wm[:, 1], Wm[:, 1], ih_mask[:, 1:2], None, ALU.mult), tm0)
            for job in in_u:
                job()
            tus = []
            for n in range(4):
                b = Ub.next()
                for m in range(8):
                    r = 8 * n + m
                    for par in range(2):
                        ps = slice(par * DK, (par + 1) * DK)
                        fn = lambda e, r=r, m=m, ps=ps, b=b: e.matmul(
                            b.ap[ps, m * DK:(m + 1) * DK], Kt.ap[ps, r, :], Wm[ps, :, :, r].rearrange("p h i -> p (h i)"),
                            start=True, stop=True)
                        if m < 7 or par < 1:
                            pe.run(fn, tm1, seg["kt_ready"], *b.free)
                tu = pe.do(fn)
                sv = ST[:, 8 * n:8 * n + 8, :].rearrange("p r i -> p (r i)")
                ts = dve.go(lambda e, b=b, sv=sv: e.tensor_tensor(sv, sv, b.ap, ALU.subtract), tu, st["sd"])
                b.free = [ts]
                tus.append(ts)
            chain["state"], chain["wm_free"] = tus, tu
            Kt.free = [tu]
            for n in ("kq", "a2", "bv", "dc", "g2"):
                seg[n].free = [seg["o"], tu, tw, st["sd"], t_dk]

        def finish(s, seg):
            xs = seg["xs"]
            t0 = s * SEG
            st = {"d": {}, "sq": {}, "sd": {}, "scaled": {}, "affine": {}, "g": {}, "b": {}}
            cols = lambda a, half: a[:, 16 * half:16 * half + 16, :].rearrange("p r t -> p (r t)")

            def turn():
                st["o"] = dve.go(lambda e: e.transpose(o1[:].rearrange("p r t -> p t r"), O2[:]), seg["o"],
                                 chain["o1_free"])
                chain["o2_free"] = st["o"]

            def mean(half):
                b = back.next()
                st["b"][half] = b
                st["m"] = pe.do(lambda e: e.matmul(b.ap, pair_ones[:], cols(o1, half), start=True, stop=True), st["o"], *b.free)

            def centre(half):
                b, v = st["b"][half], cols(o1, half)
                t = dve.go(lambda e: e.scalar_tensor_tensor(v, b.ap, -1.0 / DK, v, ALU.mult, ALU.add), st["m"])
                b.free, st["d"][half] = [t], t

            def deviation(half):
                b, v, w = back.next(), cols(o1, half), cols(sq, half)
                t = act.go(lambda e: e.activation(w, v, ACT.Square), st["d"][half], chain["y"])
                tp = pe.do(lambda e: e.matmul(b.ap, pair_ones[:], w, start=True, stop=True), t, *b.free)
                t = act.go(lambda e: e.activation(w, b.ap, ACT.Sqrt, scale=1.0 / DK, bias=eps[:, 0:1]), tp)
                b.free, st["sd"][half] = [t], t

            def scale(half):
                v, w = cols(o1, half), cols(sq, half)
                t = dve.go(lambda e: e.reciprocal(w, w), st["sd"][half])
                t = dve.do(lambda e: e.tensor_tensor(v, v, w, ALU.mult), t)
                st["scaled"][half] = t

            def gate(half):
                b, v, w = back.next(), cols(o1, half), cols(sq, half)
                for m in range(4):
                    tp = project("g", b, xs, 4 * half + m, m)
                xs.free = [tp]
                st["affine"][half] = act.go(lambda e: e.activation(v, v, ACT.Identity, scale=lnw[:, 0:1],
                                            bias=lnb[:, 0:1]), st["scaled"][half])
                t = act.go(lambda e: e.activation(w, b.ap, ACT.Sigmoid), tp, st["scaled"][half])
                b.free = [t]
                st["y"] = pool.go(lambda e: e.tensor_tensor(v, v, w, ALU.mult), t, st["affine"][half])

            def rows():
                for b_ in range(NB):
                    st["x"] = l_row.start(sp, xrow.ap[b_ * SEG:(b_ + 1) * SEG, :], x_in[b_, t0:t0 + SEG, :], *xrow.free)

            def out():
                b = back.next()
                for ct in range(NCT):
                    fn = lambda e, ct=ct: e.matmul(b.ap[:, 0:D], o1[:, ct * NB:(ct + 1) * NB, :].rearrange("p b t -> p (b t)"),
                                                   woT[:, ct, :], start=(ct == 0), stop=(ct == NCT - 1))
                    if ct < NCT - 1:
                        pe.run(fn, st["y"], *b.free)
                st["out"], st["ob"] = pe.do(fn), b
                chain["o1_free"], chain["y"] = st["out"], st["y"]

            def add():
                b = st["ob"]
                t = dve.go(lambda e: e.tensor_tensor(xrow.ap[:], xrow.ap[:], b.ap[:, 0:D], ALU.add), st["out"], st["x"])
                b.free = [t]
                for b_ in range(NB):
                    xrow.free = [w_row.start(sp, x1[b_, t0:t0 + SEG, :], xrow.ap[b_ * SEG:(b_ + 1) * SEG, :], t)]
            two = lambda fn: [lambda: fn(0), lambda: fn(1)]
            return dict(turn=[turn], mean=two(mean), centre=two(centre), deviation=two(deviation), scale=two(scale),
                        gate=two(gate), rows=[rows], out=[out], add=[add])

        chain = dict(state=[zeroed] * 4, ab_free=None, w_free=[zeroed] * NCK, wm_free=None, y=None, o1_free=None,
                     p2_free=None, o2_free=None)
        seg = segment_inputs(0)
        for job in seg["early"] + seg["mid"] + seg["gram"] + [seg["gates"], seg["values"], seg["gram_rows"]]:
            job()
        none = dict.fromkeys(("turn", "mean", "centre", "deviation", "scale", "gate", "rows", "out", "add"), [])
        old = none
        for s in range(nseg):
            nxt = segment_inputs(s + 1) if s + 1 < nseg else None
            get = lambda n: nxt[n] if nxt else []
            one = lambda n: [nxt[n]] if nxt else []
            chunk(s, 0, seg, seg["time_rows"] + get("early") + old["rows"] + old["mean"], old["turn"], old["centre"])
            chunk(s, 1, seg, get("mid") + old["deviation"] + get("gram") + old["scale"] + old["gate"] + old["out"],
                  [], one("gates") + one("values") + one("gram_rows") + old["add"])
            old = finish(s, seg)
            seg = nxt
        for n in ("turn", "mean", "centre", "deviation", "scale", "gate", "rows", "out", "add"):
            for job in old[n]:
                job()
        c.barrier(xrow.free[0])
def transposed(c, ctx, name, src, dst, scale_of=None, rows=None, affine=None):
    pe, dve, act = c.pe, c.dve, c.act
    bank = Ring([Slot(c.bank(i)) for i in range(2)])
    if scale_of:
        mv, rstd = scale_of
        xn = Ring([Slot(c.sb(ctx, f"{name}_xn{i}", [P, 4, D])) for i in range(2)])
    done = []
    for n in range(NTILE // 4):
        b, t = bank.next(), None
        s = xn.next() if scale_of else None
        for j in range(4):
            g = 4 * n + j
            if scale_of:
                t = dve.do(lambda e, g=g, j=j, s=s: e.tensor_scalar(s.ap[:, j, :], src[:, g, :], mv[:, g, 0:1],
                           rstd[:, g:g + 1], ALU.subtract, ALU.mult), *rows(g), *s.free)
        for j in range(4):
            g = 4 * n + j
            row = s.ap[:, j, :] if scale_of else src[:, g, :]
            tp = pe.do(lambda e, j=j, b=b, row=row: e.transpose(b.ap[:, j * P:(j + 1) * P], row, c.ident[:]),
                       t, *(() if scale_of else rows(g)), *b.free)
        if s:
            s.free = [tp]
        out = dst[:, n * BANK:(n + 1) * BANK]
        if affine:
            fn = lambda e, b=b, out=out: e.activation(out, b.ap, ACT.Identity, scale=affine[0], bias=affine[1])
        else:
            fn = lambda e, b=b, out=out: e.activation(out, b.ap, ACT.Copy)
        b.free = [act.do(fn, tp)]
        done += b.free * 4
    return done


class Norm:

    def __init__(self, c, ctx, name):
        self.stats = c.sb(ctx, name + "_stats", [P, NTILE, 6])
        self.mv = c.sb(ctx, name + "_mv", [P, NTILE, 2])
        self.rstd = c.sb(ctx, name + "_rstd", [P, NTILE])

    def of(self, c, src, ready):
        return layer_norm_rows(c, src, self.stats, self.mv, self.rstd, c.eps, ready)


NE, FF = 8, 512
NF = FF // P
CAPACITY = -(-5 * NT // (4 * NE))


def expert_ffn(c, k, X, x_ready, cst):
    pe, dve, act, sp = c.pe, c.dve, c.act, c.sp
    with ExitStack() as ctx:
        sb = lambda name, shape: c.sb(ctx, "b_" + name, shape)
        w1, w2 = sb("w1", [P, NE, FF]), sb("w2", [P, NE, NF, D])
        b1, b2 = sb("b1", [P, NE, NF]), sb("b2", [NE, D])
        gw, gb = sb("gw", [P, NE]), sb("gb", [1, NE])
        xnT = sb("xnT", [P, NT])
        norm = Norm(c, ctx, "b")
        tri, ones = cst["tri"], cst["ones"]
        l_w = DmaCount(c.sem("s_b_w"))
        for dst, n in ((gw, "gate_w"), (gb, "gate_b"), (b1, "b1"), (b2, "b2")):
            l_w.start(sp, dst[:], k["L0_ffn_" + n])
        l_w.start(sp, w1[:], k["L0_ffn_w1"].rearrange("e d f -> d e f"))
        w_ok = l_w.start(sp, w2[:], k["L0_ffn_w2"].rearrange("e (n f) d -> f e n d", f=P))
        t = norm.of(c, X, lambda g: (x_ready,))
        xn_ok = transposed(c, ctx, "b", X, xnT, (norm.mv, norm.rstd), lambda g: (t,))

        G = [P, NTILE, NE]
        lg, ex, eq, oh, gate, pre = (sb(n, G) for n in ("lg", "ex", "eq", "oh", "gate", "pre"))
        top, prob = sb("top", [P, NTILE]), sb("prob", [P, NTILE])
        gateT = sb("gateT", [NE, NT])
        bank = c.bank(2)
        for g in range(NTILE):
            pe.run(lambda e, g=g: e.matmul(bank[:, g * NE:(g + 1) * NE], xnT[:, g * P:(g + 1) * P], gw[:],
                   start=True, stop=False), xn_ok[g], w_ok)
            tp = pe.do(lambda e, g=g: e.matmul(bank[:, g * NE:(g + 1) * NE], c.ones_row[0:1, 0:P], gb[:],
                       start=False, stop=True))
        flat = lambda a: a[:].rearrange("p g e -> p (g e)")
        over_e = lambda a: a[:].rearrange("p (g o) -> p g o", o=1).broadcast_to(G)
        dve.do(lambda e: e.tensor_copy(flat(lg), bank[:, 0:NTILE * NE]), tp)
        dve.do(lambda e: e.tensor_reduce(top[:], lg[:], AX.X, ALU.max))
        dve.do(lambda e: e.tensor_tensor(eq[:], lg[:], over_e(top), ALU.is_equal))
        t = dve.do(lambda e: e.tensor_tensor(lg[:], lg[:], over_e(top), ALU.subtract))
        t = act.do(lambda e: e.activation(flat(ex), flat(lg), ACT.Exp), t)
        dve.do(lambda e: e.tensor_reduce(prob[:], ex[:], AX.X, ALU.add), t)
        dve.do(lambda e: e.reciprocal(prob[:], prob[:]))
        dve.do(lambda e: e.memset(pre[:], 0.0))
        for j in range(1, NE):
            dve.do(lambda e, j=j: e.tensor_tensor(pre[:, :, j], pre[:, :, j - 1], eq[:, :, j - 1], ALU.add))
        dve.do(lambda e: e.tensor_scalar(pre[:], pre[:], 0.0, None, ALU.is_equal))
        t = dve.do(lambda e: e.tensor_tensor(oh[:], eq[:], pre[:], ALU.mult))
        within, totals = c.bank(3)[:, 0:NTILE * NE], c.bank(4)[:, 0:NTILE * NE]
        pe.run(lambda e: e.matmul(within, tri[:], flat(oh), start=True, stop=True), t)
        tp = pe.do(lambda e: e.matmul(totals, ones[:], flat(oh), start=True, stop=True))
        dve.do(lambda e: e.tensor_copy(flat(ex), totals), tp)
        dve.do(lambda e: e.memset(pre[:, 0, :], 0.0))
        for g in range(1, NTILE):
            dve.do(lambda e, g=g: e.tensor_tensor(pre[:, g, :], pre[:, g - 1, :], ex[:, g - 1, :], ALU.add))
        dve.do(lambda e: e.tensor_tensor(flat(pre), flat(pre), within, ALU.add))
        dve.do(lambda e: e.tensor_scalar(pre[:], pre[:], float(CAPACITY), None, ALU.is_le))
        dve.do(lambda e: e.tensor_tensor(gate[:], oh[:], pre[:], ALU.mult))
        g_ok = dve.do(lambda e: e.tensor_tensor(gate[:], gate[:], over_e(prob), ALU.mult))

        banks = Ring([Slot(c.bank(i)) for i in range(2)])
        for n in range(NTILE // 4):
            b = banks.next()
            b.free = b.free or [act.last()]
            for j in range(4):
                g = 4 * n + j
                tp = pe.do(lambda e, b=b, j=j, g=g: e.transpose(b.ap[0:NE, j * P:(j + 1) * P], gate[:, g, :], c.ident[:]),
                           g_ok, *b.free)
            b.free = [act.do(lambda e, b=b, n=n: e.activation(gateT[:, n * BANK:(n + 1) * BANK], b.ap[0:NE, :], ACT.Copy), tp)]
        gt_ok = act.last()
        for n in range(NTILE // 4):
            b = banks.next()
            for j in range(4):
                g = 4 * n + j
                tp = pe.do(lambda e, b=b, j=j, g=g: e.matmul(b.ap[:, j * P:(j + 1) * P], gateT[:, g * P:(g + 1) * P], b2[:],
                           start=True, stop=True), gt_ok, *b.free)
            b.free = [dve.do(lambda e, b=b, n=n: e.tensor_tensor(X[:, 4 * n:4 * n + 4, :].rearrange("p g d -> p (g d)"),
                             X[:, 4 * n:4 * n + 4, :].rearrange("p g d -> p (g d)"), b.ap, ALU.add), tp)]
        up = Ring([Slot(c.bank(i)) for i in range(4)])
        down = Ring([Slot(c.bank(4 + i)) for i in range(4)])
        for s in up.slots + down.slots:
            s.free = [act.last(), dve.last()]
        hid = Ring([Slot(sb(f"hid{i}", [P, NF, BANK])) for i in range(2)])

        def rise(n, ex_):
            h = hid.next()
            for f in range(NF):
                b = up.next()
                tp = pe.do(lambda e, b=b, f=f: e.matmul(b.ap, w1[:, ex_, f * P:(f + 1) * P], xnT[:, n * BANK:(n + 1) * BANK],
                           start=True, stop=True), *b.free)
                t = act.do(lambda e, b=b, f=f, h=h: e.activation(h.ap[:, f, :], b.ap, ACT.Relu, bias=b1[:, ex_, f:f + 1]),
                           tp, *h.free)
                b.free = [t]
            return h, t

        def fall(n, ex_, h, ready):
            b = down.next()
            for j in range(4):
                for f in range(NF):
                    tp = pe.do(lambda e, b=b, j=j, f=f: e.matmul(b.ap[:, j * P:(j + 1) * P], h.ap[:, f, j * P:(j + 1) * P],
                               w2[:, ex_, f, :], start=(f == 0), stop=(f == NF - 1)), ready, *b.free)
            h.free = [tp]
            for j in range(4):
                g = 4 * n + j
                t = dve.do(lambda e, b=b, j=j, g=g: e.scalar_tensor_tensor(X[:, g, :], b.ap[:, j * P:(j + 1) * P],
                           gate[:, g, ex_:ex_ + 1], X[:, g, :], ALU.mult, ALU.add), tp)
            b.free = [t]

        waiting = None
        for n in range(NT // BANK):
            for ex_ in range(NE):
                h, t = rise(n, ex_)
                if waiting:
                    fall(*waiting)
                waiting = (n, ex_, h, t)
        fall(*waiting)
        c.barrier()


NEG = -1e30


class Attention:
    TURN_LAG, OUT_LAG = 3, 1

    def __init__(self, c, ctx, name, nkeys, scores, turns, outs):
        self.c, self.nkeys = c, nkeys
        self.score, self.turn, self.out = (Ring([Slot(c.bank(i)) for i in n]) for n in (scores, turns, outs))
        self.S = Ring([Slot(c.sb(ctx, f"{name}_s{i}", [P, nkeys])) for i in range(self.TURN_LAG + 2)])
        self.PT = Ring([Slot(c.sb(ctx, f"{name}_pt{i}", [P, nkeys])) for i in range(self.OUT_LAG + 2)])
        self.low = Ring([Slot(c.sb(ctx, f"{name}_low{i}", [P, 1])) for i in range(4)])
        self.scored, self.turned, self.n = [], [], 0

    def unit(self, score, mask, scale, rowsum, values, o, after, then=None):
        c, w = self.c, mask.shape[-1]
        b, s, lo = self.score.next(), self.S.next(), self.low.next()
        for fn in score[:-1]:
            c.pe.run(lambda e, fn=fn: fn(e, b.ap), *after, *b.free)
        tp = c.pe.do(lambda e: score[-1](e, b.ap), *after, *b.free)
        t = c.dve.go(lambda e: e.tensor_tensor_reduce(out=s.ap[:, 0:w], in0=b.ap[:, 0:w], in1=mask, scale=scale,
                     scalar=3e38, op0=ALU.add, op1=ALU.min, accum_out=lo.ap[:, 0:1]), tp, *after, *s.free, *lo.free)
        b.free = [t]
        ta = c.act.go(lambda e: e.activation(s.ap[:, 0:w], s.ap[:, 0:w], ACT.Exp, scale=-1.0, bias=lo.ap[:, 0:1],
                      accum_out=rowsum), t, *after)
        lo.free = [ta]
        self.scored.append((s, ta, w, values, o, then))
        if len(self.scored) > self.TURN_LAG:
            self.transpose()
        return tp

    def transpose(self):
        c = self.c
        s, ta, w, values, o, then = self.scored.pop(0)
        b, pt = self.turn.next(), self.PT.next()
        for j in range(w // P):
            tp = c.pe.do(lambda e, j=j: e.transpose(b.ap[:, j * P:(j + 1) * P], s.ap[:, j * P:(j + 1) * P], c.ident[:]),
                         ta, *b.free)
        s.free = [tp]
        self.n += 1
        if self.n % 2:
            t = c.act.go(lambda e: e.activation(pt.ap[:, 0:w], b.ap[:, 0:w], ACT.Copy), tp, *pt.free)
        else:
            t = c.dve.go(lambda e: e.tensor_copy(pt.ap[:, 0:w], b.ap[:, 0:w]), tp, *pt.free)
        b.free = [t]
        self.turned.append((pt, t, ta, values, o, then))
        if len(self.turned) > self.OUT_LAG:
            self.product()

    def product(self):
        pt, t, ta, values, o, then = self.turned.pop(0)
        for j, v in enumerate(values):
            tp = self.c.pe.do(lambda e, j=j, v=v: e.matmul(o.ap, pt.ap[:, j * P:(j + 1) * P], v, start=(j == 0),
                              stop=(j == len(values) - 1)), t, *o.slot.free)
        pt.free = [tp]
        if then:
            then(tp, ta)

    def drain(self):
        while self.scored:
            self.transpose()
        while self.turned:
            self.product()


class Part:

    def __init__(self, slot, ap):
        self.slot, self.ap = slot, ap


H1, HD = 16, 8
LEFT, RIGHT = 127, 128


def banded_attention(c, k, X, cst_dram):
    pe, dve, act, pool, sp = c.pe, c.dve, c.act, c.pool, c.sp
    with ExitStack() as ctx:
        sb = lambda name, shape: c.sb(ctx, "c_" + name, shape)
        wqk, wv = sb("wqk", [P, 4, P]), sb("wv", [P, P])
        wo, bo = sb("wo", [P, D]), sb("bo", [1, D])
        cos, sin, heads, band = sb("cos", [P, T]), sb("sin", [P, T]), sb("heads", [P, H1]), sb("band", [P, 3 * P])
        qT, kT = sb("qT", [P, NT]), sb("kT", [P, NT])
        V = sb("V", [P, NTILE, D])
        l_w = DmaCount(c.sem("s_c_w"))
        l_w.start(sp, wqk[:], k["L1_wqk"])
        l_w.start(sp, wv[:], k["L1_wv"])
        l_w.start(sp, wo[:], k["L1_attn_w_out"])
        l_w.start(sp, bo[:], k["L1_attn_b_out"])
        for dst, n in ((cos, "rope_cos"), (sin, "rope_sin"), (heads, "head_rows")):
            l_w.start(sp, dst[:], cst_dram[n])
        w_ok = l_w.start(sp, band[:], cst_dram["band"])
        with ExitStack() as pctx:
            xnT = c.sb(pctx, "c_xnT", [P, NT])
            tmp = Ring([Slot(c.sb(pctx, f"c_tmp{i}", [P, BANK])) for i in range(2)])
            norm = Norm(c, pctx, "c")
            t = norm.of(c, X, lambda g: ())
            xn_ok = transposed(c, pctx, "c", X, xnT, (norm.mv, norm.rstd), lambda g: (t,))
            pair = Ring([Slot(c.bank(2, 2)), Slot(c.bank(4, 2))])
            for n in range(NT // BANK):
                cols, pos = slice(n * BANK, (n + 1) * BANK), slice(n * BANK % T, n * BANK % T + BANK)
                for z, dst in enumerate((qT, kT)):
                    b, s = pair.next(), tmp.next()
                    for m in range(2):
                        tp = pe.do(lambda e, b=b, m=m, z=z, cols=cols: e.matmul(b.ap[:, m * BANK:(m + 1) * BANK],
                                   wqk[:, 2 * z + m, :], xnT[:, cols], start=True, stop=True), xn_ok[4 * n + 3], w_ok, *b.free)
                    dve.do(lambda e, b=b, dst=dst, cols=cols, pos=pos: e.tensor_tensor(dst[:, cols], b.ap[:, 0:BANK], cos[:, pos],
                           ALU.mult), tp)
                    t = dve.do(lambda e, b=b, s=s, pos=pos: e.tensor_tensor(s.ap[:], b.ap[:, BANK:], sin[:, pos], ALU.mult), *s.free)
                    b.free = [t]
                    s.free = [pool.do(lambda e, dst=dst, s=s, cols=cols: e.tensor_tensor(dst[:, cols], dst[:, cols], s.ap[:], ALU.add), t)]
            vb = Ring([Slot(c.bank(6)), Slot(c.bank(7))])
            for n in range(NTILE // 4):
                b = vb.next()
                for j in range(4):
                    g = 4 * n + j
                    tp = pe.do(lambda e, b=b, j=j, g=g: e.matmul(b.ap[:, j * P:(j + 1) * P], xnT[:, g * P:(g + 1) * P], wv[:],
                               start=True, stop=True), xn_ok[g], *b.free)
                b.free = [act.do(lambda e, b=b, n=n: e.activation(V[:, 4 * n:4 * n + 4, :].rearrange("p g d -> p (g d)"), b.ap,
                                 ACT.Copy), tp)]
            c.barrier()
        att = Attention(c, ctx, "c", 3 * P, (0, 1, 2), (3, 4), (5, 6))
        qm = Ring([Slot(sb(f"qm{i}", [P, H1, P])) for i in range(2)])
        rows = Ring([Slot(sb(f"rows{i}", [P, H1])) for i in range(2)])
        on = Ring([Slot(sb(f"on{i}", [P, D])) for i in range(2)])
        oT = Ring([Slot(sb(f"oT{i}", [P, P])) for i in range(2)])
        last = Slot(c.bank(7))
        later = []

        def project_out(g, o, ot, t):
            tp = pe.do(lambda e: e.transpose(last.ap[:, 0:P], o.ap[:], c.ident[:]), t, *last.free)
            o.free = [tp]
            t = act.do(lambda e: e.activation(ot.ap[:], last.ap[:, 0:P], ACT.Copy), tp, *ot.free)
            later.append(lambda: add_out(g, ot, t))

        def add_out(g, ot, t):
            pe.run(lambda e: e.matmul(last.ap[:, P:2 * P], ot.ap[:], wo[:], start=True, stop=False), t)
            tp = pe.do(lambda e: e.matmul(last.ap[:, P:2 * P], c.ones_row[0:1, 0:P], bo[:], start=False, stop=True))
            ot.free = [tp]
            last.free = [dve.do(lambda e: e.tensor_tensor(X[:, g, :], X[:, g, :], last.ap[:, P:2 * P], ALU.add), tp)]

        for g in range(NTILE):
            bi, tt = divmod(g, TPB)
            q = qm.next()
            src = qT[:, g * P:(g + 1) * P].rearrange("p (o t) -> p o t", o=1).broadcast_to([P, H1, P])
            hm = heads[:].rearrange("p (h o) -> p h o", o=1).broadcast_to([P, H1, P])
            tq = pool.do(lambda e, q=q, src=src, hm=hm: e.tensor_tensor(q.ap[:], src, hm, ALU.mult), *q.free)
            lo, hi = max(tt - 1, 0), min(tt + 1, TPB - 1)
            nk = hi - lo + 1
            m0 = (lo - tt + 1) * P
            mask = band[:, m0:m0 + nk * P]
            keys = kT[:, (bi * TPB + lo) * P:(bi * TPB + hi + 1) * P]
            rs, ob = rows.next(), att.out.next()
            for h in range(H1):
                part = Part(ob, ob.ap[:, h * HD:(h + 1) * HD])
                vals = [V[:, bi * TPB + j, h * HD:(h + 1) * HD] for j in range(lo, hi + 1)]
                then = None
                if h == H1 - 1:
                    def then(tp, ta, rs=rs, ob=ob, g=g):
                        o, ot = on.next(), oT.next()
                        dve.do(lambda e: e.reciprocal(rs.ap[:], rs.ap[:]), ta)
                        t = dve.do(lambda e: e.tensor_tensor(o.ap[:].rearrange("p (h d) -> p h d", d=HD),
                                   ob.ap[:, 0:D].rearrange("p (h d) -> p h d", d=HD),
                                   rs.ap[:].rearrange("p (h o) -> p h o", o=1).broadcast_to([P, H1, HD]), ALU.mult), tp, *o.free)
                        rs.free, ob.free = [t], [t]
                        later.append(lambda: project_out(g, o, ot, t))
                score = [lambda e, ap, q=q, h=h, keys=keys, nk=nk: e.matmul(ap[:, 0:nk * P], q.ap[:, h, :], keys, start=True, stop=True)]
                tp = att.unit(score, mask, -HD ** -0.5, rs.ap[:, h:h + 1], vals, part, [tq, *rs.free], then)
                if later and h % 3 == 1:
                    later.pop(0)()
            q.free = [tp]
        att.drain()
        while later:
            later.pop(0)()
        c.barrier()
DEPTH, H2, DH, WINDOW = 2, 8, 64, 64
INNER = H2 * DH
HID = int(D * 4 * 2 / 3)
NH = -(-HID // P)
QK_SCALE = 8.0


def shift_tokens(c, X, Hs, dma, zeroed):
    sp, half = c.sp, D // 2
    xr, tail = X[:], slice(half, D)
    ready = [c.dve.last(), zeroed]
    dma.start(sp, Hs[:, :, 0:half], X[:, :, 0:half], *ready)
    dma.start(sp, Hs[1:P, :, tail], X[0:P - 1, :, tail], *ready)
    for b in range(NB):
        g = b * TPB
        t = dma.start(sp, Hs[0:1, g + 1:g + TPB, tail], X[P - 1:P, g:g + TPB - 1, tail], *ready)
    return t


def local_layer(c, k, X, l, cst_dram):
    pe, dve, act, pool, sp = c.pe, c.dve, c.act, c.pool, c.sp
    with ExitStack() as ctx:
        sb = lambda name, shape: c.sb(ctx, f"d{l}_" + name, shape)
        wqkv = sb("wqkv", [P, 3 * INNER])
        wo = sb("wo", [P, INNER // P, D])
        w1 = sb("w1", [P, 2 * HID])
        w2 = sb("w2", [P, NH, D])
        b1a, b1g, b2 = sb("b1a", [P, NH]), sb("b1g", [P, NH]), sb("b2", [1, D])
        lnw, lnb = sb("lnw", [P, 1]), sb("lnb", [P, 1])
        Hs = sb("hs", [P, NTILE, D])
        hT = sb("hT", [P, NT])
        norm = Norm(c, ctx, f"d{l}")
        l_w, l_h = DmaCount(c.sem(f"s_d{l}_w")), DmaCount(c.sem(f"s_d{l}_shift"))
        z = dve.do(lambda e: e.memset(Hs[0:1, 0:NTILE:TPB, D // 2:D], 0.0))
        h_ok = shift_tokens(c, X, Hs, l_h, z)
        l_w.start(sp, wqkv[:], k["L1_ffn_wqkv"][l])
        l_w.start(sp, wo[:], k["L1_ffn_wo"][l].rearrange("(n p) d -> p n d", p=P))
        l_w.start(sp, w1[:], k["L1_ffn_w1"][l])
        full = HID // P
        l_w.start(sp, w2[:, 0:full, :], k["L1_ffn_w2"][l, 0:full * P].rearrange("(n p) d -> p n d", p=P))
        l_w.start(sp, w2[0:HID - full * P, full, :], k["L1_ffn_w2"][l, full * P:HID])
        for half, dst in enumerate((b1a, b1g)):
            l_w.start(sp, dst[:, 0:full], k["L1_b1_full"][l, half])
            l_w.start(sp, dst[0:HID - full * P, full:full + 1], k["L1_b1_rest"][l, half])
        l_w.start(sp, b2[:], k["L1_ffn_b2"][l:l + 1, :])
        l_w.start(sp, lnw[:], k["L1_ffn_ln_g"][l])
        w_ok = l_w.start(sp, lnb[:], k["L1_ffn_ln_b"][l])

        with ExitStack() as actx:
            asb = lambda name, shape: c.sb(actx, f"d{l}_" + name, shape)
            tab = asb("tab", [P, 2, 2, TPB, DH])
            sc = asb("sc", [P, 2, DH])
            mask = asb("mask", [P, 2 * P])
            l_t = DmaCount(c.sem(f"s_d{l}_tab"))
            l_t.start(sp, tab[:], cst_dram["xpos"])
            l_t.start(sp, mask[:], cst_dram["local"])
            l_t.start(sp, sc[:, 0, :], k["L1_ffn_q_scale"][l:l + 1, :].broadcast_to([P, DH]))
            t_ok = l_t.start(sp, sc[:, 1, :], k["L1_ffn_k_scale"][l:l + 1, :].broadcast_to([P, DH]))
            hf = DH // 2
            for z in range(2):
                one = sc[:, z, :].rearrange("p (o d) -> p o d", o=1).broadcast_to([P, TPB, DH])
                dve.do(lambda e, z=z, one=one: e.tensor_tensor(tab[:, z, 0], tab[:, z, 0], one, ALU.mult), t_ok)
                for a in range(2):
                    v = tab[:, z, 1, :, a * hf:(a + 1) * hf]
                    o = sc[:, z, (1 - a) * hf:(2 - a) * hf].rearrange("p (o d) -> p o d", o=1).broadcast_to([P, TPB, hf])
                    tab_ok = dve.do(lambda e, v=v, o=o: e.tensor_tensor(v, v, o, ALU.mult))
            hT_ok = transposed(c, actx, f"d{l}a", Hs, hT, rows=lambda g: (h_ok,))
            c.barrier()

            att = Attention(c, actx, f"d{l}", 2 * P, (0, 1), (2, 3), (4, 5))
            raw = Ring([Slot(asb(f"raw{i}", [P, 2, INNER])) for i in range(2)])
            rot = Ring([Slot(asb(f"rot{i}", [P, 2, INNER])) for i in range(2)])
            sw = Ring([Slot(asb(f"sw{i}", [P, 2, INNER])) for i in range(2)])
            nrm = Ring([Slot(asb(f"nrm{i}", [P, 2, H2])) for i in range(2)])
            qT = Ring([Slot(asb(f"qT{i}", [P, 4, P])) for i in range(2)])
            kT = Ring([Slot(asb(f"kT{i}", [P, 4, P])) for i in range(3)])
            V = Ring([Slot(asb(f"V{i}", [P, INNER])) for i in range(4)])
            rows = Ring([Slot(asb(f"rows{i}", [P, H2])) for i in range(2)])
            on = Ring([Slot(asb(f"on{i}", [P, INNER])) for i in range(2)])
            oT = Ring([Slot(asb(f"oT{i}", [P, 4, P])) for i in range(2)])
            pre, last = Slot(c.bank(6)), Slot(c.bank(7))
            later = []
            heads = lambda a: a.rearrange("p (h d) -> p h d", d=DH)

            def prepare(g):
                tt = g % TPB
                r, ro, s, nr, q, kk, v = (x.next() for x in (raw, rot, sw, nrm, qT, kT, V))
                cur = dict(q=q, k=kk, v=v, nr=nr)
                st = {}

                def project(z):
                    tp = pe.do(lambda e: e.matmul(pre.ap, hT[:, g * P:(g + 1) * P], wqkv[:, z * INNER:(z + 1) * INNER],
                               start=True, stop=True), w_ok, hT_ok[g], *pre.free)
                    dst = r.ap[:, z, :] if z < 2 else v.ap[:]
                    pre.free = [act.do(lambda e: e.activation(dst, pre.ap, ACT.Copy), tp, *(r.free if z < 2 else v.free))]
                    st["raw", z] = pre.free[0]

                def squares():
                    t2 = act.do(lambda e: e.activation(s.ap[:], r.ap[:], ACT.Square), *s.free)
                    st["sq"] = dve.go(lambda e: e.tensor_reduce(nr.ap[:].rearrange("p z h -> p (z h)"),
                                      s.ap[:].rearrange("p z (h d) -> p (z h) d", d=DH), AX.X, ALU.add), t2, *nr.free)

                def norms():
                    t = act.do(lambda e: e.activation(nr.ap[:], nr.ap[:], ACT.Sqrt), st["sq"])
                    dve.do(lambda e: e.tensor_scalar(nr.ap[:], nr.ap[:], 1e-12, None, ALU.max), t)
                    dve.do(lambda e: e.reciprocal(nr.ap[:], nr.ap[:]))
                    st["norms"] = dve.do(lambda e: e.tensor_scalar(nr.ap[:, 0, :], nr.ap[:, 0, :], -QK_SCALE, None, ALU.mult))

                def rotate(z):
                    cs = tab[:, z, 0, tt, :].rearrange("p (o d) -> p o d", o=1).broadcast_to([P, H2, DH])
                    for a in range(2):
                        sn = tab[:, z, 1, tt, a * hf:(a + 1) * hf].rearrange("p (o d) -> p o d", o=1).broadcast_to([P, H2, hf])
                        tb = pool.go(lambda e, z=z, a=a, sn=sn: e.tensor_tensor(heads(s.ap[:, z, :])[:, :, a * hf:(a + 1) * hf],
                                     heads(r.ap[:, z, :])[:, :, (1 - a) * hf:(2 - a) * hf], sn, ALU.mult), st["raw", 1], st["sq"])
                    ta = dve.go(lambda e: e.tensor_tensor(heads(ro.ap[:, z, :]), heads(r.ap[:, z, :]), cs, ALU.mult),
                                st["raw", 1], *ro.free)
                    st["rot", z] = ta, tb

                def add_up():
                    t = dve.go(lambda e: e.tensor_tensor(ro.ap[:], ro.ap[:], s.ap[:], ALU.add), *st["rot", 0], *st["rot", 1])
                    r.free, s.free = [t], [t]
                    kn = nr.ap[:, 1, :].rearrange("p (h o) -> p h o", o=1).broadcast_to([P, H2, DH])
                    st["done"] = dve.do(lambda e: e.tensor_tensor(heads(ro.ap[:, 1, :]), heads(ro.ap[:, 1, :]), kn, ALU.mult),
                                        st["norms"])

                def turn(z, dst):
                    for j in range(4):
                        tp = pe.do(lambda e, j=j: e.transpose(pre.ap[:, j * P:(j + 1) * P], ro.ap[:, z, j * P:(j + 1) * P],
                                   c.ident[:]), st["done"], *pre.free)
                    pre.free = [act.do(lambda e: e.activation(dst.ap[:].rearrange("p n t -> p (n t)"), pre.ap, ACT.Copy),
                                       tp, *dst.free)]
                    ro.free = [tp]
                    cur["ok"] = pre.free[0]

                cur["jobs"] = [[lambda: project(0)], [lambda: project(1)], [lambda: project(2), squares],
                               [norms, lambda: rotate(0)], [lambda: rotate(1)], [add_up], [lambda: turn(0, q)],
                               [lambda: turn(1, kk)]]
                return cur

            prev, cur = None, prepare(0)
            for batch in cur["jobs"]:
                for job in batch:
                    job()
            for g in range(NTILE):
                nxt = prepare(g + 1) if g + 1 < NTILE else None
                blocks = ([prev] if g % TPB else []) + [cur]
                m = mask[:, (2 - len(blocks)) * P:]
                rs, ob = rows.next(), att.out.next()
                for h in range(H2):
                    ps, pr = slice(h % 2 * DH, h % 2 * DH + DH), h // 2
                    part = Part(ob, ob.ap[:, h * DH:(h + 1) * DH])
                    then = None
                    if h == H2 - 1:
                        def then(tp, ta, rs=rs, ob=ob, g=g, cur=cur, prev=prev):
                            o, ot = on.next(), oT.next()
                            for x in (prev, cur):
                                if x:
                                    x["v"].free = x["k"].free = [tp]
                            dve.do(lambda e: e.reciprocal(rs.ap[:], rs.ap[:]), ta)
                            t = dve.do(lambda e: e.tensor_tensor(heads(o.ap[:]), heads(ob.ap),
                                       rs.ap[:].rearrange("p (h o) -> p h o", o=1).broadcast_to([P, H2, DH]), ALU.mult), tp, *o.free)
                            rs.free, ob.free = [t], [t]
                            later.append(lambda: turn_out(g, o, ot, t))

                        def turn_out(g, o, ot, t):
                            for j in range(4):
                                tp = pe.do(lambda e, j=j: e.transpose(last.ap[:, j * P:(j + 1) * P], o.ap[:, j * P:(j + 1) * P],
                                           c.ident[:]), t, *last.free)
                            o.free = [tp]
                            t = act.do(lambda e: e.activation(ot.ap[:].rearrange("p n t -> p (n t)"), last.ap, ACT.Copy), tp, *ot.free)
                            later.append(lambda: project_out(g, ot, t))

                        def project_out(g, ot, t):
                            for j in range(4):
                                tp = pe.do(lambda e, j=j: e.matmul(last.ap[:, 0:D], ot.ap[:, j, :], wo[:, j, :], start=(j == 0),
                                           stop=(j == 3)), t)
                            ot.free = [tp]
                            last.free = [dve.do(lambda e: e.tensor_tensor(X[:, g, :], X[:, g, :], last.ap[:, 0:D], ALU.add), tp)]
                    score = [lambda e, ap, j=j, x=x, ps=ps, pr=pr, cur=cur: e.matmul(ap[:, j * P:(j + 1) * P], cur["q"].ap[ps, pr, :],
                             x["k"].ap[ps, pr, :], start=True, stop=True) for j, x in enumerate(blocks)]
                    tp = att.unit(score, m, cur["nr"].ap[:, 0, h:h + 1], rs.ap[:, h:h + 1],
                                  [x["v"].ap[:, h * DH:(h + 1) * DH] for x in blocks], part, [cur["ok"], *rs.free], then)
                    unit_dve = dve.last()
                    if later and h % 2:
                        later.pop(0)()
                    for job in (nxt["jobs"][h] if nxt else []):
                        job()
                cur["q"].free, cur["nr"].free = [tp], [unit_dve]
                prev, cur = cur, nxt
            att.drain()
            while later:
                later.pop(0)()
            c.barrier()

        z = dve.do(lambda e: e.memset(Hs[0:1, 0:NTILE:TPB, D // 2:D], 0.0))
        h_ok = shift_tokens(c, X, Hs, l_h, z)
        t = norm.of(c, Hs, lambda g: (h_ok,))
        hT_ok = transposed(c, ctx, f"d{l}f", Hs, hT, (norm.mv, norm.rstd), lambda g: (t,), affine=(lnw[:, 0:1], lnb[:, 0:1]))
        c.barrier()
        up = Ring([Slot(c.bank(i, 2)) for i in (0, 2)])
        down = Ring([Slot(c.bank(i)) for i in (4, 5)])
        gl = Ring([Slot(sb(f"gl{i}", [P, BANK])) for i in range(2)])
        hid = Ring([Slot(sb(f"hid{i}", [P, NH, BANK])) for i in range(2)])

        def rise(n):
            h = hid.next()
            for f in range(NH):
                w = min(P, HID - f * P)
                b, s = up.next(), gl.next()
                for z in range(2):
                    c0 = z * HID + f * P
                    tp = pe.do(lambda e, b=b, z=z, c0=c0, w=w: e.matmul(b.ap[0:w, z * BANK:(z + 1) * BANK], w1[:, c0:c0 + w],
                               hT[:, n * BANK:(n + 1) * BANK], start=True, stop=True), *b.free)
                t = act.do(lambda e, b=b, s=s, f=f, w=w: e.activation(s.ap[0:w, :], b.ap[0:w, BANK:], ACT.Gelu, bias=b1g[0:w, f:f + 1]),
                           tp, *s.free)
                t = dve.do(lambda e, b=b, s=s, f=f, w=w, h=h: e.scalar_tensor_tensor(h.ap[0:w, f, :], b.ap[0:w, 0:BANK],
                           b1a[0:w, f:f + 1], s.ap[0:w, :], ALU.add, ALU.mult), t, *h.free)
                b.free, s.free = [t], [t]
            return n, h, t

        def fall(n, h, ready):
            b = down.next()
            for j in range(4):
                for f in range(NH):
                    w = min(P, HID - f * P)
                    pe.run(lambda e, b=b, j=j, f=f, w=w: e.matmul(b.ap[:, j * P:(j + 1) * P], h.ap[0:w, f, j * P:(j + 1) * P],
                           w2[0:w, f, :], start=(f == 0), stop=False), ready, *b.free)
                tp = pe.do(lambda e, b=b, j=j: e.matmul(b.ap[:, j * P:(j + 1) * P], c.ones_row[0:1, 0:P], b2[:], start=False, stop=True))
            h.free = [tp]
            xv = X[:, 4 * n:4 * n + 4, :].rearrange("p g d -> p (g d)")
            b.free = [dve.do(lambda e, b=b: e.tensor_tensor(xv, xv, b.ap, ALU.add), tp)]

        waiting = None
        for n in range(NT // BANK):
            nxt = rise(n)
            if waiting:
                fall(*waiting)
            waiting = nxt
        fall(*waiting)
        c.barrier()
def constants():
    p = np.arange(P)
    keep, phase = {}, {}
    keep["ident"] = np.eye(P)
    keep["ones_row"] = np.ones((1, P))
    keep["eps"] = np.full((P, 1), EPS)
    keep["half_of"] = np.stack([p % 32 < CK, p % 32 >= CK], 1)
    keep["ih_mask"] = np.stack([p // 32 % 2 == 0, p // 32 % 2 == 1], 1)
    same = p[:, None] // DK == p[None, :] // DK
    keep["pair_ones"] = same
    keep["own"] = ((p[:, None, None] % 32 == np.arange(R)[None, :, None]) &
                   (p[:, None, None] // 32 % 2 == np.arange(2)[None, None, :])).reshape(P, 2 * R)
    phase["tri"] = p[:, None] <= p[None, :]
    phase["ones"] = np.ones((P, P))
    f32 = np.float32
    inv = f32(1.0) / f32(10000.0) ** (np.arange(0, HD, 2, dtype=f32) / f32(HD))
    ang = (np.arange(T, dtype=f32)[None, :] * inv[p % HD % (HD // 2)][:, None]).astype(f32)
    phase["rope_cos"] = np.cos(ang)
    phase["rope_sin"] = np.sin(ang) * np.where(p % HD < HD // 2, -1.0, 1.0)[:, None]
    phase["head_rows"] = p[:, None] // HD == np.arange(H1)[None, :]
    i, j = p[:, None], np.arange(3 * P)[None, :] - P
    phase["band"] = np.where((j >= i - LEFT) & (j <= i + RIGHT), 0.0, NEG)
    i, j = p[:, None], np.arange(2 * P)[None, :] - P
    phase["local"] = np.where((j <= i) & (j >= i - WINDOW), 0.0, NEG)
    half = np.arange(0, DH, 2, dtype=f32)
    inv = f32(1.0) / f32(10000.0) ** (half / f32(DH))
    t = np.arange(T, dtype=f32)
    ang = np.concatenate([t[:, None] * inv[None, :]] * 2, 1)
    base = (half + f32(0.4 * DH)) / f32(1.4 * DH)
    power = (t - T // 2) / f32(WINDOW // 2)
    scale = np.concatenate([base[None, :] ** power[:, None]] * 2, 1).astype(f32)
    sign = np.where(np.arange(DH) < DH // 2, -1.0, 1.0)[None, :].astype(f32)
    cos, sin = np.cos(ang), np.sin(ang) * sign
    tab = np.stack([[cos * scale, sin * scale], [cos / scale, sin / scale]])
    phase["xpos"] = tab.reshape(2, 2, TPB, P, DH).transpose(3, 0, 1, 2, 4)
    conv = lambda d: {n: np.ascontiguousarray(a, dtype=np.float32) for n, a in d.items()}
    return conv(keep), conv(phase)


def layouts(inputs):
    k = {n: np.ascontiguousarray(a) for n, a in inputs.items()}
    for n in ("L0_attn_qcb", "L0_attn_kcb", "L0_attn_vcb", "L0_attn_ba"):
        k[n] = k[n].reshape(NCT, P).T
    for n in ("L0_attn_qcw", "L0_attn_kcw", "L0_attn_vcw"):
        k[n] = k[n].reshape(NCT, P, TAPS).transpose(1, 0, 2)
    for n in ("L0_attn_ln_w", "L0_attn_ln_b"):
        k[n] = np.concatenate([k[n], k[n]])[:, None]
    k["L0_attn_bb"] = k["L0_attn_bb"][None, :]
    k["L0_ffn_gate_w"] = k["L0_ffn_gate_w"].T
    k["L0_ffn_gate_b"] = k["L0_ffn_gate_b"][None, :]
    k["L0_ffn_b1"] = k["L0_ffn_b1"].reshape(NE, NF, P).transpose(2, 0, 1)
    w = k.pop("L1_attn_w_qkv").reshape(3, H1, 2, HD // 2, D)
    rows = [w[0], w[0][:, ::-1], w[1], w[1][:, ::-1]]
    k["L1_wqk"] = np.stack([r.reshape(P, D).T for r in rows], 1)
    k["L1_wv"] = w[2].reshape(P, D).T
    k["L1_attn_w_out"] = k["L1_attn_w_out"].T
    k["L1_attn_b_out"] = k["L1_attn_b_out"][None, :]
    b1 = k.pop("L1_ffn_b1").reshape(DEPTH, 2, HID)
    full = HID // P * P
    k["L1_b1_full"] = b1[:, :, :full].reshape(DEPTH, 2, HID // P, P).transpose(0, 1, 3, 2)
    k["L1_b1_rest"] = b1[:, :, full:, None]
    for n in ("L1_ffn_ln_g", "L1_ffn_ln_b"):
        k[n] = k[n][:, :, None]
    return {n: np.ascontiguousarray(a) for n, a in k.items()}


def build(nc, shapes, phases="ABCD", nseg=NSEG, x_from="L0_attn_x"):
    keep, phase = constants()
    dram = lambda n, shape, kind: nc.dram_tensor(n, list(shape), F32, kind=kind).ap()
    k = {n: dram("in_" + n, s, "ExternalInput") for n, s in shapes.items()}
    cd = {n: dram("const_" + n, a.shape, "ExternalInput") for n, a in {**keep, **phase}.items()}
    out = dram("out_0", [NB, T, D], "ExternalOutput")
    x1, xn = dram("x1", [NB, T, D], "Internal"), dram("xn", [P, NB, T + PAD], "Internal")
    with ExitStack() as ctx:
        c = Core(nc, ctx)
        cst, l_c = {}, DmaCount(c.sem("s_const"))
        for n, a in keep.items():
            cst[n] = c.sb(ctx, "k_" + n, list(a.shape))
            ready = l_c.start(c.sp, cst[n][:], cd[n])
        for s in (c.pe, c.dve, c.act, c.pool):
            s.wait(ready)
        c.ident, c.eps, c.ones_row = cst["ident"], cst["eps"], cst["ones_row"]
        if "A" in phases:
            delta_rule_attention(c, k, k["L0_attn_x"], x1, xn, cst, nseg)
        rows = lambda a: a.rearrange("b (n p) d -> p (b n) d", p=P)
        X = c.sb(ctx, "x", [P, NTILE, D])
        l_x = DmaCount(c.sem("s_x"))
        for n in ("tri", "ones"):
            cst[n] = c.sb(ctx, "k_" + n, [P, P])
            l_x.start(c.sp, cst[n][:], cd[n])
        x_ready = l_x.start(c.sp, X[:], rows(x1 if "A" in phases else k[x_from]))
        for s in (c.pe, c.dve, c.act, c.pool):
            s.wait(x_ready)
        if "B" in phases:
            expert_ffn(c, k, X, x_ready, cst)
        if "C" in phases:
            banded_attention(c, k, X, cd)
        if "D" in phases:
            Y = c.sb(ctx, "y", [P, NTILE, D])
            with ExitStack() as nctx:
                norm = Norm(c, nctx, "y")
                t = norm.of(c, X, lambda g: ())
                for g in range(NTILE):
                    c.dve.do(lambda e, g=g: e.tensor_scalar(Y[:, g, :], X[:, g, :], norm.mv[:, g, 0:1], norm.rstd[:, g:g + 1],
                             ALU.subtract, ALU.mult), t)
                c.barrier()
            for l in range(DEPTH):
                local_layer(c, k, Y, l, cd)
            c.dve.do(lambda e: e.tensor_tensor(X[:], X[:], Y[:], ALU.add))
        c.sp.wait(c.stores.start(c.sp, rows(out), X[:], c.dve.last()))
        block = ctx.enter_context(nc.Block())
        for on, s in ((block.tensor, c.pe), (block.vector, c.dve), (block.scalar, c.act), (block.gpsimd, c.pool),
                      (block.sync, c.sp)):
            queue = lambda e, s=s: s.emit(e)
            on(queue)
    return {"const_" + n: a for n, a in {**keep, **phase}.items()}


_IN = "in_"


def kernel(**inputs):
    import concourse.bacc as bacc
    from concourse.bass_utils import run_bass_kernel_spmd

    nc = bacc.Bacc("TRN2", target_bir_lowering=False, num_devices=1)
    laid_out = layouts({n: np.asarray(a) for n, a in inputs.items()})
    tables = build(nc, {n: a.shape for n, a in laid_out.items()})
    arrays = {**{_IN + n: a for n, a in laid_out.items()}, **tables}
    return run_bass_kernel_spmd(nc, [arrays], core_ids=[0]).results[0]["out_0"]
```

```python
from contextlib import ExitStack

import numpy as np
import concourse.bass as bass
from concourse import mybir

F32 = mybir.dt.float32
ALU = mybir.AluOpType
ACT = mybir.ActivationFunctionType
AX = mybir.AxisListType

P = 128
NB, T, D = 4, 1024, 128
NT = NB * T
TPB = T // P
NTILE = NT // P
BANK = 512
EPS = 1e-5


class Token:

    def __init__(self, sem, value):
        self.sem, self.value = sem, value


class Stream:

    def __init__(self, sem, in_line=False):
        self.sem, self.count, self.queue, self.seen, self.in_line = sem, 0, [], {}, in_line

    def wait(self, *tokens):
        for t in tokens:
            if t is None:
                continue
            if self.seen.get(t.sem, 0) >= t.value:
                continue
            self.seen[t.sem] = t.value
            self.queue.append((t, None))

    def do(self, fn, *after):
        self.wait(*after)
        if self.in_line:
            self.wait(self.last())
        self.count += 1
        self.queue.append((self.sem, fn))
        return Token(self.sem, self.count)

    def go(self, fn, *after):
        self.wait(*after)
        self.count += 1
        self.queue.append((self.sem, fn))
        return Token(self.sem, self.count)

    def run(self, fn, *after):
        self.wait(*after)
        self.queue.append((None, fn))

    def last(self):
        return Token(self.sem, self.count) if self.count else None

    def emit(self, engine):
        for what, fn in self.queue:
            if fn is None:
                engine.wait_ge(what.sem, what.value)
            elif what is None:
                fn(engine)
            else:
                fn(engine).then_inc(what, 1)


class DmaCount:

    def __init__(self, sem):
        self.sem, self.count = sem, 0

    def start(self, stream, out, in_, *after):
        stream.wait(*after)
        self.count += 16
        sem = self.sem
        stream.queue.append((None, lambda e: e.dma_start(out, in_).then_inc(sem, 16)))
        return Token(self.sem, self.count)


class Slot:

    def __init__(self, ap):
        self.ap, self.free = ap, []


class Ring:
    def __init__(self, slots):
        self.slots, self.at = slots, 0

    def next(self):
        s = self.slots[self.at % len(self.slots)]
        self.at += 1
        return s


class Core:

    def __init__(self, nc, ctx):
        self.nc, self.ctx = nc, ctx
        self.pe, self.dve, self.act, self.pool, self.sp = (
            Stream(self.sem(n), in_line=n in ("s_dve", "s_act", "s_pool")) for n in ("s_pe", "s_dve", "s_act", "s_pool", "s_sp"))
        self.banks = ctx.enter_context(nc.psum_tensor("banks", [P, 8 * BANK], F32))
        self.stores = DmaCount(self.sem("s_stores"))

    def sem(self, name):
        return self.ctx.enter_context(self.nc.semaphore(name))

    def bank(self, n, k=1):
        return self.banks[:, n * BANK:(n + k) * BANK]

    def sb(self, ctx, name, shape):
        return ctx.enter_context(self.nc.sbuf_tensor(name, shape, F32))

    def barrier(self, *more):
        streams = (self.pe, self.dve, self.act, self.pool)
        tokens = [s.last() for s in streams]
        for s in streams + (self.sp,):
            s.wait(*[t for t in tokens], *more)


def layer_norm_rows(c, src, stats, mv, rstd, eps, ready):
    roots, done = [], []

    def invert():
        gs, t = roots.pop(0)
        t = c.dve.go(lambda e: e.reciprocal(rstd[:, gs], rstd[:, gs]), t)
        done.extend([t] * TPB)

    for b in range(NB):
        gs = slice(b * TPB, (b + 1) * TPB)
        tiles = [c.dve.go(lambda e, g=g: e.bn_stats(stats[:, g, :], src[:, g, :]), *ready(g)) for g in range(gs.start, gs.stop)]
        for g, t in zip(range(gs.start, gs.stop), tiles):
            t = c.dve.go(lambda e, g=g: e.bn_aggr(mv[:, g, :], stats[:, g, :]), t)
        roots.append((gs, c.act.go(lambda e, gs=gs: e.activation(rstd[:, gs], mv[:, gs, 1], ACT.Sqrt, bias=eps[:, 0:1]), t)))
        if b:
            invert()
    invert()
    return done
H0, DK = 16, 64
CH = H0 * DK
NCT = CH // P
R = NCT * NB
SEG, CK = 32, 16
NSEG, NCK = T // SEG, SEG // CK
TAPS = 4
PAD = TAPS - 1
SW = NB * SEG
assert R == 32 and SEG == 32


def delta_rule_attention(c, k, x_in, x1, xn_dram, cst, nseg=NSEG):
    pe, dve, act, pool, sp = c.pe, c.dve, c.act, c.pool, c.sp
    ident, eps = cst["ident"], cst["eps"]
    w_pads = DmaCount(c.sem("s_xn_pads"))
    w_xn = [DmaCount(c.sem(f"s_xn_store{i}")) for i in range(2)]

    with ExitStack() as ctx:
        sb = lambda name, shape: c.sb(ctx, "a_" + name, shape)
        wT = {n: sb("w_" + n, [P, TAPS if n in "qkv" else 1, CH]) for n in "qkvag"}
        woT = sb("w_o", [P, NCT, D])
        bias = {n: sb("bias_" + n, [P, NCT]) for n in "qkva"}
        wbT = sb("w_b", [P, H0])
        lnw, lnb = sb("lnw", [P, 1]), sb("lnb", [P, 1])
        beta = sb("beta", [P, T])
        l_x, l_b, l_w = (DmaCount(c.sem(n)) for n in ("s_a_x", "s_a_wb", "s_a_w"))
        with ExitStack() as wctx:
            raw = {n: c.sb(wctx, "a_raw_" + n, [P, NCT, D]) for n in "qkvag"}
            tap = {n: c.sb(wctx, "a_tap_" + n, [P, NCT, TAPS]) for n in "qkv"}
            raw_o = c.sb(wctx, "a_raw_o", [P, CH])
            raw_b, bb = c.sb(wctx, "a_raw_b", [H0, D]), c.sb(wctx, "a_bb", [H0, 1])
            betaT = c.sb(wctx, "a_betaT", [H0, NT])
            X = c.sb(wctx, "a_x", [P, NTILE, D])
            scaled = Ring([Slot(c.sb(wctx, f"a_scaled{i}", [P, 4, D])) for i in range(2)])
            l_b.start(sp, raw_b[:], k["L0_attn_Wb"])
            wb_loaded = l_b.start(sp, bb[:], k["L0_attn_bb"])
            loaded = l_x.start(sp, X[:], x_in.rearrange("b (n p) d -> p (b n) d", p=P))
            for n in "qkvag":
                wtok = l_w.start(sp, raw[n][:], k["L0_attn_W" + n].rearrange("(t p) d -> p t d", p=P))
            for n in "qkv":
                wtok = l_w.start(sp, tap[n][:], k[f"L0_attn_{n}cw"])
                wtok = l_w.start(sp, bias[n][:], k[f"L0_attn_{n}cb"])
            wtok = l_w.start(sp, bias["a"][:], k["L0_attn_ba"])
            wtok = l_w.start(sp, raw_o[:], k["L0_attn_Wo"])
            wtok = l_w.start(sp, lnw[:], k["L0_attn_ln_w"])
            wtok = l_w.start(sp, lnb[:], k["L0_attn_ln_b"])
            stats = c.sb(wctx, "a_stats", [P, NTILE, 6])
            mv = c.sb(wctx, "a_mv", [P, NTILE, 2])
            rstd = c.sb(wctx, "a_rstd", [P, NTILE])
            xn = Ring([Slot(c.sb(wctx, f"a_xn{i}", [P, 4, D])) for i in range(2)])
            xnT = Ring([Slot(c.sb(wctx, f"a_xnT{i}", [P, BANK])) for i in range(2)])
            zero = c.sb(wctx, "a_zero", [P, NB, PAD])
            t_z = dve.do(lambda e: e.memset(zero[:], 0.0))
            w_pads.start(sp, xn_dram[:, :, 0:PAD], zero[:], t_z)
            t_n = layer_norm_rows(c, X, stats, mv, rstd, eps, lambda g: (loaded,))
            bank, lbank = (Ring([Slot(c.bank(2 * j + i)) for i in range(2)]) for j in range(2))
            tp = pe.do(lambda e: e.transpose(c.bank(4)[:, 0:H0], raw_b[:], ident[0:H0, 0:H0]), wb_loaded)
            pe.wait(act.do(lambda e: e.activation(wbT[:], c.bank(4)[:, 0:H0], ACT.Copy), tp, wb_loaded))
            for n in range(NTILE // 4):
                s, o, b = xn.next(), xnT.next(), bank.next()
                for j in range(4):
                    g = 4 * n + j
                    t = dve.do(lambda e, g=g, j=j, s=s: e.tensor_scalar(s.ap[:, j, :], X[:, g, :], mv[:, g, 0:1],
                               rstd[:, g:g + 1], ALU.subtract, ALU.mult), t_n[g], *s.free)
                for j in range(4):
                    tp = pe.do(lambda e, j=j, s=s, b=b: e.transpose(b.ap[:, j * P:(j + 1) * P], s.ap[:, j, :],
                               ident[:]), t, *b.free)
                s.free = [tp]
                ta = act.do(lambda e, o=o, b=b: e.activation(o.ap[:], b.ap, ACT.Copy), tp, *o.free)
                b.free = [ta]
                bl = lbank.next()
                tl = pe.do(lambda e, o=o, bl=bl: e.matmul(bl.ap[0:H0, :], wbT[:], o.ap[:], start=True, stop=True), ta, *bl.free)
                beta_ok = act.go(lambda e, n=n, bl=bl: e.activation(betaT[:, n * BANK:(n + 1) * BANK], bl.ap[0:H0, :], ACT.Sigmoid,
                                 bias=bb[:, 0:1]), tl)
                bl.free = [beta_ok]
                bi, t0 = divmod(n * BANK, T)
                o.free = [w_xn[n % 2].start(sp, xn_dram[:, bi, PAD + t0:PAD + t0 + BANK], o.ap[:], ta), tl]

            bank = Ring([Slot(c.bank(i)) for i in range(4)])
            for b in bank.slots:
                b.free = [beta_ok]
            for n in "qkvag":
                for half in range(2):
                    for j in range(TAPS if n in "qkv" else 1):
                        b = bank.next()
                        src = raw[n][:, 4 * half:4 * half + 4, :]
                        ready, s = [wtok], None
                        if n in "qkv":
                            s = scaled.next()
                            tj = tap[n][:, 4 * half:4 * half + 4, j:j + 1].broadcast_to([P, 4, D])
                            ready = [dve.do(lambda e, s=s, src=src, tj=tj: e.tensor_tensor(s.ap[:], src, tj, ALU.mult),
                                            wtok, *s.free)]
                            src = s.ap[:]
                        for m in range(4):
                            tp = pe.do(lambda e, b=b, m=m, src=src: e.transpose(b.ap[:, m * P:(m + 1) * P],
                                       src[:, m, :], ident[:]), *ready, *b.free)
                        if s is not None:
                            s.free = [tp]
                        b.free = [act.do(lambda e, n=n, j=j, half=half, b=b: e.activation(
                            wT[n][:, j, half * BANK:(half + 1) * BANK], b.ap, ACT.Copy), tp)]
            for half in range(2):
                b = bank.next()
                for m in range(4):
                    ct = 4 * half + m
                    tp = pe.do(lambda e, b=b, m=m, ct=ct: e.transpose(b.ap[:, m * P:(m + 1) * P],
                               raw_o[:, ct * P:(ct + 1) * P], ident[:]), wtok, *b.free)
                b.free = [act.do(lambda e, b=b, half=half: e.activation(
                    woT[:, 4 * half:4 * half + 4, :], b.ap.rearrange("p (m d) -> p m d", m=4), ACT.Copy), tp)]

            btx = c.sb(wctx, "a_btx", [P, TPB, 2, 2, NCT, NB])
            bt = c.bank(4).rearrange("p (g h) -> p g h", h=H0)
            for g in range(NTILE):
                t = pe.do(lambda e, g=g: e.transpose(bt[:, g, :], betaT[:, g * P:(g + 1) * P], ident[0:H0, 0:H0]), beta_ok)
            for tt in range(TPB):
                for ih in range(2):
                    for par in range(2):
                        src = bt[:, tt::TPB, par::2].rearrange("p b c -> p c b")
                        td = dve.go(lambda e, tt=tt, ih=ih, par=par, src=src: e.tensor_copy(btx[:, tt, par, ih, :, :], src), t)
            for tt in range(TPB):
                b = c.bank(5 + tt // 4)[:, (tt % 4) * P:(tt % 4 + 1) * P]
                tp = pe.do(lambda e, tt=tt, b=b: e.transpose(b, btx[:, tt].rearrange("p a i c b -> p (a i c b)"),
                           ident[:]), td)
            for half in range(2):
                act.do(lambda e, half=half: e.activation(beta[:, half * BANK:(half + 1) * BANK], c.bank(5 + half),
                       ACT.Copy), tp)
            c.barrier(*[Token(w.sem, w.count) for w in w_xn + [w_pads]])

        xseg = Ring([Slot(sb(f"xseg{i}", [P, NB, PAD + SEG])) for i in range(4)])
        KQ = Ring([Slot(sb(f"kq{i}", [P, R, 3, SEG])) for i in range(2)])
        kraw = Slot(sb("kraw", [P, R, SEG]))
        v1, a1 = Slot(sb("v1", [P, SEG, R])), Slot(sb("a1", [P, SEG, R]))
        a2 = Ring([Slot(sb(f"a2_{i}", [P, SEG, 32])) for i in range(2)])
        bv = Ring([Slot(sb(f"bv{i}", [P, SEG, 32])) for i in range(2)])
        Dc = Ring([Slot(sb(f"dc{i}", [P, SEG, 32])) for i in range(2)])
        Dk = Slot(sb("dk", [P, CK, 32]))
        G1, G1b = Slot(sb("g1", [P, R, 2, CK])), Slot(sb("g1b", [P, 8, 2, CK]))
        G2 = Ring([Slot(sb(f"g2_{i}", [P, 2, CK, SEG])) for i in range(2)])
        Kt = Slot(sb("kt", [P, R, DK]))
        W = [sb(f"w{i}", [P, SEG, 32]) for i in range(NCK)]
        Wm = sb("wm", [P, 2, 32, R])
        ST = sb("st", [P, R, DK])
        AB = Ring([Slot(sb(f"ab{i}", [P, 8, DK])) for i in range(2)])
        Dx = Ring([Slot(sb(f"dx{i}", [P, 8, 2, 32])) for i in range(2)])
        P2 = sb("p2", [P, 2, CK, 32])
        tmp_e, tmp_o = sb("tmp_e", [P, CK, 32]), sb("tmp_o", [P, CK, 32])
        red = sb("red", [P, 2, 32])
        O2 = Ring([Slot(sb(f"o2_{i}", [P, SEG, 32])) for i in range(2)])
        tot, mom = sb("tot", [P, SEG]), sb("mom", [P, SEG])
        o1 = sb("o1", [P, R, SEG])
        og = Slot(sb("og", [P, R // 2, SEG]))
        xrow = Slot(sb("xrow", [P, D]))
        back = Ring([Slot(c.bank(i)) for i in range(4)])
        Pb = Slot(c.bank(4, 2))
        Ub = Ring([Slot(c.bank(6 + i)) for i in range(2)])
        l_seg = [DmaCount(c.sem(f"s_a_seg{i}")) for i in range(4)]
        l_row, w_row = (DmaCount(c.sem(n)) for n in ("s_a_row", "s_a_out"))
        half_of, pair_ones, row_mean, ih_mask, own = (cst[n] for n in ("half_of", "pair_ones", "row_mean", "ih_mask", "own"))

        for w in W + [ST]:
            zeroed = dve.do(lambda e, w=w: e.memset(w[:], 0.0))

        def project(n, b, xs, ct, m):
            taps = TAPS if n in "qkv" else 1
            for j in range(taps):
                off = j if taps > 1 else PAD
                fn = lambda e, j=j, off=off: e.matmul(
                    b.ap[:, m * SW:(m + 1) * SW].rearrange("p (b t) -> p b t", b=NB), wT[n][:, j, ct * P:(ct + 1) * P],
                    xs.ap[:, :, off:off + SEG], start=(j == 0), stop=(j == taps - 1))
                if j < taps - 1:
                    pe.run(fn, *b.free, *xs.ready)
                else:
                    return pe.do(fn, *b.free, *xs.ready)

        def segment_inputs(s):
            seg = dict(xs=xseg.next(), kq=KQ.next(), a2=a2.next(), bv=bv.next(), dc=Dc.next(), g2=G2.next(), o2=O2.next())
            xs, kq = seg["xs"], seg["kq"]
            t0 = s * SEG
            xs.ready = [l_seg[s % 4].start(sp, xs.ap[:], xn_dram[:, :, t0:t0 + SEG + PAD], *xs.free)]
            done = {}

            def proj(n, half):
                b = back.next()
                for m in range(4):
                    tp = project(n, b, xs, 4 * half + m, m)
                for m in range(4):
                    ct = 4 * half + m
                    src = b.ap[:, m * SW:(m + 1) * SW].rearrange("p (b t) -> p b t", b=NB)
                    rr = slice(ct * NB, (ct + 1) * NB)
                    if n == "k":
                        dst, fn, free = kraw.ap[:, rr, :], ACT.Silu, kraw.free
                    elif n == "q":
                        dst, fn, free = kq.ap[:, rr, 2, :], ACT.Silu, kq.free
                    elif n == "v":
                        dst, fn, free = v1.ap[:, :, rr].rearrange("p t b -> p b t"), ACT.Silu, v1.free
                    else:
                        dst, fn, free = a1.ap[:, :, rr].rearrange("p t b -> p b t"), ACT.Sigmoid, a1.free
                    t = act.go(lambda e, dst=dst, src=src, fn=fn, ct=ct, n=n: e.activation(
                        dst, src, fn, bias=bias[n][:, ct:ct + 1]), tp, *free)
                b.free = [t]
                done[n] = t
                if n == "k" and half == 1:
                    src = kraw.ap[:].rearrange("p r (o t) -> p r o t", o=1).broadcast_to([P, R, 2, SEG])
                    done["kk"] = act.go(lambda e, src=src: e.activation(kq.ap[:, :, 0:2, :], src,
                                        ACT.Copy, scale=DK ** -0.5), t, *kq.free)
                    kraw.free = [done["kk"]]

            def gates():
                t = dve.go(lambda e: e.transpose(seg["a2"].ap[:].rearrange("p t i -> p (t i)"),
                                                 a1.ap[:].rearrange("p t r -> p (t r)")), done["a"], *seg["a2"].free)
                a1.free = [t]
                A, Dd = seg["a2"].ap, seg["dc"].ap
                view = lambda x, j: x[:].rearrange("p (c t) i -> p c t i", t=CK)[:, :, j, :]
                tt = pool.do(lambda e: e.tensor_copy(view(Dd, 0), view(A, 0)), t, *seg["dc"].free)
                for j in range(1, CK):
                    tt = pool.do(lambda e, j=j: e.tensor_tensor(view(Dd, j), view(Dd, j - 1), view(A, j), ALU.mult), tt)
                seg["a_ready"], seg["d_ready"] = t, tt

            def values():
                t = dve.go(lambda e: e.transpose(seg["bv"].ap[:].rearrange("p t i -> p (t i)"),
                                                 v1.ap[:].rearrange("p t r -> p (t r)")), done["v"], *seg["bv"].free)
                v1.free = [t]
                bcol = beta[:, t0:t0 + SEG].rearrange("p (t o) -> p t o", o=1).broadcast_to([P, SEG, 32])
                seg["v_ready"] = pool.go(lambda e: e.tensor_tensor(seg["bv"].ap[:], seg["bv"].ap[:], bcol, ALU.mult), t)

            def gram(n):
                b = back.next()
                for m in range(8):
                    r = 8 * n + m
                    for par in range(2):
                        ps = slice(par * DK, (par + 1) * DK)
                        fn = lambda e, r=r, m=m, ps=ps: e.matmul(
                            b.ap[ps, m * 2 * SEG:(m + 1) * 2 * SEG].rearrange("p (z t) -> p z t", z=2),
                            kq.ap[ps, r, 0:2, :].rearrange("p z t -> p (z t)"), kq.ap[ps, r, 0:3:2, :],
                            start=True, stop=True)
                        if m < 7 or par < 1:
                            pe.run(fn, done["kk"], done["q"], *b.free)
                tp = pe.do(fn)
                v = b.ap.rearrange("p (rz c t) -> p rz c t", c=NCK, t=CK)
                dst = G1.ap[:, 8 * n:8 * n + 8, :, :].rearrange("p r z t -> p (r z) t")
                oth = G1b.ap[:, :, :, :].rearrange("p r z t -> p (r z) t")
                act.go(lambda e: e.activation(oth, v[:, :, 0, :], ACT.Copy, scale=half_of[:, 0:1]), tp, *G1b.free)
                t = act.go(lambda e: e.activation(dst, v[:, :, 1, :], ACT.Copy, scale=half_of[:, 1:2]), *G1.free)
                b.free = [t]
                seg["g1"] = pool.go(lambda e: e.tensor_tensor(dst, dst, oth, ALU.add), t)
                G1b.free = [seg["g1"]]

            def gram_rows():
                g2 = seg["g2"]
                tr = dve.go(lambda e: e.transpose(g2.ap[:].rearrange("p z t j -> p (z t) j"),
                                                  G1.ap[:].rearrange("p r z t -> p (z t) r")), seg["g1"], *g2.free)
                G1.free = [tr]
                for ch in range(NCK):
                    v = g2.ap[:, 0, :, ch * CK:(ch + 1) * CK]
                    bc = beta[:, t0 + ch * CK:t0 + (ch + 1) * CK].rearrange("p (t o) -> p t o", o=1).broadcast_to([P, CK, CK])
                    seg["g_ready"] = pool.go(lambda e, v=v, bc=bc: e.tensor_tensor(v, v, bc, ALU.mult), tr)

            def time_rows(n):
                b = back.next()
                for m in range(8):
                    r = 8 * n + m
                    for par in range(2):
                        ps = slice(par * DK, (par + 1) * DK)
                        fn = lambda e, r=r, m=m, ps=ps: e.matmul(
                            b.ap[ps, m * DK:(m + 1) * DK], kq.ap[ps, r, 0:2, :].rearrange("p z t -> p (z t)"),
                            ident[ps, ps], start=True, stop=True)
                        if m < 7 or par < 1:
                            pe.run(fn, done["kk"], *b.free)
                tp = pe.do(fn)
                t = act.go(lambda e: e.activation(Kt.ap[:, 8 * n:8 * n + 8, :].rearrange("p r d -> p (r d)"), b.ap, ACT.Copy),
                           tp, *Kt.free)
                b.free = [t]
                seg["kt_ready"] = t

            each = lambda fn, args: [lambda a=a: fn(*a) for a in args]
            halves = lambda n: each(proj, [(n, 0), (n, 1)])
            seg["early"] = halves("k") + halves("q")
            seg["mid"] = halves("a") + halves("v")
            seg["gates"], seg["values"], seg["gram_rows"] = gates, values, gram_rows
            seg["gram"] = each(gram, [(n,) for n in range(4)])
            seg["time_rows"] = each(time_rows, [(n,) for n in range(4)])
            return seg

        def chunk(s, ch, seg, jobs, last_jobs, in_u, after_u):
            t0 = s * SEG + ch * CK
            kq, a2_, bv_, dc, g2, o2 = (seg[n] for n in ("kq", "a2", "bv", "dc", "g2", "o2"))
            js = slice(ch * CK, (ch + 1) * CK)
            Wc = W[ch]

            st = {}

            def spread_gates(n):
                dx = st["dx", n] = Dx.next()
                d15 = dc.ap[:, (ch + 1) * CK - 1:(ch + 1) * CK, :].rearrange("p (o q) i -> p o q i", o=1).broadcast_to([P, 8, 2, 32])
                ow = own[:, 16 * n:16 * n + 16].rearrange("p (r h o) -> p r h o", h=2, o=1).broadcast_to([P, 8, 2, 32])
                dx.ready = pool.go(lambda e: e.tensor_tensor(dx.ap[:], d15, ow, ALU.mult), seg["d_ready"], *dx.free)

            def sum_gates(n):
                b, dx, ab = back.next(), st["dx", n], AB.next()
                tb = pe.do(lambda e: e.matmul(b.ap, pair_ones[:], dx.ap[:].rearrange("p r h i -> p (r h i)"),
                           start=True, stop=True), dx.ready, *b.free)
                dx.free = [tb]
                ab.ready = act.go(lambda e: e.activation(ab.ap[:].rearrange("p r i -> p (r i)"), b.ap, ACT.Copy), tb, *ab.free)
                b.free, st["ab", n] = [ab.ready], ab

            def decay(n):
                ab, sv = st["ab", n], ST[:, 8 * n:8 * n + 8, :]
                st[n] = pool.go(lambda e: e.tensor_tensor(sv, sv, ab.ap[:], ALU.mult), ab.ready, tp, chain["state"][n])
                ab.free = [st[n]]

            spread_gates(0)
            spread_gates(1)
            for r in range(R):
                for par in range(2):
                    ps = slice(par * DK, (par + 1) * DK)
                    fn = lambda e, r=r, ps=ps: e.matmul(
                        Pb.ap[ps, r * 2 * CK:(r + 1) * 2 * CK].rearrange("p (z t) -> p z t", z=2), ST[ps, r, :],
                        kq.ap[ps, r, 0:3:2, js], start=True, stop=True)
                    if r < R - 1 or par < 1:
                        pe.run(fn, chain["state"][r // 8], *Pb.free)
            tp = pe.do(fn)
            t = pool.go(lambda e: e.tensor_copy(Dk.ap[:, 1:, :], dc.ap[:, ch * CK:(ch + 1) * CK - 1, :]), seg["d_ready"], *Dk.free)
            t1 = pool.go(lambda e: e.memset(Dk.ap[:, 0, :], 1.0), *Dk.free)
            bc = beta[:, t0:t0 + CK].rearrange("p (t o) -> p t o", o=1).broadcast_to([P, CK, 32])
            t_dk = pool.go(lambda e: e.tensor_tensor(Dk.ap[:], Dk.ap[:], bc, ALU.mult), t, t1)
            tt = dve.go(lambda e: e.transpose(P2[:].rearrange("p z t i -> p (z t) i"),
                        Pb.ap.rearrange("p (r n) -> p n r", r=R)), tp, chain["p2_free"])
            Pb.free = [tt]
            te = []
            for on, rows_ in ((dve, slice(0, CK // 2)), (pool, slice(CK // 2, CK))):
                tk = on.go(lambda e, q=rows_: e.tensor_tensor(P2[:, 0, q], P2[:, 0, q], Dk.ap[:, q], ALU.mult), tt, t_dk)
                te.append(on.go(lambda e, q=rows_: e.tensor_tensor(P2[:, 0, q], bv_.ap[:, ch * CK + q.start:ch * CK + q.stop, :],
                                P2[:, 0, q], ALU.subtract), tk, seg["v_ready"]))
            Dk.free = te
            tq = pool.go(lambda e: e.tensor_tensor(P2[:, 1], P2[:, 1], dc.ap[:, js, :], ALU.mult), tt, seg["d_ready"])
            parts = [[(sum_gates, 0)], [(sum_gates, 1)], [(decay, 0), (spread_gates, 2)], [(decay, 1), (spread_gates, 3), (sum_gates, 2)],
                     [(sum_gates, 3)], [(decay, 2)], [(decay, 3)]]
            parts = [lambda fns=fns: [fn(n) for fn, n in fns] for fns in parts]
            jobs = jobs + last_jobs
            early = max(len(jobs) - len(parts), 0)
            tail = jobs[early:]
            jobs = jobs[:early]
            for i, part in enumerate(parts):
                jobs += [part] + tail[i:i + 1]
            work = np.cumsum([t + 2 for t in range(CK)])
            due = [int(n) for n in np.ceil(work / work[-1] * len(jobs))]
            queued = 0

            tr = to = None
            tw = dve.go(lambda e: e.tensor_scalar(Wc[:, ch * CK, :], P2[:, 0, 0, :], -1.0, None, ALU.mult), te[0], chain["w_free"][ch])
            td = None
            for t in range(1, CK):
                row = ch * CK + t
                wj = Wc[:, ch * CK:row, :]
                gk = g2.ap[:, 0, t, ch * CK:row].rearrange("p (j o) -> p j o", o=1).broadcast_to([P, t, 32])
                tm = dve.go(lambda e, t=t, wj=wj, gk=gk: e.tensor_tensor(tmp_e[:, 0:t, :], wj, gk, ALU.mult), tw, td, tr,
                            seg["g_ready"])
                gq = g2.ap[:, 1, t - 1, ch * CK:row].rearrange("p (j o) -> p j o", o=1).broadcast_to([P, t, 32])
                tm_o = dve.go(lambda e, t=t, wj=wj, gq=gq: e.tensor_tensor(tmp_o[:, 0:t, :], wj, gq, ALU.mult), tw, td, to,
                              seg["g_ready"])
                tr = dve.go(lambda e, t=t: e.tensor_reduce(red[:, t % 2, :], tmp_e[:, 0:t, :].rearrange("p j i -> p i j"),
                            AX.X, ALU.add), tm)
                at = a2_.ap[:, row:row + 1, :].broadcast_to([P, t, 32])
                td = dve.go(lambda e, wj=wj, at=at: e.tensor_tensor(wj, wj, at, ALU.mult), tm_o, seg["a_ready"])
                tw = dve.go(lambda e, t=t, row=row: e.scalar_tensor_tensor(Wc[:, row, :], red[:, t % 2, :], -1.0,
                            P2[:, 0, t, :], ALU.mult, ALU.subtract), tr, te[t >= CK // 2])
                to = dve.go(lambda e, t=t, row=row: e.tensor_reduce(o2.ap[:, row - 1, :], tmp_o[:, 0:t, :].rearrange(
                            "p j i -> p i j"), AX.X, ALU.add), tm_o, *o2.free)
                while queued < due[t]:
                    jobs[queued]()
                    queued += 1
            tt = dve.go(lambda e: e.transpose(Wm[:, 1].rearrange("p i r -> p i r"), Wc[:].rearrange("p j i -> p i j")),
                        tw, td, chain["wm_free"])
            chain["w_free"][ch] = tt
            masked = []
            for rr in (slice(0, R // 2), slice(R // 2, R)):
                t = dve.go(lambda e, rr=rr: e.tensor_scalar(Wm[:, 0, :, rr], Wm[:, 1, :, rr], ih_mask[:, 0:1], None, ALU.mult), tt)
                masked.append(dve.go(lambda e, rr=rr: e.tensor_scalar(Wm[:, 1, :, rr], Wm[:, 1, :, rr], ih_mask[:, 1:2], None,
                                     ALU.mult), t))
            for job in in_u:
                job()
            row = (ch + 1) * CK
            gq = g2.ap[:, 1, CK - 1, ch * CK:row].rearrange("p (j o) -> p j o", o=1).broadcast_to([P, CK, 32])

            def output(n):
                if n == 0:
                    st["tm"] = dve.go(lambda e: e.tensor_tensor(tmp_o[:], Wc[:, ch * CK:row, :], gq, ALU.mult), tw, td, to)
                elif n == 1:
                    st["to"] = dve.go(lambda e: e.tensor_reduce(o2.ap[:, row - 1, :], tmp_o[:].rearrange("p j i -> p i j"),
                                      AX.X, ALU.add), st["tm"], to, *o2.free)
                elif n == 2:
                    seg["o"] = dve.go(lambda e: e.tensor_tensor(o2.ap[:, js, :], P2[:, 1], o2.ap[:, js, :], ALU.subtract), st["to"], tq)

            tus = []
            for n in range(4):
                b = Ub.next()
                for m in range(8):
                    r = 8 * n + m
                    for par in range(2):
                        ps = slice(par * DK, (par + 1) * DK)
                        fn = lambda e, r=r, m=m, ps=ps, b=b: e.matmul(
                            b.ap[ps, m * DK:(m + 1) * DK], Kt.ap[ps, r, :], Wm[ps, :, :, r].rearrange("p h i -> p (h i)"),
                            start=True, stop=True)
                        if m < 7 or par < 1:
                            pe.run(fn, masked[n // 2], seg["kt_ready"], *b.free)
                tu = pe.do(fn)
                sv = ST[:, 8 * n:8 * n + 8, :].rearrange("p r i -> p (r i)")
                ts = dve.go(lambda e, b=b, sv=sv: e.tensor_tensor(sv, sv, b.ap, ALU.subtract), tu, st[n])
                b.free = [ts]
                tus.append(ts)
                output(n)
            for job in after_u:
                job()
            chain["w_free"][ch], chain["p2_free"] = st["tm"], seg["o"]
            chain["state"], chain["wm_free"] = tus, tu
            Kt.free = [tu]
            for n in ("kq", "a2", "bv", "dc", "g2"):
                seg[n].free = [seg["o"], tu, tw, st[3], t_dk, te[1]]

        def finish(s, seg):
            xs = seg["xs"]
            t0 = s * SEG
            o2, st = seg["o2"], {}
            over_i = lambda a: a[:].rearrange("p (t o) -> p t o", o=1).broadcast_to([P, SEG, 32])
            cols = lambda a, half: a[:, 16 * half:16 * half + 16, :].rearrange("p r t -> p (r t)")

            def total():
                st["tot"] = dve.go(lambda e: e.tensor_reduce(tot[:], o2.ap[:], AX.X, ALU.add), seg["o"], chain["tot_free"])

            def moment(fn, name, **how):
                b = back.next()
                tp = pe.do(lambda e: e.matmul(b.ap[:, 0:SEG], row_mean[:], tot[:], start=True, stop=True), st["tot"], *b.free)
                chain["tot_free"] = tp
                st[name] = act.go(lambda e: e.activation(mom[:], b.ap[:, 0:SEG], fn, **how), tp, chain["mom_free"])
                b.free = [st[name]]

            def mean():
                moment(ACT.Copy, "mean")

            def centre():
                t = dve.go(lambda e: e.tensor_tensor(o2.ap[:], o2.ap[:], over_i(mom), ALU.subtract), st["mean"])
                chain["mom_free"] = st["centred"] = t
                st["sq"] = act.go(lambda e: e.activation(o1[:].rearrange("p r t -> p (r t)"), o2.ap[:].rearrange("p t i -> p (t i)"),
                                  ACT.Square), t, chain["o1_free"])

            def spread():
                st["tot"] = dve.go(lambda e: e.tensor_reduce(tot[:], o1[:].rearrange("p (t x) i -> p t (x i)", x=1), AX.X, ALU.add),
                                   st["sq"], chain["tot_free"])

            def deviation():
                moment(ACT.Sqrt, "dev", bias=eps[:, 0:1])

            def scale():
                t = dve.go(lambda e: e.reciprocal(mom[:], mom[:]), st["dev"])
                st["scaled"] = pool.go(lambda e: e.tensor_tensor(o2.ap[:], o2.ap[:], over_i(mom), ALU.mult), t, st["sq"])
                chain["mom_free"] = st["scaled"]

            def turn():
                st["o"] = dve.go(lambda e: e.transpose(o1[:].rearrange("p r t -> p t r"), o2.ap[:]), st["scaled"],
                                 chain["o1_free"])
                o2.free = [st["o"]]

            def affine():
                v = o1[:].rearrange("p r t -> p (r t)")
                st["affine"] = act.go(lambda e: e.activation(v, v, ACT.Identity, scale=lnw[:, 0:1], bias=lnb[:, 0:1]), st["o"])

            def gate(half):
                b, v, w = back.next(), cols(o1, half), og.ap[:].rearrange("p r t -> p (r t)")
                for m in range(4):
                    tp = project("g", b, xs, 4 * half + m, m)
                xs.free = [tp]
                t = act.go(lambda e: e.activation(w, b.ap, ACT.Sigmoid), tp, *og.free)
                b.free = [t]
                st["y"] = pool.go(lambda e: e.tensor_tensor(v, v, w, ALU.mult), t, st["affine"])
                og.free = [st["y"]]

            def rows():
                for b_ in range(NB):
                    st["x"] = l_row.start(sp, xrow.ap[b_ * SEG:(b_ + 1) * SEG, :], x_in[b_, t0:t0 + SEG, :], *xrow.free)

            def out():
                b = back.next()
                for ct in range(NCT):
                    fn = lambda e, ct=ct: e.matmul(b.ap[:, 0:D], o1[:, ct * NB:(ct + 1) * NB, :].rearrange("p b t -> p (b t)"),
                                                   woT[:, ct, :], start=(ct == 0), stop=(ct == NCT - 1))
                    if ct < NCT - 1:
                        pe.run(fn, st["y"], *b.free)
                st["out"], st["ob"] = pe.do(fn), b
                chain["o1_free"] = st["out"]

            def add():
                b = st["ob"]
                t = dve.go(lambda e: e.tensor_tensor(xrow.ap[:], xrow.ap[:], b.ap[:, 0:D], ALU.add), st["out"], st["x"])
                b.free = [t]
                for b_ in range(NB):
                    xrow.free = [w_row.start(sp, x1[b_, t0:t0 + SEG, :], xrow.ap[b_ * SEG:(b_ + 1) * SEG, :], t)]
            return {fn.__name__: fn for fn in (total, mean, centre, spread, deviation, scale, turn, affine, rows, out, add)} | {
                "gate0": lambda: gate(0), "gate1": lambda: gate(1)}

        chain = dict(state=[zeroed] * 4, w_free=[zeroed] * NCK, wm_free=None, o1_free=None,
                     p2_free=None, tot_free=None, mom_free=None)
        seg = segment_inputs(0)
        for job in seg["early"] + seg["mid"] + seg["gram"] + [seg["gates"], seg["values"], seg["gram_rows"]]:
            job()
        old, older = {}, {}
        for s in range(nseg):
            nxt = segment_inputs(s + 1) if s + 1 < nseg else {}
            get = lambda n, i=0, j=None: nxt[n][i:j] if nxt else []
            one = lambda of, *names: [of[n] for n in names if n in of]
            chunk(s, 0, seg, seg["time_rows"] + one(older, "rows", "affine", "gate0", "gate1") + one(old, "mean") + get("early", 0, 3),
                  one(older, "out"), one(old, "centre"), one(older, "add") + one(old, "spread"))
            chunk(s, 1, seg, one(old, "deviation") + get("early", 3) + get("mid", 0, 2) + get("gram") + one(old, "scale") + get("mid", 2),
                  [], one(nxt, "gates"), one(nxt, "values", "gram_rows") + one(old, "turn"))
            older, old = old, finish(s, seg)
            old["total"]()
            seg = nxt
        for n in ("rows", "affine", "gate0", "gate1", "out", "add"):
            if older:
                older[n]()
        for n in ("mean", "centre", "spread", "deviation", "scale", "turn", "rows", "affine", "gate0", "gate1", "out", "add"):
            old[n]()
        c.barrier(xrow.free[0])
def transposed(c, ctx, name, src, dst, scale_of=None, rows=None, affine=None):
    pe, dve, act = c.pe, c.dve, c.act
    bank = Ring([Slot(c.bank(i)) for i in range(2)])
    if scale_of:
        mv, rstd = scale_of
        xn = Ring([Slot(c.sb(ctx, f"{name}_xn{i}", [P, 4, D])) for i in range(2)])
    done = []
    for n in range(NTILE // 4):
        b, t = bank.next(), None
        s = xn.next() if scale_of else None
        for j in range(4):
            g = 4 * n + j
            if scale_of:
                t = dve.go(lambda e, g=g, j=j, s=s: e.tensor_scalar(s.ap[:, j, :], src[:, g, :], mv[:, g, 0:1],
                           rstd[:, g:g + 1], ALU.subtract, ALU.mult), *rows(g), *s.free)
        for j in range(4):
            g = 4 * n + j
            row = s.ap[:, j, :] if scale_of else src[:, g, :]
            tp = pe.do(lambda e, j=j, b=b, row=row: e.transpose(b.ap[:, j * P:(j + 1) * P], row, c.ident[:]),
                       t, *(() if scale_of else rows(g)), *b.free)
        if s:
            s.free = [tp]
        out = dst[:, n * BANK:(n + 1) * BANK]
        if affine:
            fn = lambda e, b=b, out=out: e.activation(out, b.ap, ACT.Identity, scale=affine[0], bias=affine[1])
        else:
            fn = lambda e, b=b, out=out: e.activation(out, b.ap, ACT.Copy)
        b.free = [act.go(fn, tp)]
        done += b.free * 4
    return done


class Norm:

    def __init__(self, c, ctx, name):
        self.stats = c.sb(ctx, name + "_stats", [P, NTILE, 6])
        self.mv = c.sb(ctx, name + "_mv", [P, NTILE, 2])
        self.rstd = c.sb(ctx, name + "_rstd", [P, NTILE])

    def of(self, c, src, ready):
        return layer_norm_rows(c, src, self.stats, self.mv, self.rstd, c.eps, ready)


NE, FF = 8, 512
NF = FF // P
CAPACITY = -(-5 * NT // (4 * NE))


def expert_ffn(c, k, X, x_ready, cst):
    pe, dve, act, sp = c.pe, c.dve, c.act, c.sp
    with ExitStack() as ctx:
        sb = lambda name, shape: c.sb(ctx, "b_" + name, shape)
        w1, w2 = sb("w1", [P, NE, FF]), sb("w2", [P, NE, NF, D])
        b1, b2 = sb("b1", [P, NE, NF]), sb("b2", [NE, D])
        gw, gb = sb("gw", [P, NE]), sb("gb", [1, NE])
        xnT = sb("xnT", [P, NT])
        norm = Norm(c, ctx, "b")
        tri, ones = cst["tri"], cst["ones"]
        l_w = DmaCount(c.sem("s_b_w"))
        for dst, n in ((gw, "gate_w"), (gb, "gate_b"), (b1, "b1"), (b2, "b2")):
            l_w.start(sp, dst[:], k["L0_ffn_" + n])
        l_w.start(sp, w1[:], k["L0_ffn_w1"].rearrange("e d f -> d e f"))
        w_ok = l_w.start(sp, w2[:], k["L0_ffn_w2"].rearrange("e (n f) d -> f e n d", f=P))
        t = norm.of(c, X, lambda g: (x_ready,))
        xn_ok = transposed(c, ctx, "b", X, xnT, (norm.mv, norm.rstd), lambda g: (t[g],))

        G = [P, NTILE, NE]
        lg, ex, eq, oh, gate, pre = (sb(n, G) for n in ("lg", "ex", "eq", "oh", "gate", "pre"))
        top, prob = sb("top", [P, NTILE]), sb("prob", [P, NTILE])
        gateT = sb("gateT", [NE, NT])
        bank = c.bank(2)
        for g in range(NTILE):
            pe.run(lambda e, g=g: e.matmul(bank[:, g * NE:(g + 1) * NE], xnT[:, g * P:(g + 1) * P], gw[:],
                   start=True, stop=False), xn_ok[g], w_ok)
            tp = pe.do(lambda e, g=g: e.matmul(bank[:, g * NE:(g + 1) * NE], c.ones_row[0:1, 0:P], gb[:],
                       start=False, stop=True))
        flat = lambda a: a[:].rearrange("p g e -> p (g e)")
        over_e = lambda a: a[:].rearrange("p (g o) -> p g o", o=1).broadcast_to(G)
        dve.do(lambda e: e.tensor_copy(flat(lg), bank[:, 0:NTILE * NE]), tp)
        dve.do(lambda e: e.tensor_reduce(top[:], lg[:], AX.X, ALU.max))
        dve.do(lambda e: e.tensor_tensor(eq[:], lg[:], over_e(top), ALU.is_equal))
        t = dve.do(lambda e: e.tensor_tensor(lg[:], lg[:], over_e(top), ALU.subtract))
        t = act.do(lambda e: e.activation(flat(ex), flat(lg), ACT.Exp), t)
        dve.do(lambda e: e.tensor_reduce(prob[:], ex[:], AX.X, ALU.add), t)
        dve.do(lambda e: e.reciprocal(prob[:], prob[:]))
        dve.do(lambda e: e.memset(pre[:], 0.0))
        for j in range(1, NE):
            dve.do(lambda e, j=j: e.tensor_tensor(pre[:, :, j], pre[:, :, j - 1], eq[:, :, j - 1], ALU.add))
        dve.do(lambda e: e.tensor_scalar(pre[:], pre[:], 0.0, None, ALU.is_equal))
        t = dve.do(lambda e: e.tensor_tensor(oh[:], eq[:], pre[:], ALU.mult))
        within, totals = c.bank(3)[:, 0:NTILE * NE], c.bank(4)[:, 0:NTILE * NE]
        pe.run(lambda e: e.matmul(within, tri[:], flat(oh), start=True, stop=True), t)
        tp = pe.do(lambda e: e.matmul(totals, ones[:], flat(oh), start=True, stop=True))
        dve.do(lambda e: e.tensor_copy(flat(ex), totals), tp)
        dve.do(lambda e: e.memset(pre[:, 0, :], 0.0))
        for g in range(1, NTILE):
            dve.do(lambda e, g=g: e.tensor_tensor(pre[:, g, :], pre[:, g - 1, :], ex[:, g - 1, :], ALU.add))
        dve.do(lambda e: e.tensor_tensor(flat(pre), flat(pre), within, ALU.add))
        dve.do(lambda e: e.tensor_scalar(pre[:], pre[:], float(CAPACITY), None, ALU.is_le))
        dve.do(lambda e: e.tensor_tensor(gate[:], oh[:], pre[:], ALU.mult))
        g_ok = dve.do(lambda e: e.tensor_tensor(gate[:], gate[:], over_e(prob), ALU.mult))

        banks = Ring([Slot(c.bank(i)) for i in range(2)])
        for n in range(NTILE // 4):
            b = banks.next()
            b.free = b.free or [act.last()]
            for j in range(4):
                g = 4 * n + j
                tp = pe.do(lambda e, b=b, j=j, g=g: e.transpose(b.ap[0:NE, j * P:(j + 1) * P], gate[:, g, :], c.ident[:]),
                           g_ok, *b.free)
            b.free = [act.do(lambda e, b=b, n=n: e.activation(gateT[:, n * BANK:(n + 1) * BANK], b.ap[0:NE, :], ACT.Copy), tp)]
        gt_ok = act.last()
        for n in range(NTILE // 4):
            b = banks.next()
            for j in range(4):
                g = 4 * n + j
                tp = pe.do(lambda e, b=b, j=j, g=g: e.matmul(b.ap[:, j * P:(j + 1) * P], gateT[:, g * P:(g + 1) * P], b2[:],
                           start=True, stop=True), gt_ok, *b.free)
            b.free = [dve.do(lambda e, b=b, n=n: e.tensor_tensor(X[:, 4 * n:4 * n + 4, :].rearrange("p g d -> p (g d)"),
                             X[:, 4 * n:4 * n + 4, :].rearrange("p g d -> p (g d)"), b.ap, ALU.add), tp)]
        up = Ring([Slot(c.bank(i)) for i in range(4)])
        down = Ring([Slot(c.bank(4 + i)) for i in range(4)])
        for s in up.slots + down.slots:
            s.free = [act.last(), dve.last()]
        hid = Ring([Slot(sb(f"hid{i}", [P, NF, BANK])) for i in range(2)])
        x_ok = [dve.last()] * NTILE

        def rise(n, ex_):
            h = hid.next()
            for f in range(NF):
                b = up.next()
                tp = pe.do(lambda e, b=b, f=f: e.matmul(b.ap, w1[:, ex_, f * P:(f + 1) * P], xnT[:, n * BANK:(n + 1) * BANK],
                           start=True, stop=True), *b.free)
                t = act.go(lambda e, b=b, f=f, h=h: e.activation(h.ap[:, f, :], b.ap, ACT.Relu, bias=b1[:, ex_, f:f + 1]),
                           tp, *h.free)
                b.free = [t]
            return h, t

        def fall(n, ex_, h, ready):
            b = down.next()
            for j in range(4):
                for f in range(NF):
                    tp = pe.do(lambda e, b=b, j=j, f=f: e.matmul(b.ap[:, j * P:(j + 1) * P], h.ap[:, f, j * P:(j + 1) * P],
                               w2[:, ex_, f, :], start=(f == 0), stop=(f == NF - 1)), ready, *b.free)
            h.free = [tp]
            for j in range(4):
                g = 4 * n + j
                t = x_ok[g] = dve.go(lambda e, b=b, j=j, g=g: e.scalar_tensor_tensor(X[:, g, :], b.ap[:, j * P:(j + 1) * P],
                                     gate[:, g, ex_:ex_ + 1], X[:, g, :], ALU.mult, ALU.add), tp, x_ok[g])
            b.free = [t]

        waiting = None
        for n in range(NT // BANK):
            for ex_ in range(NE):
                h, t = rise(n, ex_)
                if waiting:
                    fall(*waiting)
                waiting = (n, ex_, h, t)
        fall(*waiting)
        c.barrier()


NEG = -1e30


class Attention:
    TURN_LAG, OUT_LAG = 3, 2

    def __init__(self, c, ctx, name, nkeys, scores, turns, outs):
        self.c, self.nkeys = c, nkeys
        self.score, self.turn, self.out = (Ring([Slot(c.bank(i)) for i in n]) for n in (scores, turns, outs))
        self.S = Ring([Slot(c.sb(ctx, f"{name}_s{i}", [P, nkeys])) for i in range(self.TURN_LAG + 2)])
        self.PT = Ring([Slot(c.sb(ctx, f"{name}_pt{i}", [P, nkeys])) for i in range(self.OUT_LAG + 2)])
        self.low = Ring([Slot(c.sb(ctx, f"{name}_low{i}", [P, 1])) for i in range(4)])
        self.scored, self.turned, self.n = [], [], 0

    def unit(self, score, mask, scale, rowsum, values, o, after, then=None):
        c, w = self.c, mask.shape[-1]
        b, s, lo = self.score.next(), self.S.next(), self.low.next()
        for fn in score[:-1]:
            c.pe.run(lambda e, fn=fn: fn(e, b.ap), *after, *b.free)
        tp = c.pe.do(lambda e: score[-1](e, b.ap), *after, *b.free)
        t = c.dve.go(lambda e: e.tensor_tensor_reduce(out=s.ap[:, 0:w], in0=b.ap[:, 0:w], in1=mask, scale=scale,
                     scalar=3e38, op0=ALU.add, op1=ALU.min, accum_out=lo.ap[:, 0:1]), tp, *after, *s.free, *lo.free)
        b.free = [t]
        ta = c.act.go(lambda e: e.activation(s.ap[:, 0:w], s.ap[:, 0:w], ACT.Exp, scale=-1.0, bias=lo.ap[:, 0:1],
                      accum_out=rowsum), t, *after)
        lo.free = [ta]
        self.scored.append((s, ta, w, values, o, then))
        if len(self.scored) > self.TURN_LAG:
            self.transpose()
        return tp

    def transpose(self):
        c = self.c
        s, ta, w, values, o, then = self.scored.pop(0)
        b, pt = self.turn.next(), self.PT.next()
        for j in range(w // P):
            tp = c.pe.do(lambda e, j=j: e.transpose(b.ap[:, j * P:(j + 1) * P], s.ap[:, j * P:(j + 1) * P], c.ident[:]),
                         ta, *b.free)
        s.free = [tp]
        self.n += 1
        if self.n % 4 == 1:
            t = c.act.go(lambda e: e.activation(pt.ap[:, 0:w], b.ap[:, 0:w], ACT.Copy), tp, *pt.free)
        else:
            t = c.dve.go(lambda e: e.tensor_copy(pt.ap[:, 0:w], b.ap[:, 0:w]), tp, *pt.free)
        b.free = [t]
        self.turned.append((pt, t, ta, values, o, then))
        if len(self.turned) > self.OUT_LAG:
            self.product()

    def product(self):
        pt, t, ta, values, o, then = self.turned.pop(0)
        for j, v in enumerate(values):
            tp = self.c.pe.do(lambda e, j=j, v=v: e.matmul(o.ap, pt.ap[:, j * P:(j + 1) * P], v, start=(j == 0),
                              stop=(j == len(values) - 1)), t, *o.slot.free)
        pt.free = [tp]
        if then:
            then(tp, ta)

    def drain(self):
        while self.scored:
            self.transpose()
        while self.turned:
            self.product()


class Part:

    def __init__(self, slot, ap):
        self.slot, self.ap = slot, ap


H1, HD = 16, 8
LEFT, RIGHT = 127, 128


class BandedWeights:

    def __init__(self, c, ctx, k, cst_dram):
        sb = lambda name, shape: c.sb(ctx, "c_" + name, shape)
        self.wqk, self.wv = sb("wqk", [P, 4, P]), sb("wv", [P, P])
        self.wo, self.bo = sb("wo", [P, D]), sb("bo", [1, D])
        self.cos, self.sin, self.heads, self.band = sb("cos", [P, T]), sb("sin", [P, T]), sb("heads", [P, H1]), sb("band", [P, 3 * P])
        dma = DmaCount(c.sem("s_c_w"))
        for dst, src in ((self.wqk, k["L1_wqk"]), (self.wv, k["L1_wv"]), (self.wo, k["L1_attn_w_out"]), (self.bo, k["L1_attn_b_out"]),
                         (self.cos, cst_dram["rope_cos"]), (self.sin, cst_dram["rope_sin"]), (self.heads, cst_dram["head_rows"]),
                         (self.band, cst_dram["band"])):
            self.ready = dma.start(c.sp, dst[:], src)


def banded_attention(c, X, W):
    pe, dve, act, pool = c.pe, c.dve, c.act, c.pool
    wqk, wv, wo, bo, cos, sin, heads, band = W.wqk, W.wv, W.wo, W.bo, W.cos, W.sin, W.heads, W.band
    for s in (pe, dve, pool):
        s.wait(W.ready)
    with ExitStack() as ctx:
        sb = lambda name, shape: c.sb(ctx, "c_" + name, shape)
        qT, kT = sb("qT", [P, NT]), sb("kT", [P, NT])
        V = sb("V", [P, NTILE, D])
        with ExitStack() as pctx:
            xnT = c.sb(pctx, "c_xnT", [P, NT])
            tmp = Ring([Slot(c.sb(pctx, f"c_tmp{i}", [P, BANK])) for i in range(2)])
            norm = Norm(c, pctx, "c")
            t = norm.of(c, X, lambda g: ())
            xn_ok = transposed(c, pctx, "c", X, xnT, (norm.mv, norm.rstd), lambda g: (t[g],))
            pair = Ring([Slot(c.bank(2, 2)), Slot(c.bank(4, 2))])
            for n in range(NT // BANK):
                cols, pos = slice(n * BANK, (n + 1) * BANK), slice(n * BANK % T, n * BANK % T + BANK)
                for z, dst in enumerate((qT, kT)):
                    b, s = pair.next(), tmp.next()
                    for m in range(2):
                        tp = pe.do(lambda e, b=b, m=m, z=z, cols=cols: e.matmul(b.ap[:, m * BANK:(m + 1) * BANK],
                                   wqk[:, 2 * z + m, :], xnT[:, cols], start=True, stop=True), xn_ok[4 * n + 3], *b.free)
                    dve.go(lambda e, b=b, dst=dst, cols=cols, pos=pos: e.tensor_tensor(dst[:, cols], b.ap[:, 0:BANK], cos[:, pos],
                           ALU.mult), tp)
                    t = dve.go(lambda e, b=b, s=s, pos=pos: e.tensor_tensor(s.ap[:], b.ap[:, BANK:], sin[:, pos], ALU.mult), *s.free)
                    b.free = [t]
                    s.free = [pool.go(lambda e, dst=dst, s=s, cols=cols: e.tensor_tensor(dst[:, cols], dst[:, cols], s.ap[:], ALU.add), t)]
            vb = Ring([Slot(c.bank(6)), Slot(c.bank(7))])
            for n in range(NTILE // 4):
                b = vb.next()
                for j in range(4):
                    g = 4 * n + j
                    tp = pe.do(lambda e, b=b, j=j, g=g: e.matmul(b.ap[:, j * P:(j + 1) * P], xnT[:, g * P:(g + 1) * P], wv[:],
                               start=True, stop=True), xn_ok[g], *b.free)
                b.free = [act.do(lambda e, b=b, n=n: e.activation(V[:, 4 * n:4 * n + 4, :].rearrange("p g d -> p (g d)"), b.ap,
                                 ACT.Copy), tp)]
            c.barrier()
        att = Attention(c, ctx, "c", 3 * P, (0, 1, 2), (3, 4), (5, 6))
        qm = Ring([Slot(sb(f"qm{i}", [P, H1, P])) for i in range(2)])
        rows = Ring([Slot(sb(f"rows{i}", [P, H1])) for i in range(2)])
        on = Ring([Slot(sb(f"on{i}", [P, D])) for i in range(2)])
        oT = Ring([Slot(sb(f"oT{i}", [P, P])) for i in range(2)])
        last = Slot(c.bank(7))
        later = []

        def project_out(g, o, ot, t):
            tp = pe.do(lambda e: e.transpose(last.ap[:, 0:P], o.ap[:], c.ident[:]), t, *last.free)
            o.free = [tp]
            t = act.do(lambda e: e.activation(ot.ap[:], last.ap[:, 0:P], ACT.Copy), tp, *ot.free)
            later.append((att.n + 2, lambda: add_out(g, ot, t)))

        def add_out(g, ot, t):
            pe.run(lambda e: e.matmul(last.ap[:, P:2 * P], ot.ap[:], wo[:], start=True, stop=False), t)
            tp = pe.do(lambda e: e.matmul(last.ap[:, P:2 * P], c.ones_row[0:1, 0:P], bo[:], start=False, stop=True))
            ot.free = [tp]
            last.free = [dve.do(lambda e: e.tensor_tensor(X[:, g, :], X[:, g, :], last.ap[:, P:2 * P], ALU.add), tp)]

        for g in range(NTILE):
            bi, tt = divmod(g, TPB)
            q = qm.next()
            src = qT[:, g * P:(g + 1) * P].rearrange("p (o t) -> p o t", o=1).broadcast_to([P, H1, P])
            hm = heads[:].rearrange("p (h o) -> p h o", o=1).broadcast_to([P, H1, P])
            tq = pool.do(lambda e, q=q, src=src, hm=hm: e.tensor_tensor(q.ap[:], src, hm, ALU.mult), *q.free)
            lo, hi = max(tt - 1, 0), min(tt + 1, TPB - 1)
            nk = hi - lo + 1
            m0 = (lo - tt + 1) * P
            mask = band[:, m0:m0 + nk * P]
            keys = kT[:, (bi * TPB + lo) * P:(bi * TPB + hi + 1) * P]
            rs, ob = rows.next(), att.out.next()
            for h in range(H1):
                part = Part(ob, ob.ap[:, h * HD:(h + 1) * HD])
                vals = [V[:, bi * TPB + j, h * HD:(h + 1) * HD] for j in range(lo, hi + 1)]
                then = None
                if h == H1 - 1:
                    def then(tp, ta, rs=rs, ob=ob, g=g):
                        o, ot = on.next(), oT.next()
                        dve.do(lambda e: e.reciprocal(rs.ap[:], rs.ap[:]), ta)
                        t = dve.do(lambda e: e.tensor_tensor(o.ap[:].rearrange("p (h d) -> p h d", d=HD),
                                   ob.ap[:, 0:D].rearrange("p (h d) -> p h d", d=HD),
                                   rs.ap[:].rearrange("p (h o) -> p h o", o=1).broadcast_to([P, H1, HD]), ALU.mult), tp, *o.free)
                        rs.free, ob.free = [t], [t]
                        later.append((att.n + 3, lambda: project_out(g, o, ot, t)))
                score = [lambda e, ap, q=q, h=h, keys=keys, nk=nk: e.matmul(ap[:, 0:nk * P], q.ap[:, h, :], keys, start=True, stop=True)]
                tp = att.unit(score, mask, -HD ** -0.5, rs.ap[:, h:h + 1], vals, part, [tq, *rs.free], then)
                if later and att.n >= later[0][0]:
                    later.pop(0)[1]()
            q.free = [tp]
        att.drain()
        while later:
            later.pop(0)[1]()
        c.barrier()
DEPTH, H2, DH, WINDOW = 2, 8, 64, 64
INNER = H2 * DH
HID = int(D * 4 * 2 / 3)
NH = -(-HID // P)
QK_SCALE = 8.0


class Shifted:

    def __init__(self, c, ctx, X):
        self.c, self.X = c, X
        self.ap = c.sb(ctx, "hs", [P, NTILE, D])
        self.dma = [DmaCount(c.sem(f"s_shift{b}")) for b in range(NB)]
        self.zero = c.dve.go(lambda e: e.memset(self.ap[0:1, 0:NTILE:TPB, D // 2:D], 0.0))
        self.ready = [None] * NB
        self.read = None

    def bring(self, b):
        sp, half, X, Hs = self.c.sp, D // 2, self.X, self.ap
        g, tail, after = b * TPB, slice(D // 2, D), (self.c.dve.last(), self.read)
        self.dma[b].start(sp, Hs[:, g:g + TPB, 0:half], X[:, g:g + TPB, 0:half], *after)
        self.dma[b].start(sp, Hs[1:P, g:g + TPB, tail], X[0:P - 1, g:g + TPB, tail], *after)
        self.ready[b] = self.dma[b].start(sp, Hs[0:1, g + 1:g + TPB, tail], X[P - 1:P, g:g + TPB - 1, tail], *after)


class LocalWeights:

    def __init__(self, c, ctx, k, l):
        sb = lambda name, shape: c.sb(ctx, f"d{l}_" + name, shape)
        full = HID // P
        self.wqkv, self.wo = sb("wqkv", [P, 3 * INNER]), sb("wo", [P, INNER // P, D])
        self.w1, self.w2 = sb("w1", [P, 2 * HID]), sb("w2", [P, NH, D])
        self.b1a, self.b1g, self.b2 = sb("b1a", [P, NH]), sb("b1g", [P, NH]), sb("b2", [1, D])
        self.lnw, self.lnb = sb("lnw", [P, 1]), sb("lnb", [P, 1])
        dma = DmaCount(c.sem(f"s_d{l}_w"))
        load = lambda out, in_: dma.start(c.sp, out, in_)
        load(self.wqkv[:], k["L1_ffn_wqkv"][l])
        load(self.wo[:], k["L1_ffn_wo"][l].rearrange("(n p) d -> p n d", p=P))
        load(self.w1[:], k["L1_ffn_w1"][l])
        load(self.w2[:, 0:full, :], k["L1_ffn_w2"][l, 0:full * P].rearrange("(n p) d -> p n d", p=P))
        load(self.w2[0:HID - full * P, full, :], k["L1_ffn_w2"][l, full * P:HID])
        for half, dst in enumerate((self.b1a, self.b1g)):
            load(dst[:, 0:full], k["L1_b1_full"][l, half])
            load(dst[0:HID - full * P, full:full + 1], k["L1_b1_rest"][l, half])
        load(self.b2[:], k["L1_ffn_b2"][l:l + 1, :])
        load(self.lnw[:], k["L1_ffn_ln_g"][l])
        self.ready = load(self.lnb[:], k["L1_ffn_ln_b"][l])


def local_layer(c, k, X, Hs, W, l, cst_dram, batch_done):
    pe, dve, act, pool, sp = c.pe, c.dve, c.act, c.pool, c.sp
    wqkv, wo, w1, w2, b1a, b1g, b2, lnw, lnb = W.wqkv, W.wo, W.w1, W.w2, W.b1a, W.b1g, W.b2, W.lnw, W.lnb
    for s in (pe, dve, act):
        s.wait(W.ready)
    with ExitStack() as ctx:
        sb = lambda name, shape: c.sb(ctx, f"d{l}_" + name, shape)
        hT = sb("hT", [P, NT])
        norm = Norm(c, ctx, f"d{l}")

        with ExitStack() as actx:
            asb = lambda name, shape: c.sb(actx, f"d{l}_" + name, shape)
            tab = asb("tab", [P, 2, 2, TPB, DH])
            sc = asb("sc", [P, 2, DH])
            mask = asb("mask", [P, 2 * P])
            l_t = DmaCount(c.sem(f"s_d{l}_tab"))
            l_t.start(sp, tab[:], cst_dram["xpos"])
            l_t.start(sp, mask[:], cst_dram["local"])
            l_t.start(sp, sc[:, 0, :], k["L1_ffn_q_scale"][l:l + 1, :].broadcast_to([P, DH]))
            t_ok = l_t.start(sp, sc[:, 1, :], k["L1_ffn_k_scale"][l:l + 1, :].broadcast_to([P, DH]))
            hf = DH // 2
            for z in range(2):
                one = sc[:, z, :].rearrange("p (o d) -> p o d", o=1).broadcast_to([P, TPB, DH])
                dve.do(lambda e, z=z, one=one: e.tensor_tensor(tab[:, z, 0], tab[:, z, 0], one, ALU.mult), t_ok)
                for a in range(2):
                    v = tab[:, z, 1, :, a * hf:(a + 1) * hf]
                    o = sc[:, z, (1 - a) * hf:(2 - a) * hf].rearrange("p (o d) -> p o d", o=1).broadcast_to([P, TPB, hf])
                    tab_ok = dve.do(lambda e, v=v, o=o: e.tensor_tensor(v, v, o, ALU.mult))
            hT_ok = transposed(c, actx, f"d{l}a", Hs.ap, hT, rows=lambda g: (Hs.ready[g // TPB], Hs.zero))
            Hs.read = pe.last()
            pe.wait(hT_ok[-1])
            for s in (dve, pool):
                s.wait(tab_ok)

            att = Attention(c, actx, f"d{l}", 2 * P, (0, 1, 2), (3, 4), (5,))
            raw = Ring([Slot(asb(f"raw{i}", [P, 2, INNER])) for i in range(2)])
            rot = Ring([Slot(asb(f"rot{i}", [P, 2, INNER])) for i in range(2)])
            sw = Ring([Slot(asb(f"sw{i}", [P, 2, INNER])) for i in range(2)])
            nrm = Ring([Slot(asb(f"nrm{i}", [P, 2, H2])) for i in range(3)])
            qT = Ring([Slot(asb(f"qT{i}", [P, 4, P])) for i in range(2)])
            kT = Ring([Slot(asb(f"kT{i}", [P, 4, P])) for i in range(3)])
            V = Ring([Slot(asb(f"V{i}", [P, INNER])) for i in range(4)])
            rows = Ring([Slot(asb(f"rows{i}", [P, H2])) for i in range(2)])
            on = Ring([Slot(asb(f"on{i}", [P, INNER])) for i in range(2)])
            oT = Ring([Slot(asb(f"oT{i}", [P, 4, P])) for i in range(2)])
            side = Ring([Slot(c.bank(6)), Slot(c.bank(7))])
            later = []
            heads = lambda a: a.rearrange("p (h d) -> p h d", d=DH)

            def prepare(g):
                tt = g % TPB
                r, ro, s, nr, q, kk, v = (x.next() for x in (raw, rot, sw, nrm, qT, kT, V))
                cur = dict(q=q, k=kk, v=v, nr=nr)
                st = {}

                def project(z):
                    b = side.next()
                    tp = pe.do(lambda e: e.matmul(b.ap, hT[:, g * P:(g + 1) * P], wqkv[:, z * INNER:(z + 1) * INNER],
                               start=True, stop=True), hT_ok[g], *b.free)
                    if z < 2:
                        t = act.go(lambda e: e.activation(r.ap[:, z, :], b.ap, ACT.Copy), tp, *r.free)
                    else:
                        t = dve.go(lambda e: e.tensor_copy(v.ap[:], b.ap), tp, *v.free)
                        cur["v_ok"] = t
                    b.free, st["raw", z] = [t], t

                def squares():
                    t2 = act.go(lambda e: e.activation(s.ap[:], r.ap[:], ACT.Square), st["raw", 0], st["raw", 1], *s.free)
                    st["sq"] = dve.go(lambda e: e.tensor_reduce(nr.ap[:].rearrange("p z h -> p (z h)"),
                                      s.ap[:].rearrange("p z (h d) -> p (z h) d", d=DH), AX.X, ALU.add), t2, *nr.free)

                def roots():
                    st["root"] = act.go(lambda e: e.activation(nr.ap[:], nr.ap[:], ACT.Sqrt), st["sq"])

                def norms():
                    dve.do(lambda e: e.tensor_scalar(nr.ap[:], nr.ap[:], 1e-12, None, ALU.max), st["root"])
                    dve.do(lambda e: e.reciprocal(nr.ap[:], nr.ap[:]))
                    st["norms"] = dve.do(lambda e: e.tensor_scalar(nr.ap[:, 0, :], nr.ap[:, 0, :], -QK_SCALE, None, ALU.mult))

                def rotate(z):
                    cs = tab[:, z, 0, tt, :].rearrange("p (o d) -> p o d", o=1).broadcast_to([P, H2, DH])
                    for a in range(2):
                        sn = tab[:, z, 1, tt, a * hf:(a + 1) * hf].rearrange("p (o d) -> p o d", o=1).broadcast_to([P, H2, hf])
                        tb = pool.go(lambda e, z=z, a=a, sn=sn: e.tensor_tensor(heads(s.ap[:, z, :])[:, :, a * hf:(a + 1) * hf],
                                     heads(r.ap[:, z, :])[:, :, (1 - a) * hf:(2 - a) * hf], sn, ALU.mult), st["raw", 1], st["sq"])
                    ta = dve.go(lambda e: e.tensor_tensor(heads(ro.ap[:, z, :]), heads(r.ap[:, z, :]), cs, ALU.mult),
                                st["raw", 1], *ro.free)
                    st["rot", z] = ta, tb

                def add_up():
                    t = pool.go(lambda e: e.tensor_tensor(ro.ap[:], ro.ap[:], s.ap[:], ALU.add), *st["rot", 0], *st["rot", 1])
                    r.free, s.free = [t], [t]
                    kn = nr.ap[:, 1, :].rearrange("p (h o) -> p h o", o=1).broadcast_to([P, H2, DH])
                    st["done"] = pool.go(lambda e: e.tensor_tensor(heads(ro.ap[:, 1, :]), heads(ro.ap[:, 1, :]), kn, ALU.mult),
                                         t, st["norms"])

                def turn(z, dst):
                    b = side.next()
                    for j in range(4):
                        tp = pe.do(lambda e, j=j: e.transpose(b.ap[:, j * P:(j + 1) * P], ro.ap[:, z, j * P:(j + 1) * P],
                                   c.ident[:]), st["done"], *b.free)
                    b.free = [act.go(lambda e: e.activation(dst.ap[:].rearrange("p n t -> p (n t)"), b.ap, ACT.Copy),
                                     tp, *dst.free)]
                    ro.free = [tp]
                    cur["ok"] = b.free[0]

                plan = {0: [lambda: project(0)], 1: [lambda: project(1)], 2: [squares, lambda: project(2)], 3: [roots, lambda: rotate(0)],
                        4: [lambda: rotate(1)], 5: [norms], 6: [add_up], 9: [lambda: turn(0, q)], 10: [lambda: turn(1, kk)]}
                for n, jobs in plan.items():
                    jobs_at.setdefault((g - 1) * H2 - AHEAD + n, []).extend(jobs)
                return cur

            jobs_at = {}
            AHEAD = 4

            def prepare_for(unit):
                if (unit + AHEAD) % H2 == 0 and (unit + AHEAD) // H2 + 1 < NTILE:
                    tiles.append(prepare((unit + AHEAD) // H2 + 1))
                for job in jobs_at.pop(unit, []):
                    job()

            tiles = []
            for unit in range(-AHEAD - H2, 0):
                prepare_for(unit)
            prev = None
            for g in range(NTILE):
                cur = tiles.pop(0)
                blocks = ([prev] if g % TPB else []) + [cur]
                m = mask[:, (2 - len(blocks)) * P:]
                rs, ob = rows.next(), att.out.next()
                for h in range(H2):
                    ps, pr = slice(h % 2 * DH, h % 2 * DH + DH), h // 2
                    part = Part(ob, ob.ap[:, h * DH:(h + 1) * DH])
                    then = None
                    if h == H2 - 1:
                        def then(tp, ta, rs=rs, ob=ob, g=g, cur=cur, prev=prev):
                            o, ot = on.next(), oT.next()
                            for x in (prev, cur):
                                if x:
                                    x["v"].free = x["k"].free = [tp]
                            dve.do(lambda e: e.reciprocal(rs.ap[:], rs.ap[:]), ta)
                            t = dve.do(lambda e: e.tensor_tensor(heads(o.ap[:]), heads(ob.ap),
                                       rs.ap[:].rearrange("p (h o) -> p h o", o=1).broadcast_to([P, H2, DH]), ALU.mult), tp, *o.free)
                            rs.free, ob.free = [t], [t]
                            later.append((att.n + 2, lambda: turn_out(g, o, ot, t)))

                        def turn_out(g, o, ot, t):
                            b = side.next()
                            for j in range(4):
                                tp = pe.do(lambda e, j=j: e.transpose(b.ap[:, j * P:(j + 1) * P], o.ap[:, j * P:(j + 1) * P],
                                           c.ident[:]), t, *b.free)
                            o.free = [tp]
                            t = act.go(lambda e: e.activation(ot.ap[:].rearrange("p n t -> p (n t)"), b.ap, ACT.Copy), tp, *ot.free)
                            b.free = [t]
                            later.append((att.n + 2, lambda: project_out(g, ot, t)))

                        def project_out(g, ot, t):
                            b = side.next()
                            for j in range(4):
                                tp = pe.do(lambda e, j=j: e.matmul(b.ap[:, 0:D], ot.ap[:, j, :], wo[:, j, :], start=(j == 0),
                                           stop=(j == 3)), t, *b.free)
                            ot.free = [tp]
                            b.free = [dve.go(lambda e: e.tensor_tensor(X[:, g, :], X[:, g, :], b.ap[:, 0:D], ALU.add), tp)]
                            if g % TPB == TPB - 1:
                                Hs.bring(g // TPB)
                    score = [lambda e, ap, j=j, x=x, ps=ps, pr=pr, cur=cur: e.matmul(ap[:, j * P:(j + 1) * P], cur["q"].ap[ps, pr, :],
                             x["k"].ap[ps, pr, :], start=True, stop=True) for j, x in enumerate(blocks)]
                    tp = att.unit(score, m, cur["nr"].ap[:, 0, h:h + 1], rs.ap[:, h:h + 1],
                                  [x["v"].ap[:, h * DH:(h + 1) * DH] for x in blocks], part, [cur["ok"], cur["v_ok"], *rs.free], then)
                    unit_dve = dve.last()
                    if later and att.n >= later[0][0]:
                        later.pop(0)[1]()
                    prepare_for(g * H2 + h)
                cur["q"].free, cur["nr"].free = [tp], [unit_dve]
                prev = cur
            att.drain()
            while later:
                later.pop(0)[1]()
            c.barrier()

        t = norm.of(c, Hs.ap, lambda g: (Hs.ready[g // TPB],))
        hT_ok = transposed(c, ctx, f"d{l}f", Hs.ap, hT, (norm.mv, norm.rstd), lambda g: (t[g],), affine=(lnw[:, 0:1], lnb[:, 0:1]))
        up = Ring([Slot(c.bank(i, 2)) for i in (2, 4)])
        down = Ring([Slot(c.bank(i)) for i in (6, 7)])
        gl = Ring([Slot(sb(f"gl{i}", [P, BANK])) for i in range(2)])
        hid = Ring([Slot(sb(f"hid{i}", [P, NH, BANK])) for i in range(2)])

        def rise(n):
            h = hid.next()
            for f in range(NH):
                w = min(P, HID - f * P)
                b, s = up.next(), gl.next()
                for z in range(2):
                    c0 = z * HID + f * P
                    tp = pe.do(lambda e, b=b, z=z, c0=c0, w=w: e.matmul(b.ap[0:w, z * BANK:(z + 1) * BANK], w1[:, c0:c0 + w],
                               hT[:, n * BANK:(n + 1) * BANK], start=True, stop=True), hT_ok[4 * n + 3], *b.free)
                t = act.go(lambda e, b=b, s=s, f=f, w=w: e.activation(s.ap[0:w, :], b.ap[0:w, BANK:], ACT.Gelu, bias=b1g[0:w, f:f + 1]),
                           tp, *s.free)
                t = dve.go(lambda e, b=b, s=s, f=f, w=w, h=h: e.scalar_tensor_tensor(h.ap[0:w, f, :], b.ap[0:w, 0:BANK],
                           b1a[0:w, f:f + 1], s.ap[0:w, :], ALU.add, ALU.mult), t, *h.free)
                b.free, s.free = [t], [t]
            return n, h, t

        def fall(n, h, ready):
            b = down.next()
            for j in range(4):
                for f in range(NH):
                    w = min(P, HID - f * P)
                    pe.run(lambda e, b=b, j=j, f=f, w=w: e.matmul(b.ap[:, j * P:(j + 1) * P], h.ap[0:w, f, j * P:(j + 1) * P],
                           w2[0:w, f, :], start=(f == 0), stop=False), ready, *b.free)
                tp = pe.do(lambda e, b=b, j=j: e.matmul(b.ap[:, j * P:(j + 1) * P], c.ones_row[0:1, 0:P], b2[:], start=False, stop=True))
            h.free = [tp]
            xv = X[:, 4 * n:4 * n + 4, :].rearrange("p g d -> p (g d)")
            b.free = [dve.go(lambda e, b=b: e.tensor_tensor(xv, xv, b.ap, ALU.add), tp)]
            if (n + 1) * BANK % T == 0:
                batch_done(n * BANK // T)

        waiting = None
        for n in range(NT // BANK):
            nxt = rise(n)
            if waiting:
                fall(*waiting)
            waiting = nxt
        fall(*waiting)
        c.barrier()
def constants():
    p = np.arange(P)
    keep, phase = {}, {}
    keep["ident"] = np.eye(P)
    keep["ones_row"] = np.ones((1, P))
    keep["eps"] = np.full((P, 1), EPS)
    keep["half_of"] = np.stack([p % 32 < CK, p % 32 >= CK], 1)
    keep["ih_mask"] = np.stack([p // 32 % 2 == 0, p // 32 % 2 == 1], 1)
    same = p[:, None] // DK == p[None, :] // DK
    keep["pair_ones"] = same
    keep["row_mean"] = (same & (p[:, None] % 32 == p[None, :] % 32)) / DK
    keep["own"] = ((p[:, None, None] % 32 == np.arange(R)[None, :, None]) &
                   (p[:, None, None] // 32 % 2 == np.arange(2)[None, None, :])).reshape(P, 2 * R)
    phase["tri"] = p[:, None] <= p[None, :]
    phase["ones"] = np.ones((P, P))
    f32 = np.float32
    inv = f32(1.0) / f32(10000.0) ** (np.arange(0, HD, 2, dtype=f32) / f32(HD))
    ang = (np.arange(T, dtype=f32)[None, :] * inv[p % HD % (HD // 2)][:, None]).astype(f32)
    phase["rope_cos"] = np.cos(ang)
    phase["rope_sin"] = np.sin(ang) * np.where(p % HD < HD // 2, -1.0, 1.0)[:, None]
    phase["head_rows"] = p[:, None] // HD == np.arange(H1)[None, :]
    i, j = p[:, None], np.arange(3 * P)[None, :] - P
    phase["band"] = np.where((j >= i - LEFT) & (j <= i + RIGHT), 0.0, NEG)
    i, j = p[:, None], np.arange(2 * P)[None, :] - P
    phase["local"] = np.where((j <= i) & (j >= i - WINDOW), 0.0, NEG)
    half = np.arange(0, DH, 2, dtype=f32)
    inv = f32(1.0) / f32(10000.0) ** (half / f32(DH))
    t = np.arange(T, dtype=f32)
    ang = np.concatenate([t[:, None] * inv[None, :]] * 2, 1)
    base = (half + f32(0.4 * DH)) / f32(1.4 * DH)
    power = (t - T // 2) / f32(WINDOW // 2)
    scale = np.concatenate([base[None, :] ** power[:, None]] * 2, 1).astype(f32)
    sign = np.where(np.arange(DH) < DH // 2, -1.0, 1.0)[None, :].astype(f32)
    cos, sin = np.cos(ang), np.sin(ang) * sign
    tab = np.stack([[cos * scale, sin * scale], [cos / scale, sin / scale]])
    phase["xpos"] = tab.reshape(2, 2, TPB, P, DH).transpose(3, 0, 1, 2, 4)
    conv = lambda d: {n: np.ascontiguousarray(a, dtype=np.float32) for n, a in d.items()}
    return conv(keep), conv(phase)


def layouts(inputs):
    k = {n: np.ascontiguousarray(a) for n, a in inputs.items()}
    for n in ("L0_attn_qcb", "L0_attn_kcb", "L0_attn_vcb", "L0_attn_ba"):
        k[n] = k[n].reshape(NCT, P).T
    for n in ("L0_attn_qcw", "L0_attn_kcw", "L0_attn_vcw"):
        k[n] = k[n].reshape(NCT, P, TAPS).transpose(1, 0, 2)
    for n in ("L0_attn_ln_w", "L0_attn_ln_b"):
        k[n] = np.concatenate([k[n], k[n]])[:, None]
    k["L0_attn_bb"] = k["L0_attn_bb"][:, None]
    k["L0_ffn_gate_w"] = k["L0_ffn_gate_w"].T
    k["L0_ffn_gate_b"] = k["L0_ffn_gate_b"][None, :]
    k["L0_ffn_b1"] = k["L0_ffn_b1"].reshape(NE, NF, P).transpose(2, 0, 1)
    w = k.pop("L1_attn_w_qkv").reshape(3, H1, 2, HD // 2, D)
    rows = [w[0], w[0][:, ::-1], w[1], w[1][:, ::-1]]
    k["L1_wqk"] = np.stack([r.reshape(P, D).T for r in rows], 1)
    k["L1_wv"] = w[2].reshape(P, D).T
    k["L1_attn_w_out"] = k["L1_attn_w_out"].T
    k["L1_attn_b_out"] = k["L1_attn_b_out"][None, :]
    b1 = k.pop("L1_ffn_b1").reshape(DEPTH, 2, HID)
    full = HID // P * P
    k["L1_b1_full"] = b1[:, :, :full].reshape(DEPTH, 2, HID // P, P).transpose(0, 1, 3, 2)
    k["L1_b1_rest"] = b1[:, :, full:, None]
    for n in ("L1_ffn_ln_g", "L1_ffn_ln_b"):
        k[n] = k[n][:, :, None]
    return {n: np.ascontiguousarray(a) for n, a in k.items()}


def build(nc, shapes, phases="ABCD", nseg=NSEG, x_from="L0_attn_x"):
    keep, phase = constants()
    dram = lambda n, shape, kind: nc.dram_tensor(n, list(shape), F32, kind=kind).ap()
    k = {n: dram("in_" + n, s, "ExternalInput") for n, s in shapes.items()}
    cd = {n: dram("const_" + n, a.shape, "ExternalInput") for n, a in {**keep, **phase}.items()}
    out = dram("out_0", [NB, T, D], "ExternalOutput")
    x1, xn = dram("x1", [NB, T, D], "Internal"), dram("xn", [P, NB, T + PAD], "Internal")
    with ExitStack() as ctx:
        c = Core(nc, ctx)
        cst, l_c = {}, DmaCount(c.sem("s_const"))
        for n, a in keep.items():
            cst[n] = c.sb(ctx, "k_" + n, list(a.shape))
            ready = l_c.start(c.sp, cst[n][:], cd[n])
        for s in (c.pe, c.dve, c.act, c.pool):
            s.wait(ready)
        c.ident, c.eps, c.ones_row = cst["ident"], cst["eps"], cst["ones_row"]
        if "A" in phases:
            delta_rule_attention(c, k, k["L0_attn_x"], x1, xn, cst, nseg)
        rows = lambda a: a.rearrange("b (n p) d -> p (b n) d", p=P)
        X = c.sb(ctx, "x", [P, NTILE, D])
        l_x = DmaCount(c.sem("s_x"))
        for n in ("tri", "ones"):
            cst[n] = c.sb(ctx, "k_" + n, [P, P])
            l_x.start(c.sp, cst[n][:], cd[n])
        x_ready = l_x.start(c.sp, X[:], rows(x1 if "A" in phases else k[x_from]))
        for s in (c.pe, c.dve, c.act, c.pool):
            s.wait(x_ready)
        banded = BandedWeights(c, ctx, k, cd) if "C" in phases else None
        if "B" in phases:
            expert_ffn(c, k, X, x_ready, cst)
        weights = [LocalWeights(c, ctx, k, l) for l in range(DEPTH)] if "D" in phases else None
        if "C" in phases:
            banded_attention(c, X, banded)
        if "D" in phases:
            Y = c.sb(ctx, "y", [P, NTILE, D])
            Hs = Shifted(c, ctx, Y)
            with ExitStack() as nctx:
                norm = Norm(c, nctx, "y")
                t = norm.of(c, X, lambda g: ())
                for g in range(NTILE):
                    c.dve.go(lambda e, g=g: e.tensor_scalar(Y[:, g, :], X[:, g, :], norm.mv[:, g, 0:1], norm.rstd[:, g:g + 1],
                             ALU.subtract, ALU.mult), t[g])
                    if g % TPB == TPB - 1:
                        Hs.bring(g // TPB)
                c.barrier()

            def finish(b):
                g = slice(b * TPB, (b + 1) * TPB)
                t = c.dve.do(lambda e: e.tensor_tensor(X[:, g], X[:, g], Y[:, g], ALU.add))
                c.stores.start(c.sp, rows(out)[:, g], X[:, g], t)

            for l in range(DEPTH):
                local_layer(c, k, Y, Hs, weights[l], l, cd, Hs.bring if l < DEPTH - 1 else finish)
        else:
            c.stores.start(c.sp, rows(out), X[:], c.dve.last())
        c.sp.wait(Token(c.stores.sem, c.stores.count))
        block = ctx.enter_context(nc.Block())
        for on, s in ((block.tensor, c.pe), (block.vector, c.dve), (block.scalar, c.act), (block.gpsimd, c.pool),
                      (block.sync, c.sp)):
            queue = lambda e, s=s: s.emit(e)
            on(queue)
    return {"const_" + n: a for n, a in {**keep, **phase}.items()}


_IN = "in_"


def kernel(**inputs):
    import concourse.bacc as bacc
    from concourse.bass_utils import run_bass_kernel_spmd

    nc = bacc.Bacc("TRN2", target_bir_lowering=False, num_devices=1)
    laid_out = layouts({n: np.asarray(a) for n, a in inputs.items()})
    tables = build(nc, {n: a.shape for n, a in laid_out.items()})
    arrays = {**{_IN + n: a for n, a in laid_out.items()}, **tables}
    return run_bass_kernel_spmd(nc, [arrays], core_ids=[0]).results[0]["out_0"]
```
